# Optimizing a Trainium2 kernel written in Bass

```python
import numpy as np
import jax
import jax.numpy as jnp

def _softmax(x, axis=-1):
    return jax.nn.softmax(x, axis=axis)

def _gelu(x):
    return jax.nn.gelu(x, approximate=True)

def _silu(x):
    return jax.nn.silu(x)

def _sigmoid(x):
    return jax.nn.sigmoid(x)

def _layernorm(x, axis=-1, eps=1e-05):
    m = jnp.mean(x, axis=axis, keepdims=True)
    v = jnp.var(x, axis=axis, keepdims=True)
    return (x - m) / jnp.sqrt(v + eps)

def _scatter_add(tgt, idx, src, axis=0):
    return tgt.at[idx].add(src)

def _segment_sum(src, seg, n):
    return jax.ops.segment_sum(src, seg, n)
kernel_name = 'mk_decoder_preln_d2_seqx_r4_b5cb97'

def setup_inputs(seed: int=0):
    np.random.seed(seed)
    _w = jnp.asarray

    def _rec_inputs():
        import jax
        import jax.numpy as jnp
        _rk = jax.random.key(seed)
        x = 7.22e-05 + 1 * jax.random.normal(jax.random.fold_in(_rk, 1), (8, 512, 256), jnp.float32)
        _lenS = 512 - jax.random.randint(jax.random.fold_in(_rk, 7), (8,), 0, max(1, 512 // 4) + 1, jnp.int32)
        _lenS2 = 64 - jax.random.randint(jax.random.fold_in(_rk, 8), (8,), 0, max(1, 64 // 4) + 1, jnp.int32)
        _ctx_1024P = jax.random.normal(jax.random.fold_in(_rk, 11), (8, 16, 256), jnp.float32)
        _ctx_1024c = jax.random.dirichlet(jax.random.fold_in(_rk, 511), 0.3 * jnp.ones((16,), jnp.float32), (8, 64))
        _ctx_1024t = jnp.einsum('bsk,bkd->bsd', _ctx_1024c, _ctx_1024P)
        _ctx_1024t = _ctx_1024t * jax.lax.rsqrt(jnp.mean(jnp.square(_ctx_1024t)) + 1e-12) * 0.953939
        ctx_1024 = 4.13588e-05 + 0.999923 * (_ctx_1024t + 0.3 * jax.random.normal(jax.random.fold_in(_rk, 611), (8, 64, 256), jnp.float32))
        return (x, ctx_1024)
    x, ctx_1024 = _rec_inputs()

    def _L0_attn_setup():
        import jax, jax.numpy as jnp
        import numpy as np
        HEADS = 16

        def _binarize(W):
            alpha = jnp.mean(jnp.abs(W), axis=tuple(range(1, W.ndim)), keepdims=True)
            B = W + jax.lax.stop_gradient(jnp.sign(W) - W)
            return alpha * B

        def _binlinear(x, W, b):
            Wb = _binarize(W)
            return jnp.einsum('btc,oc->bto', x, Wb) + b
        key = jax.random.key(seed)
        ks = jax.random.split(key, 9)
        dim = 256
        B, T = (4, 512)
        inp = {'x': jax.random.normal(ks[0], (B, T, dim), jnp.float32), 'Wq': jax.random.normal(ks[1], (dim, dim), jnp.float32) * 0.02, 'bq': jax.random.normal(ks[2], (dim,), jnp.float32) * 0.02, 'Wk': jax.random.normal(ks[3], (dim, dim), jnp.float32) * 0.02, 'bk': jax.random.normal(ks[4], (dim,), jnp.float32) * 0.02, 'Wv': jax.random.normal(ks[5], (dim, dim), jnp.float32) * 0.02, 'bv': jax.random.normal(ks[6], (dim,), jnp.float32) * 0.02, 'Wp': jax.random.normal(ks[7], (dim, dim), jnp.float32) * 0.02, 'bp': jax.random.normal(ks[8], (dim,), jnp.float32) * 0.02}
        return inp
    _L0_attn_all = _L0_attn_setup()
    _L0_attn_in = {k: v for k, v in _L0_attn_all.items() if k in ('Wq', 'bq', 'Wk', 'bk', 'Wv', 'bv', 'Wp', 'bp')}
    del _L0_attn_all

    def _L0_xattn_setup():
        import jax, jax.numpy as jnp
        import numpy as np
        C = 256
        B, SQ, SKV = (4, 512, 512)
        key = jax.random.key(seed)
        ks = jax.random.split(key, 10)
        s = 1.0 / np.sqrt(C)
        return {'x': jax.random.normal(ks[0], (B, SQ, C), jnp.float32), 'content_embeddings': jax.random.normal(ks[1], (B, SKV, C), jnp.float32), 'Wq': jax.random.normal(ks[2], (C, C), jnp.float32) * s, 'bq': jnp.zeros((C,), jnp.float32), 'Wk': jax.random.normal(ks[3], (C, C), jnp.float32) * s, 'bk': jnp.zeros((C,), jnp.float32), 'Wv': jax.random.normal(ks[4], (C, C), jnp.float32) * s, 'bv': jnp.zeros((C,), jnp.float32), 'Wo': jax.random.normal(ks[5], (C, C), jnp.float32) * s, 'bo': jnp.zeros((C,), jnp.float32)}
    _L0_xattn_all = _L0_xattn_setup()
    _L0_xattn_in = {k: v for k, v in _L0_xattn_all.items() if k in ('Wq', 'bq', 'Wk', 'bk', 'Wv', 'bv', 'Wo', 'bo')}
    del _L0_xattn_all

    def _L0_ffn_setup():
        import jax, jax.numpy as jnp
        import numpy as np
        HIDDEN = 256
        INNER = 1024

        def _weight_quant(w):
            scale = 1.0 / jnp.clip(jnp.mean(jnp.abs(w)), 1e-05)
            wq = jnp.clip(jnp.round(w * scale), -1.0, 1.0) / scale
            return w + jax.lax.stop_gradient(wq - w)

        def _act_quant(x):
            scale = 127.0 / jnp.clip(jnp.max(jnp.abs(x), axis=-1, keepdims=True), 1e-05)
            xq = jnp.clip(jnp.round(x * scale), -128.0, 127.0) / scale
            return x + jax.lax.stop_gradient(xq - x)

        def _bitlinear(x, w):
            return jnp.einsum('bsi,oi->bso', _act_quant(x), _weight_quant(w))
        key = jax.random.key(seed)
        k0, k1, k2, k3 = jax.random.split(key, 4)
        x = jax.random.normal(k0, (4, 512, HIDDEN), dtype=jnp.float32)
        w_gate = jax.random.normal(k1, (INNER, HIDDEN), dtype=jnp.float32) / np.sqrt(HIDDEN)
        w_up = jax.random.normal(k2, (INNER, HIDDEN), dtype=jnp.float32) / np.sqrt(HIDDEN)
        w_down = jax.random.normal(k3, (HIDDEN, INNER), dtype=jnp.float32) / np.sqrt(INNER)
        return {'x': x, 'w_gate': w_gate, 'w_up': w_up, 'w_down': w_down}
    _L0_ffn_all = _L0_ffn_setup()
    _L0_ffn_in = {k: v for k, v in _L0_ffn_all.items() if k in ('w_gate', 'w_up', 'w_down')}
    del _L0_ffn_all

    def _L1_attn_setup():
        import jax, jax.numpy as jnp
        import numpy as np
        EMBED_DIM = 256
        NUM_HEADS = 16
        NUM_GLOBAL = 4
        NUM_LOCAL = NUM_HEADS - NUM_GLOBAL
        WINDOW = 64
        HEAD_DIM = EMBED_DIM // NUM_HEADS

        def _masks(seq_len):
            i = jnp.arange(seq_len)[:, None]
            j = jnp.arange(seq_len)[None, :]
            diff = i - j
            global_mask = diff < 0
            local_mask = (diff < 0) | (diff > WINDOW)
            return (global_mask, local_mask)

        def _attend(q, k, v, mask):
            scores = jnp.einsum('bhqd,bhkd->bhqk', q, k) * HEAD_DIM ** (-0.5)
            scores = jnp.where(mask[None, None], -jnp.inf, scores)
            w = jax.nn.softmax(scores, axis=-1)
            return jnp.einsum('bhqk,bhkd->bhqd', w, v)
        key = jax.random.key(seed)
        k1, k2, k3 = jax.random.split(key, 3)
        B, S = (4, 512)
        x = jax.random.normal(k1, (B, S, EMBED_DIM), dtype=jnp.float32)
        w_qkv = jax.random.normal(k2, (EMBED_DIM, 3 * EMBED_DIM), dtype=jnp.float32) * EMBED_DIM ** (-0.5)
        b_qkv = jnp.zeros((3 * EMBED_DIM,), dtype=jnp.float32)
        w_out = jax.random.normal(k3, (EMBED_DIM, EMBED_DIM), dtype=jnp.float32) * EMBED_DIM ** (-0.5)
        b_out = jnp.zeros((EMBED_DIM,), dtype=jnp.float32)
        return {'x': x, 'w_qkv': w_qkv, 'b_qkv': b_qkv, 'w_out': w_out, 'b_out': b_out}
    _L1_attn_all = _L1_attn_setup()
    _L1_attn_in = {k: v for k, v in _L1_attn_all.items() if k in ('w_qkv', 'b_qkv', 'w_out', 'b_out')}
    del _L1_attn_all

    def _L1_xattn_setup():
        import jax, jax.numpy as jnp
        import numpy as np
        D_MODEL = 256
        N_HEADS = 16
        HEAD_DIM = D_MODEL // N_HEADS
        SCALE = HEAD_DIM ** (-0.5)
        key = jax.random.key(seed)
        ks = jax.random.split(key, 11)
        B, L = (4, 512)
        s = 1.0 / np.sqrt(D_MODEL)
        inp = {'queries': jax.random.normal(ks[0], (B, L, D_MODEL), jnp.float32), 'keys': jax.random.normal(ks[1], (B, L, D_MODEL), jnp.float32), 'values': jax.random.normal(ks[2], (B, L, D_MODEL), jnp.float32), 'Wq': jax.random.normal(ks[3], (D_MODEL, D_MODEL), jnp.float32) * s, 'bq': jnp.zeros((D_MODEL,), jnp.float32), 'Wk': jax.random.normal(ks[4], (D_MODEL, D_MODEL), jnp.float32) * s, 'bk': jnp.zeros((D_MODEL,), jnp.float32), 'Wv': jax.random.normal(ks[5], (D_MODEL, D_MODEL), jnp.float32) * s, 'bv': jnp.zeros((D_MODEL,), jnp.float32), 'Wo': jax.random.normal(ks[6], (D_MODEL, D_MODEL), jnp.float32) * s, 'bo': jnp.zeros((D_MODEL,), jnp.float32)}
        return inp
    _L1_xattn_all = _L1_xattn_setup()
    _L1_xattn_in = {k: v for k, v in _L1_xattn_all.items() if k in ('Wq', 'bq', 'Wk', 'bk', 'Wv', 'bv', 'Wo', 'bo')}
    del _L1_xattn_all

    def _L1_ffn_setup():
        import jax, jax.numpy as jnp
        import numpy as np
        H = 256
        I = 512
        E = 8
        TOP_K = 2
        NUM_SHARED = 1
        key = jax.random.key(seed)
        ks = jax.random.split(key, 9)
        s = 0.02
        x = jax.random.normal(ks[0], (2, 512, H), dtype=jnp.float32)
        sg_w = jax.random.normal(ks[1], (I, H), dtype=jnp.float32) * s
        su_w = jax.random.normal(ks[2], (I, H), dtype=jnp.float32) * s
        sd_w = jax.random.normal(ks[3], (H, I), dtype=jnp.float32) * s
        router_w = jax.random.normal(ks[4], (E, H), dtype=jnp.float32) * s
        routing_bias = jnp.zeros((E,), dtype=jnp.float32)
        wg = jax.random.normal(ks[5], (E, I, H), dtype=jnp.float32) * s
        wu = jax.random.normal(ks[6], (E, I, H), dtype=jnp.float32) * s
        wd = jax.random.normal(ks[7], (E, H, I), dtype=jnp.float32) * s
        return {'x': x, 'sg_w': sg_w, 'su_w': su_w, 'sd_w': sd_w, 'router_w': router_w, 'routing_bias': routing_bias, 'wg': wg, 'wu': wu, 'wd': wd}
    _L1_ffn_all = _L1_ffn_setup()
    _L1_ffn_in = {k: v for k, v in _L1_ffn_all.items() if k in ('sg_w', 'su_w', 'sd_w', 'router_w', 'routing_bias', 'wg', 'wu', 'wd')}
    del _L1_ffn_all
    return {'x': x, 'ctx_1024': ctx_1024, 'L0_attn_Wq': _L0_attn_in['Wq'], 'L0_attn_bq': _L0_attn_in['bq'], 'L0_attn_Wk': _L0_attn_in['Wk'], 'L0_attn_bk': _L0_attn_in['bk'], 'L0_attn_Wv': _L0_attn_in['Wv'], 'L0_attn_bv': _L0_attn_in['bv'], 'L0_attn_Wp': _L0_attn_in['Wp'], 'L0_attn_bp': _L0_attn_in['bp'], 'L0_xattn_Wq': _L0_xattn_in['Wq'], 'L0_xattn_bq': _L0_xattn_in['bq'], 'L0_xattn_Wk': _L0_xattn_in['Wk'], 'L0_xattn_bk': _L0_xattn_in['bk'], 'L0_xattn_Wv': _L0_xattn_in['Wv'], 'L0_xattn_bv': _L0_xattn_in['bv'], 'L0_xattn_Wo': _L0_xattn_in['Wo'], 'L0_xattn_bo': _L0_xattn_in['bo'], 'L0_ffn_w_gate': _L0_ffn_in['w_gate'], 'L0_ffn_w_up': _L0_ffn_in['w_up'], 'L0_ffn_w_down': _L0_ffn_in['w_down'], 'L1_attn_w_qkv': _L1_attn_in['w_qkv'], 'L1_attn_b_qkv': _L1_attn_in['b_qkv'], 'L1_attn_w_out': _L1_attn_in['w_out'], 'L1_attn_b_out': _L1_attn_in['b_out'], 'L1_xattn_Wq': _L1_xattn_in['Wq'], 'L1_xattn_bq': _L1_xattn_in['bq'], 'L1_xattn_Wk': _L1_xattn_in['Wk'], 'L1_xattn_bk': _L1_xattn_in['bk'], 'L1_xattn_Wv': _L1_xattn_in['Wv'], 'L1_xattn_bv': _L1_xattn_in['bv'], 'L1_xattn_Wo': _L1_xattn_in['Wo'], 'L1_xattn_bo': _L1_xattn_in['bo'], 'L1_ffn_sg_w': _L1_ffn_in['sg_w'], 'L1_ffn_su_w': _L1_ffn_in['su_w'], 'L1_ffn_sd_w': _L1_ffn_in['sd_w'], 'L1_ffn_router_w': _L1_ffn_in['router_w'], 'L1_ffn_routing_bias': _L1_ffn_in['routing_bias'], 'L1_ffn_wg': _L1_ffn_in['wg'], 'L1_ffn_wu': _L1_ffn_in['wu'], 'L1_ffn_wd': _L1_ffn_in['wd']}

def reference(x, ctx_1024, L0_attn_Wq, L0_attn_bq, L0_attn_Wk, L0_attn_bk, L0_attn_Wv, L0_attn_bv, L0_attn_Wp, L0_attn_bp, L0_xattn_Wq, L0_xattn_bq, L0_xattn_Wk, L0_xattn_bk, L0_xattn_Wv, L0_xattn_bv, L0_xattn_Wo, L0_xattn_bo, L0_ffn_w_gate, L0_ffn_w_up, L0_ffn_w_down, L1_attn_w_qkv, L1_attn_b_qkv, L1_attn_w_out, L1_attn_b_out, L1_xattn_Wq, L1_xattn_bq, L1_xattn_Wk, L1_xattn_bk, L1_xattn_Wv, L1_xattn_bv, L1_xattn_Wo, L1_xattn_bo, L1_ffn_sg_w, L1_ffn_su_w, L1_ffn_sd_w, L1_ffn_router_w, L1_ffn_routing_bias, L1_ffn_wg, L1_ffn_wu, L1_ffn_wd):
    import jax
    import jax.numpy as jnp

    def _L0_attn_ref(x, Wq, bq, Wk, bk, Wv, bv, Wp, bp):
        import jax, jax.numpy as jnp
        import numpy as np
        HEADS = 16

        def _binarize(W):
            alpha = jnp.mean(jnp.abs(W), axis=tuple(range(1, W.ndim)), keepdims=True)
            B = W + jax.lax.stop_gradient(jnp.sign(W) - W)
            return alpha * B

        def _binlinear(x, W, b):
            Wb = _binarize(W)
            return jnp.einsum('btc,oc->bto', x, Wb) + b
        B, T, C = x.shape
        H = HEADS
        Dh = C // H
        scale = Dh ** (-0.5)

        def split_heads(t):
            return t.reshape(B, T, H, Dh).transpose(0, 2, 1, 3)
        q = split_heads(_binlinear(x, Wq, bq))
        k = split_heads(_binlinear(x, Wk, bk))
        v = split_heads(_binlinear(x, Wv, bv))
        att = jnp.einsum('bhtd,bhsd->bhts', q, k) * scale
        att = jax.nn.softmax(att, axis=-1)
        y = jnp.einsum('bhts,bhsd->bhtd', att, v)
        y = y.transpose(0, 2, 1, 3).reshape(B, T, C)
        return _binlinear(y, Wp, bp)

    def _L0_xattn_ref(x, content_embeddings, Wq, bq, Wk, bk, Wv, bv, Wo, bo):
        import jax, jax.numpy as jnp
        import numpy as np
        C = 256
        B, SQ, SKV = (4, 512, 512)
        queries = x @ Wq.T + bq
        keys = content_embeddings @ Wk.T + bk
        values = content_embeddings @ Wv.T + bv
        scale = 1.0 / jnp.sqrt(jnp.asarray(C, x.dtype))
        scores = jnp.einsum('bqc,bkc->bqk', queries, keys) * scale
        attn = jax.nn.softmax(scores, axis=-1)
        attended = jnp.einsum('bqk,bkc->bqc', attn, values)
        out = x + attended
        return out @ Wo.T + bo

    def _L0_ffn_ref(x, w_gate, w_up, w_down):
        import jax, jax.numpy as jnp
        import numpy as np
        HIDDEN = 256
        INNER = 1024

        def _weight_quant(w):
            scale = 1.0 / jnp.clip(jnp.mean(jnp.abs(w)), 1e-05)
            wq = jnp.clip(jnp.round(w * scale), -1.0, 1.0) / scale
            return w + jax.lax.stop_gradient(wq - w)

        def _act_quant(x):
            scale = 127.0 / jnp.clip(jnp.max(jnp.abs(x), axis=-1, keepdims=True), 1e-05)
            xq = jnp.clip(jnp.round(x * scale), -128.0, 127.0) / scale
            return x + jax.lax.stop_gradient(xq - x)

        def _bitlinear(x, w):
            return jnp.einsum('bsi,oi->bso', _act_quant(x), _weight_quant(w))
        gate = jax.nn.silu(_bitlinear(x, w_gate))
        up = _bitlinear(x, w_up)
        return _bitlinear(gate * up, w_down)

    def _L1_attn_ref(x, w_qkv, b_qkv, w_out, b_out):
        import jax, jax.numpy as jnp
        import numpy as np
        EMBED_DIM = 256
        NUM_HEADS = 16
        NUM_GLOBAL = 4
        NUM_LOCAL = NUM_HEADS - NUM_GLOBAL
        WINDOW = 64
        HEAD_DIM = EMBED_DIM // NUM_HEADS

        def _masks(seq_len):
            i = jnp.arange(seq_len)[:, None]
            j = jnp.arange(seq_len)[None, :]
            diff = i - j
            global_mask = diff < 0
            local_mask = (diff < 0) | (diff > WINDOW)
            return (global_mask, local_mask)

        def _attend(q, k, v, mask):
            scores = jnp.einsum('bhqd,bhkd->bhqk', q, k) * HEAD_DIM ** (-0.5)
            scores = jnp.where(mask[None, None], -jnp.inf, scores)
            w = jax.nn.softmax(scores, axis=-1)
            return jnp.einsum('bhqk,bhkd->bhqd', w, v)
        B, S, _ = x.shape
        qkv = x @ w_qkv + b_qkv
        q, k, v = jnp.split(qkv, 3, axis=-1)

        def heads(t):
            return t.reshape(B, S, NUM_HEADS, HEAD_DIM).transpose(0, 2, 1, 3)
        q, k, v = (heads(q), heads(k), heads(v))
        gmask, lmask = _masks(S)
        ctx_g = _attend(q[:, :NUM_GLOBAL], k[:, :NUM_GLOBAL], v[:, :NUM_GLOBAL], gmask)
        ctx_l = _attend(q[:, NUM_GLOBAL:], k[:, NUM_GLOBAL:], v[:, NUM_GLOBAL:], lmask)
        ctx = jnp.concatenate([ctx_g, ctx_l], axis=1)
        ctx = ctx.transpose(0, 2, 1, 3).reshape(B, S, EMBED_DIM)
        return ctx @ w_out + b_out

    def _L1_xattn_ref(queries, keys, values, Wq, bq, Wk, bk, Wv, bv, Wo, bo):
        import jax, jax.numpy as jnp
        import numpy as np
        D_MODEL = 256
        N_HEADS = 16
        HEAD_DIM = D_MODEL // N_HEADS
        SCALE = HEAD_DIM ** (-0.5)
        B, L, _ = queries.shape
        S = keys.shape[1]
        q = (queries @ Wq + bq).reshape(B, L, N_HEADS, HEAD_DIM).transpose(0, 2, 1, 3)
        k = (keys @ Wk + bk).reshape(B, S, N_HEADS, HEAD_DIM).transpose(0, 2, 1, 3)
        v = (values @ Wv + bv).reshape(B, S, N_HEADS, HEAD_DIM).transpose(0, 2, 1, 3)
        scores = jnp.einsum('bhld,bhsd->bhls', q, k) * SCALE
        weights = jax.nn.softmax(scores, axis=-1)
        out = jnp.einsum('bhls,bhsd->bhld', weights, v)
        out = out.transpose(0, 2, 1, 3).reshape(B, L, D_MODEL)
        out = out @ Wo + bo
        return out

    def _L1_ffn_ref(x, sg_w, su_w, sd_w, router_w, routing_bias, wg, wu, wd):
        import jax, jax.numpy as jnp
        import numpy as np
        H = 256
        I = 512
        E = 8
        TOP_K = 2
        NUM_SHARED = 1
        orig_shape = x.shape
        xt = x.reshape(-1, H)
        T = xt.shape[0]
        shared = jax.nn.silu(xt @ sg_w.T) * (xt @ su_w.T) @ sd_w.T
        shared = shared / NUM_SHARED
        logits = xt @ router_w.T + routing_bias
        probs = jax.nn.sigmoid(logits)
        topk_p, topk_idx = jax.lax.top_k(probs, TOP_K)
        topk_p = topk_p / jnp.sum(topk_p, axis=-1, keepdims=True)
        w = jnp.zeros((T, E), dtype=xt.dtype)
        w = w.at[jnp.arange(T)[:, None], topk_idx].add(topk_p)
        g = jnp.einsum('th,eih->tei', xt, wg)
        u = jnp.einsum('th,eih->tei', xt, wu)
        h = jax.nn.silu(g) * u
        y = jnp.einsum('tei,ehi->teh', h, wd)
        routed = jnp.einsum('te,teh->th', w, y)
        return (shared + routed).reshape(orig_shape)
    x = x + _L0_attn_ref(_layernorm(x, axis=-1), L0_attn_Wq, L0_attn_bq, L0_attn_Wk, L0_attn_bk, L0_attn_Wv, L0_attn_bv, L0_attn_Wp, L0_attn_bp)
    x = x + _L0_xattn_ref(_layernorm(x, axis=-1), ctx_1024, L0_xattn_Wq, L0_xattn_bq, L0_xattn_Wk, L0_xattn_bk, L0_xattn_Wv, L0_xattn_bv, L0_xattn_Wo, L0_xattn_bo)
    x = x + _L0_ffn_ref(_layernorm(x, axis=-1), L0_ffn_w_gate, L0_ffn_w_up, L0_ffn_w_down)
    x = x + _L1_attn_ref(_layernorm(x, axis=-1), L1_attn_w_qkv, L1_attn_b_qkv, L1_attn_w_out, L1_attn_b_out)
    x = x + _L1_xattn_ref(_layernorm(x, axis=-1), ctx_1024, ctx_1024, L1_xattn_Wq, L1_xattn_bq, L1_xattn_Wk, L1_xattn_bk, L1_xattn_Wv, L1_xattn_bv, L1_xattn_Wo, L1_xattn_bo)
    x = x + _L1_ffn_ref(_layernorm(x, axis=-1), L1_ffn_sg_w, L1_ffn_su_w, L1_ffn_sd_w, L1_ffn_router_w, L1_ffn_routing_bias, L1_ffn_wg, L1_ffn_wu, L1_ffn_wd)
    return x

_drawn_inputs = setup_inputs


def setup_inputs(seed=0):
    import zlib

    import numpy as np

    out = dict(_drawn_inputs(seed))
    spreads = {'L0_xattn_bq': (0.0, 0.499),
     'L0_xattn_bk': (0.0, 0.8),
     'L0_xattn_bv': (0.0, 0.1),
     'L0_xattn_bo': (0.0, 0.1),
     'L1_attn_b_qkv': (0.0, 0.1),
     'L1_attn_b_out': (0.0, 0.1),
     'L1_xattn_bq': (0.0, 0.549),
     'L1_xattn_bk': (0.0, 0.8),
     'L1_xattn_bv': (0.0, 0.1),
     'L1_xattn_bo': (0.0, 0.1),
     'L1_ffn_routing_bias': (0.0, 0.8)}
    factors = {'L0_attn_Wq': 8.0,
     'L0_attn_bq': 8.0,
     'L0_attn_Wk': 8.0,
     'L0_attn_bk': 8.0,
     'L0_attn_Wv': 8.0,
     'L0_attn_bv': 8.0,
     'L0_attn_Wp': 8.0,
     'L0_attn_bp': 2.751,
     'L1_ffn_sg_w': 3.913,
     'L1_ffn_su_w': 3.837,
     'L1_ffn_sd_w': 3.809,
     'L1_ffn_router_w': 6.602,
     'L1_ffn_wg': 5.713,
     'L1_ffn_wu': 5.655,
     'L1_ffn_wd': 5.637}
    for name, (base, spread) in spreads.items():
        noise = np.random.default_rng([zlib.crc32(name.encode()), seed]).standard_normal(out[name].shape)
        drawn = base * np.exp(spread * noise) if base else spread * noise
        out[name] = jnp.asarray(drawn.astype(out[name].dtype))
    for name, factor in factors.items():
        out[name] = (out[name] * factor).astype(out[name].dtype)
    return out
```

```python
from contextlib import ExitStack

import concourse.bass as bass
from concourse import mybir

F32 = mybir.dt.float32
F16 = mybir.dt.float16
BF16 = mybir.dt.bfloat16
U32 = mybir.dt.uint32
ALU = mybir.AluOpType
ACT = mybir.ActivationFunctionType
AX = mybir.AxisListType

B, T, D = 8, 512, 256
P = 128
NJ = T // P
NC = D // P
H, DH = 16, 16
NP_ = H // 2
SKV = 64
BT = NJ * D
LN_EPS = 1e-5
WS = 256.0
MS = 64.0
NEG = -1e30
BANK = 512
MAGIC = 12582912.0

LIN = ["x0q", "x0k", "x0v", "x0o", "a1q", "a1k", "a1v", "a1o", "x1q", "x1k", "x1v", "x1o"]
COL = {n: D * i for i, n in enumerate(LIN)}
NLIN = D * len(LIN)


class Count:

    def __init__(self, per):
        self.per, self.n = per, 0

    def up(self):
        self.n += 1
        return self.n

    def at(self, b):
        return b * self.per + self.n

    def done(self):
        assert self.n == self.per, (self.n, self.per)


class Core:
    pass


def tensors(nc, es, r):
    r.X = es.enter_context(nc.sbuf_tensor("X", [P, B * BT], F32))
    r.ident = es.enter_context(nc.sbuf_tensor("ident", [P, P], F32))
    r.identb = es.enter_context(nc.sbuf_tensor("identb", [P, P], BF16))
    r.ones = es.enter_context(nc.sbuf_tensor("ones", [P, P], F32))
    r.wh = es.enter_context(nc.sbuf_tensor("wh", [P, NC, NLIN], F16))
    r.wl = es.enter_context(nc.sbuf_tensor("wl", [P, NC, NLIN], F16))
    r.ps = es.enter_context(nc.psum_tensor("ps", [P, 8 * BANK], F32))


def new_semaphore(nc, r, name):
    s = nc.alloc_semaphore(name=name)
    r.semaphores.append(s)
    return s


def end_phase(nc, r):
    nc.clear_and_free_semaphores(r.semaphores)
    r.semaphores = []
    nc.all_engine_barrier()


def banks(r, first, n=1):
    return r.ps[:, first * BANK:(first + n) * BANK]


def setup_phase(nc, r, d):
    with ExitStack() as es:
        stage = es.enter_context(nc.sbuf_tensor("stage", [P, NC, NLIN], F32))
        x_in = new_semaphore(nc, r, ("x_in"))
        w_in = new_semaphore(nc, r, ("w_in"))
        w_hi = new_semaphore(nc, r, ("w_hi"))
        w_lo = new_semaphore(nc, r, ("w_lo"))
        consts = new_semaphore(nc, r, ("consts"))
        block = es.enter_context(nc.Block())

        @block.sync
        def _(sp):
            for c in range(NC):
                sp.dma_start(stage[:, c, :], d["wlin"][c * P:(c + 1) * P, :]).then_inc(w_in, 16)
            for b in range(B):
                sp.dma_start(r.X[:, b * BT:(b + 1) * BT].rearrange("p (j c) -> p j c", c=D),
                             d["x"][b].rearrange("(j p) c -> p j c", p=P)).then_inc(x_in, 16)
            sp.wait_ge(x_in, 16 * B)

        @block.gpsimd
        def _(pool):
            pool.memset(r.ones[:], 1.0).then_inc(consts, 1)
            pool.memset(r.ident[:], 0.0).then_inc(consts, 1)
            pool.memset(r.identb[:], 0.0).then_inc(consts, 1)
            pool.wait_ge(consts, 3)
            for m in (r.ident, r.identb):
                pool.affine_select(out=m[:], in_=m[:], compare_op=ALU.not_equal, fill=1.0, base=0,
                                   pattern=[[-1, P]], channel_multiplier=1).then_inc(consts, 1)

        @block.scalar
        def _(act):
            act.wait_ge(w_in, 16 * NC)
            for c in range(NC):
                act.activation(r.wh[:, c, :], stage[:, c, :], ACT.Copy, scale=WS).then_inc(w_hi, 1)

        @block.vector
        def _(ve):
            for c in range(NC):
                ve.wait_ge(w_hi, c + 1)
                ve.scalar_tensor_tensor(out=r.wl[:, c, :], in0=stage[:, c, :], scalar=WS,
                                        in1=r.wh[:, c, :], op0=ALU.mult, op1=ALU.subtract).then_inc(w_lo, 1)


class Norm:

    def __init__(self, nc, es, tag, r):
        sb = lambda n, s: es.enter_context(nc.sbuf_tensor(f"{tag}_{n}", s, F32))
        sem = lambda n: new_semaphore(nc, r, (f"{tag}_{n}"))
        self.stats, self.mv = sb("stats", [P, NJ, 6]), sb("mv", [P, NJ, 2])
        self.var, self.rstd = sb("var", [P, NJ]), sb("rstd", [P, NJ])
        self.power, self.pad = sb("power", [P, NJ]), sb("pad", [P, 1])
        self.xn = sb("xn", [P, NJ, D])
        self.step, self.var_ready, self.rstd_ready = sem("norm_step"), sem("var_ready"), sem("rstd_ready")
        self.power_ready = sem("power_ready")
        self.xn_ready = sem("xn_ready")

    def vector(self, ve, r, b):
        steps = Count(8)
        x = [r.X[:, bass.ds(b * BT + j * D, D)] for j in range(NJ)]
        for j in range(NJ):
            ve.bn_stats(self.stats[:, j, :], x[j]).then_inc(self.step, 1)
            steps.up()
        ve.wait_ge(self.step, steps.at(b))
        ve.memset(self.pad[:], 0.0)
        for j in range(NJ):
            ve.bn_aggr(self.mv[:, j, :], self.stats[:, j, :]).then_inc(self.step, 1)
            steps.up()
        ve.wait_ge(self.step, steps.at(b))
        ve.tensor_scalar(self.var[:], self.mv[:, :, 1], LN_EPS, None, ALU.add).then_inc(self.var_ready, 1)
        ve.wait_ge(self.rstd_ready, b + 1)
        for j in range(NJ):
            last = ve.tensor_scalar(self.xn[:, j, :], x[j], self.mv[:, j, 0:1], self.rstd[:, j:j + 1],
                                    ALU.subtract, ALU.mult)
        last.then_inc(self.xn_ready, 1)
        steps.done()

    def pool_start(self, pool):
        pool.memset(self.power[:], -0.5).then_inc(self.power_ready, 1)
        pool.wait_ge(self.power_ready, 1)

    def pool(self, pool, b):
        pool.wait_ge(self.var_ready, b + 1)
        pool.tensor_tensor(self.rstd[:], self.var[:], self.power[:], ALU.pow).then_inc(self.rstd_ready, 1)


def transpose_tiles(nc, r, src, bank):
    for c in range(NC):
        for j in range(NJ):
            last = nc.tensor.transpose(banks(r, bank + c)[:, j * P:(j + 1) * P],
                                       src[:, j, c * P:(c + 1) * P], r.ident[:])
    return last


def product(nc, out, terms):
    for n, (lhs, rhs) in enumerate(terms):
        last = nc.tensor.matmul(out, lhs, rhs, start=(n == 0), stop=(n == len(terms) - 1))
    return last


class Piece:

    def __init__(self, at, idx, lo, n, mask=None, mask_at=0):
        self.at, self.idx, self.lo, self.n, self.mask, self.mask_at = at, idx, lo, n, mask, mask_at


def full_head():
    return [([Piece(BANK * k, 2 * s + k, 0, T) for k in range(2)], [(0, 2, BANK, T, 2 * s)]) for s in range(2)]


def causal_head_max(mask):
    out = []
    for s in range(2):
        ps = [Piece(BANK * k, 2 * s + k, 0, (2 * s + k + 1) * P, mask, (2 * s + k) * P) for k in range(2)]
        out.append((ps, [(p.at, 1, BANK, p.n, p.idx) for p in ps]))
    return out


def causal_head_main(mask):
    out = []
    for s in range(2):
        ps = [Piece(BANK * k, 2 * s + k, (2 * s + k) * P, T - (2 * s + k) * P, mask, 0) for k in range(2)]
        out.append((ps, [(p.at, 1, BANK, p.n, p.idx) for p in ps]))
    return out


WIN = 64
LW = P + WIN


def local_head_max(mask, mask0):
    ps = [Piece(256 * j, j, max(0, j * P - WIN), LW, mask if j else mask0) for j in range(NJ)]
    return [(ps, [(0, NJ, 256, LW, 0)])]


def local_head_main(mask, mask3):
    ps = [Piece(256 * s, s, min(s * P, T - LW), LW, mask if s < NJ - 1 else mask3) for s in range(NJ)]
    return [(ps, [(0, NJ, 256, LW, 0)])]


def attention_phase(nc, r, d, layer, nb=B):
    binary = layer == 0
    tag = f"at{layer}"
    with ExitStack() as es:
        sb = lambda n, s, t=F32: es.enter_context(nc.sbuf_tensor(f"{tag}_{n}", s, t))
        sem = lambda n: new_semaphore(nc, r, (f"{tag}_{n}"))
        norm = Norm(nc, es, tag, r)
        xh, xl = sb("xh", [P, NC, T], F16), sb("xl", [P, NC, T], F16)
        qk32 = sb("qk32", [P, 4, T])
        qkh, qkl = sb("qkh", [P, 4, T], F16), sb("qkl", [P, 4, T], F16)
        qs = sb("qs", [P, NP_, T], F16)
        ks = sb("ks", [P, H, T], F16)
        vaug = sb("vaug", [P, NJ, H, 32])
        mx = sb("mx", [P, NJ, H])
        mh, ml = sb("mh", [H, T], F16), sb("ml", [H, T], F16)
        nrow = sb("nrow", [2, NP_, T], F16)
        krow = sb("krow", [2, T], F16)
        pexp = sb("pexp", [P, 2, 4, NJ, T])
        ot = sb("ot", [P, 4, T])
        rec = sb("rec", [P, NJ, H])
        y = norm.xn
        yh, yl, y32 = xh, xl, qk32[:, 0:2, :]
        res = qk32[:, 2:4, :].rearrange("p a b -> p (a b)")
        bias_out = sb("bias_out", [P, D])
        bqk = sb("bqk", [P, 4, 1])
        if binary:
            stage = pexp[:, 0, 0:4, 0, :].rearrange("p a (c n) -> p a c n", c=NC)
            wabs = pexp[:, 1, 0:4, 0, :].rearrange("p a (c n) -> p a c n", c=NC)
            wsign = sb("wsign", [P, 4, NC, D], F16)
            bv = sb("bv", [P, NC, 1])
            alpha = sb("alpha", [P, 6, 1])
            alpha_out = sb("alpha_out", [P, D])
        else:
            bv_row = sb("bv_row", [P, D])
            masks = [sb(f"mask{i}", [P, LW], BF16) for i in range(6)]
        scratch = es.enter_context(nc.dram_tensor(f"{tag}_scratch", (2, P, 4, T), F16, kind="Internal")).ap() \
            if False else nc.dram_tensor(f"{tag}_scratch", (2, P, 4, T), F16, kind="Internal").ap()

        w_in, consts, mask_zero, w_abs, alpha_done, alpha_ready = (sem(n) for n in ("w_in", "consts", "mask_zero", "w_abs", "alpha_done", "alpha_ready"))
        step, xt_done, xh_ready, xl_ready = (sem(n) for n in ("step", "xt_done", "xh_ready", "xl_ready"))
        proj_done, projv_done, qk_ready, qkl_ready, v_ready = (sem(n) for n in ("proj_done", "projv_done", "qk_ready", "qkl_ready", "v_ready"))
        saved, stacked, mxs_ready, mx_read, mt_done = (sem(n) for n in ("saved", "stacked", "mxs_ready", "mx_read", "mt_done"))
        mh_ready, ml_ready, rows_in, st_ready, exp_done = (sem(n) for n in ("mh_ready", "ml_ready", "rows_in", "st_ready", "exp_done"))
        av_done, ot_ready, ott_done, y_ready, yt_done = (sem(n) for n in ("av_done", "ot_ready", "ott_done", "y_ready", "yt_done"))
        y32_ready, yl_ready, out_done = (sem(n) for n in ("y32_ready", "yl_ready", "out_done"))

        if binary:
            heads_max = heads_main = [full_head() for _ in range(H)]
        else:
            NG = 4
            heads_max = [causal_head_max(masks[0]) if h < NG else local_head_max(masks[1], masks[2]) for h in range(H)]
            heads_main = [causal_head_main(masks[3]) if h < NG else local_head_main(masks[4], masks[5]) for h in range(H)]
        max_slots = [(h, *slot) for h in range(H) for slot in heads_max[h]]
        main_slots = [(h, *slot) for h in range(H) for slot in heads_main[h]]
        NMAX, NMAIN = len(max_slots), len(main_slots)
        slots_upto = [sum(len(heads_main[h]) for h in range(4 * (g + 1))) for g in range(4)]
        MAXB, MAINB = (0, 6), (2, 4)

        block = es.enter_context(nc.Block())

        @block.sync
        def _(sp):
            n_const = 0

            def const(dst, src):
                sp.dma_start(dst, src, allow_slow_non_contiguous=True).then_inc(w_in, 16)
            if binary:
                for a in range(4):
                    const(stage[:, a], d["w0"][:, a * D:(a + 1) * D].rearrange("(c p) n -> p c n", p=P))
                const(bv[:], d["a0_bv"].rearrange("(c p) -> p c", p=P).unsqueeze(2))
                const(bqk[:, 0:2], d["a0_bq"].rearrange("(c p) -> p c", p=P).unsqueeze(2))
                const(bqk[:, 2:4], d["a0_bk"].rearrange("(c p) -> p c", p=P).unsqueeze(2))
                const(bias_out[:], d["a0_bp"].partition_broadcast(P))
            else:
                const(bqk[:], d["a1_bqkv"][0:2 * D].rearrange("(c p) -> p c", p=P).unsqueeze(2))
                const(bv_row[:], d["a1_bqkv"][2 * D:3 * D].partition_broadcast(P))
                const(bias_out[:], d["a1_bout"].partition_broadcast(P))
            sp.wait_ge(consts, 3)
            for par in range(2):
                for h in range(par * NP_, (par + 1) * NP_):
                    sp.dma_start(ks[64 * par + 48:64 * par + 50, h, :], krow[:]).then_inc(stacked, 16)
            const_dmas = H
            sp.wait_ge(stacked, 16 * const_dmas)
            with sp.Fori(0, nb) as b:
                sp.wait_ge(qk_ready, (b + 1) * 4)
                sp.dma_start(scratch[0], qkh[:]).then_inc(saved, 16)
                sp.wait_ge(qkl_ready, (b + 1) * 4)
                sp.dma_start(scratch[1], qkl[:]).then_inc(saved, 16)
                sp.wait_ge(saved, (b + 1) * 32)
                for par in range(2):
                    for rep, (qpart, kpart) in enumerate(((0, 0), (0, 1), (1, 0))):
                        rows = slice(64 * par + 16 * rep, 64 * par + 16 * rep + 16)
                        sp.dma_start(qs[rows, :, :], scratch[qpart][:, par, :].rearrange("(i d) t -> d i t", d=DH)).then_inc(stacked, 16)
                        sp.dma_start(ks[rows, par * NP_:(par + 1) * NP_, :],
                                     scratch[kpart][:, 2 + par, :].rearrange("(i d) t -> d i t", d=DH)).then_inc(stacked, 16)
                    sp.dma_start(qs[64 * par + 48:64 * par + 50, :, :], nrow[:]).then_inc(stacked, 16)
                sp.wait_ge(ml_ready, b + 1)
                sp.wait_ge(stacked, 16 * (14 * (b + 1) + const_dmas))
                for par in range(2):
                    for row, m in ((48, mh), (49, ml)):
                        sp.dma_start(qs[64 * par + row:64 * par + row + 1, :, :], m[par * NP_:(par + 1) * NP_, :]).then_inc(rows_in, 16)
            sp.wait_ge(rows_in, 16 * 4 * nb)

        @block.gpsimd
        def _(pool):
            pool.memset(krow[:], MS).then_inc(consts, 1)
            pool.memset(nrow[:], 0.0).then_inc(consts, 1)
            if not binary:
                for m in masks:
                    pool.memset(m[:], 0.0).then_inc(mask_zero, 1)
                pool.wait_ge(mask_zero, 6)

                def keep(m, base, step, mult):
                    return pool.affine_select(out=m[:], in_=m[:], compare_op=ALU.is_ge, fill=NEG, base=base,
                                              pattern=[[step, LW]], channel_multiplier=mult)
                keep(masks[0], 0, -1, 1).then_inc(w_abs, 1)
                keep(masks[1], WIN, -1, 1).then_inc(w_abs, 1)
                keep(masks[2], 0, -1, 1).then_inc(w_abs, 1)
                keep(masks[3], 0, 1, -1).then_inc(w_abs, 1)
                keep(masks[4], 0, 1, -1).then_inc(w_abs, 1)
                keep(masks[5], -WIN, 1, -1).then_inc(w_abs, 1)
                pool.wait_ge(w_abs, 6)
                keep(masks[1], 0, 1, -1).then_inc(w_abs, 1)
                keep(masks[2], WIN, 1, -1).then_inc(w_abs, 1)
                keep(masks[4], WIN, -1, 1).then_inc(w_abs, 1)
                keep(masks[5], 2 * WIN, -1, 1).then_inc(w_abs, 1)
            norm.pool_start(pool)
            with pool.Fori(0, nb) as b:
                norm.pool(pool, b)
                for m in range(4):
                    pool.wait_ge(qk_ready, b * 4 + m + 1)
                    pool.tensor_tensor(qkl[:, m, :], qk32[:, m, :], qkh[:, m, :], ALU.subtract).then_inc(qkl_ready, 1)

        @block.scalar
        def _(act):
            act.wait_ge(w_in, 16 * (8 if binary else 3))
            if binary:
                act.activation(wsign[:].rearrange("p a c n -> p (a c n)"), stage.rearrange("p a c n -> p a (c n)") if False else
                               pexp[:, 0, 0:4, 0, :], ACT.Sign).then_inc(w_abs, 1)
                act.activation(pexp[:, 1, 0:4, 0, :], pexp[:, 0, 0:4, 0, :], ACT.Abs).then_inc(w_abs, 1)
                act.wait_ge(alpha_done, 1)
                act.activation(alpha[:].rearrange("p a b -> p (a b)"), banks(r, 0)[:, 0:6], ACT.Copy, scale=1.0 / D).then_inc(alpha_ready, 1)
                act.activation(alpha_out[:], banks(r, 1)[:, 0:D], ACT.Copy, scale=1.0 / D).then_inc(alpha_ready, 1)
                act.wait_ge(alpha_ready, 2)
            with act.Fori(0, nb) as b:
                act.wait_ge(xt_done, b + 1)
                act.activation(xh[:].rearrange("p c t -> p (c t)"), banks(r, 0, 2), ACT.Copy).then_inc(xh_ready, 1)
                for m in range(4):
                    act.wait_ge(proj_done, b * 4 + m + 1)
                    scale = alpha[:, m, :] if binary else 1.0 / WS
                    act.activation(qk32[:, m, :], banks(r, 2 + m), ACT.Identity, bias=bqk[:, m, :], scale=scale)
                    act.activation(qkh[:, m, :], banks(r, 2 + m), ACT.Identity, bias=bqk[:, m, :], scale=scale).then_inc(qk_ready, 1)
                act.wait_ge(mt_done, b + 1)
                act.activation(mh[:], banks(r, 0)[0:H, :], ACT.Copy, scale=-1.0 / MS).then_inc(mh_ready, 1)
                for k, (h, pieces, reads) in enumerate(main_slots):
                    act.wait_ge(st_ready, b * NMAIN + k + 1)
                    if k in slots_upto[1:3]:
                        g = slots_upto.index(k)
                        act.wait_ge(av_done, b * 4 + g)
                    bank = banks(r, MAINB[k % 2], 2)
                    for at, n, stride, length, idx in reads:
                        src = bank[:, at:at + (n - 1) * stride + length] if n == 1 else \
                            bank.rearrange("p (n w) -> p n w", w=stride)[:, :n, 0:length]
                        dst = pexp[:, (h // 4) % 2, h % 4, idx:idx + n, 0:length]
                        if n == 1:
                            dst = pexp[:, (h // 4) % 2, h % 4, idx, 0:length]
                        last = act.activation(dst, src, ACT.Exp, scale=DH ** -0.5)
                    last.then_inc(exp_done, 1)
                act.wait_ge(yt_done, b + 1)
                src = banks(r, 2, 2)
                if binary:
                    for c in range(NC):
                        act.activation(y32[:, c, :], banks(r, 2 + c), ACT.Identity, bias=bv[:, c, :], scale=alpha[:, 4 + c, :])
                        last = act.activation(yh[:, c, :], banks(r, 2 + c), ACT.Identity, bias=bv[:, c, :], scale=alpha[:, 4 + c, :])
                    last.then_inc(y32_ready, 1)
                else:
                    act.activation(yh[:].rearrange("p c t -> p (c t)"), src, ACT.Copy).then_inc(y32_ready, 1)

        @block.vector
        def _(ve):
            ve.memset(ks[:], 0.0).then_inc(consts, 1)
            ve.memset(vaug[:], 0.0).then_inc(step, 1)
            ve.memset(qs[:], 0.0).then_inc(step, 1)
            ve.wait_ge(step, 2)
            ve.memset(vaug[:, :, :, DH:DH + 1], 1.0).then_inc(step, 1)
            ve.wait_ge(step, 3)
            ve.wait_ge(w_in, 16 * (8 if binary else 3))
            if binary:
                ve.wait_ge(alpha_ready, 2)
            PER = 4 + (2 if binary else 1)
            with ve.Fori(0, nb) as b:
                steps = Count(PER)
                norm.vector(ve, r, b)
                ve.wait_ge(xh_ready, b + 1)
                ve.tensor_tensor(xl[:].rearrange("p c t -> p (c t)"), banks(r, 0, 2), xh[:].rearrange("p c t -> p (c t)"), ALU.subtract).then_inc(xl_ready, 1)
                ve.wait_ge(projv_done, b + 1)
                v_ps = banks(r, 6, 2)
                if binary:
                    ve.tensor_copy(vaug[:].rearrange("p s h e -> p (s h) e")[:, :, 0:DH], v_ps.rearrange("p (n e) -> p n e", e=DH)).then_inc(v_ready, 1)
                else:
                    for s in range(NJ):
                        last = ve.scalar_tensor_tensor(out=vaug[:, s, :, 0:DH], in0=v_ps[:, s * D:(s + 1) * D].rearrange("p (h e) -> p h e", e=DH),
                                                       scalar=1.0 / WS, in1=bv_row[:].rearrange("p (h e) -> p h e", e=DH), op0=ALU.mult, op1=ALU.add)
                    last.then_inc(v_ready, 1)
                for k, (h, pieces, reads) in enumerate(max_slots):
                    ve.wait_ge(mxs_ready, b * NMAX + k + 1)
                    bank = banks(r, MAXB[k % 2], 2)
                    for at, n, stride, length, idx in reads:
                        src = bank[:, at:at + length] if n == 1 else bank.rearrange("p (n w) -> p n w", w=stride)[:, :n, 0:length]
                        last = ve.reduce_max(mx[:, idx:idx + n, h], src, AX.X)
                    last.then_inc(mx_read, 1)
                ve.wait_ge(mh_ready, b + 1)
                ve.scalar_tensor_tensor(out=ml[:], in0=banks(r, 0)[0:H, :], scalar=-1.0 / MS, in1=mh[:], op0=ALU.mult, op1=ALU.subtract).then_inc(ml_ready, 1)
                for g in range(4):
                    ve.wait_ge(av_done, b * 4 + g + 1)
                    ve.tensor_copy(ot[:, g, :], banks(r, 6 + g % 2)).then_inc(ot_ready, 1)
                for j in range(NJ):
                    ve.wait_ge(ott_done, b * NJ + j + 1)
                    o = banks(r, j % 2).rearrange("p (h e) -> p h e", e=32)
                    ve.reciprocal(rec[:, j, :], o[:, :, DH]).then_inc(step, 1)
                    steps.up()
                    ve.wait_ge(step, steps.at(b) + 3)
                    ve.tensor_tensor(y[:, j, :].rearrange("p (h e) -> p h e", e=DH), o[:, :, 0:DH],
                                     rec[:, j, :].unsqueeze(2).broadcast_to([P, H, DH]), ALU.mult).then_inc(y_ready, 1)
                ve.wait_ge(y32_ready, b + 1)
                yl_f, yh_f = yl[:].rearrange("p c t -> p (c t)"), yh[:].rearrange("p c t -> p (c t)")
                ve.tensor_tensor(yl_f, y32.rearrange("p c t -> p (c t)") if binary else banks(r, 2, 2), yh_f, ALU.subtract).then_inc(yl_ready, 1)
                ve.wait_ge(out_done, b + 1)
                x = r.X[:, bass.ds(b * BT, BT)]
                if binary:
                    ve.tensor_tensor(res.rearrange("p (j n) -> p j n", n=D), banks(r, 4, 2).rearrange("p (j n) -> p j n", n=D),
                                     alpha_out[:].unsqueeze(1).broadcast_to([P, NJ, D]), ALU.mult).then_inc(step, 1)
                    steps.up()
                    ve.wait_ge(step, steps.at(b) + 3)
                    ve.tensor_tensor(x, x, res, ALU.add).then_inc(step, 1)
                else:
                    ve.scalar_tensor_tensor(out=x, in0=banks(r, 4, 2), scalar=1.0 / WS, in1=x, op0=ALU.mult, op1=ALU.add).then_inc(step, 1)
                steps.up()
                ve.wait_ge(step, steps.at(b) + 3)
                ve.tensor_tensor(x.rearrange("p (j n) -> p j n", n=D), x.rearrange("p (j n) -> p j n", n=D),
                                 bias_out[:].unsqueeze(1).broadcast_to([P, NJ, D]), ALU.add)
                steps.done()

        @block.tensor
        def _(pe):
            if binary:
                pe.wait_ge(w_abs, 2)
                for a in range(6):
                    for c in range(NC):
                        nc.tensor.matmul(banks(r, 0)[:, a:a + 1], wabs[:, a // 2, c, (a % 2) * P:(a % 2 + 1) * P], r.ones[:, 0:1],
                                         start=(c == 0), stop=(c == NC - 1))
                for c in range(NC):
                    last = nc.tensor.matmul(banks(r, 1)[:, 0:D], r.ones[:], wabs[:, 3, c, :], start=(c == 0), stop=(c == NC - 1))
                last.then_inc(alpha_done, 1)
                pe.wait_ge(alpha_ready, 2)
            else:
                pe.wait_ge(w_abs, 10)
                pe.wait_ge(consts, 3)

            def weights(name, m0, m1):
                if binary:
                    a = "qkvo".index(name)
                    return [(wsign[:, a, c, m0:m1], c, part) for c in range(NC) for part in (xh, xl)]
                at = COL[f"a1{name}"]
                return [(w[:, c, at + m0:at + m1], c, part) for c in range(NC) for w, part in ((r.wh, xh), (r.wh, xl), (r.wl, xh))]

            with pe.Fori(0, nb) as b:
                pe.wait_ge(norm.xn_ready, b + 1)
                transpose_tiles(nc, r, norm.xn, 0).then_inc(xt_done, 1)
                pe.wait_ge(xh_ready, b + 1)
                pe.wait_ge(xl_ready, b + 1)
                for m in range(4):
                    product(nc, banks(r, 2 + m), [(w, part[:, c, :]) for w, c, part in weights("qk"[m // 2], (m % 2) * P, (m % 2 + 1) * P)]).then_inc(proj_done, 1)
                for s in range(NJ):
                    last = product(nc, banks(r, 6, 2)[:, s * D:(s + 1) * D],
                                   [(part[:, c, s * P:(s + 1) * P], w) for w, c, part in weights("v", 0, D)])
                last.then_inc(projv_done, 1)
                pe.wait_ge(stacked, 16 * (14 * (b + 1) + H))
                pe.wait_ge(v_ready, b + 1)
                for k, (h, pieces, reads) in enumerate(max_slots):
                    if k >= 2:
                        pe.wait_ge(mx_read, b * NMAX + k - 1)
                    for p in pieces:
                        out = banks(r, MAXB[k % 2], 2)[:, p.at:p.at + p.n]
                        last = nc.tensor.matmul(out, qs[:, h % NP_, p.idx * P:(p.idx + 1) * P], ks[:, h, p.lo:p.lo + p.n],
                                                start=True, stop=True)
                        if p.mask is not None:
                            n = P if h < 4 else LW
                            last = nc.tensor.matmul(out[:, p.mask_at:p.mask_at + n], r.identb[:], p.mask[:, 0:n], start=False, stop=True,
                                                    skip_group_check=True)
                    last.then_inc(mxs_ready, 1)
                pe.wait_ge(mx_read, (b + 1) * NMAX)
                for j in range(NJ):
                    last = nc.tensor.transpose(banks(r, 0)[0:H, j * P:(j + 1) * P], mx[:, j, :], r.ident[:])
                last.then_inc(mt_done, 1)
                pe.wait_ge(rows_in, 64 * (b + 1))
                pe.wait_ge(qk_ready, 4 * (b + 1))

                def values(g):
                    pe.wait_ge(exp_done, b * NMAIN + slots_upto[g])
                    if g >= 2:
                        pe.wait_ge(ot_ready, b * 4 + g - 1)
                    for s in range(NJ):
                        for hh in range(4):
                            h = 4 * g + hh
                            p = [p for slot in heads_main[h] for p in slot[0] if p.idx == s][0]
                            last = nc.tensor.matmul(banks(r, 6 + g % 2)[32 * hh:32 * hh + 32, p.lo:p.lo + p.n], vaug[:, s, h, :],
                                                    pexp[:, g % 2, hh, s, 0:p.n], start=(s == 0), stop=(s == NJ - 1) or not binary,
                                                    skip_group_check=True)
                    return last

                for k, (h, pieces, reads) in enumerate(main_slots):
                    if k >= 2:
                        pe.wait_ge(exp_done, b * NMAIN + k - 1)
                    for p in pieces:
                        out = banks(r, MAINB[k % 2], 2)[:, p.at:p.at + p.n]
                        last = nc.tensor.matmul(out, ks[:, h, p.idx * P:(p.idx + 1) * P], qs[:, h % NP_, p.lo:p.lo + p.n],
                                                start=True, stop=True)
                        if p.mask is not None:
                            n = P if h < 4 else LW
                            last = nc.tensor.matmul(out[:, 0:n], r.identb[:], p.mask[:, 0:n], start=False, stop=True,
                                                    skip_group_check=True)
                    last.then_inc(st_ready, 1)
                    if k + 1 in slots_upto[1:]:
                        values(slots_upto.index(k + 1) - 1).then_inc(av_done, 1)
                values(3).then_inc(av_done, 1)
                pe.wait_ge(ot_ready, 4 * (b + 1))
                for j in range(NJ):
                    if j >= 2:
                        pe.wait_ge(y_ready, b * NJ + j - 1)
                    for g in range(4):
                        last = nc.tensor.transpose(banks(r, j % 2)[:, g * P:(g + 1) * P], ot[:, g, j * P:(j + 1) * P], r.ident[:])
                    last.then_inc(ott_done, 1)
                pe.wait_ge(y_ready, NJ * (b + 1))
                transpose_tiles(nc, r, y, 2).then_inc(yt_done, 1)
                pe.wait_ge(yl_ready, b + 1)
                for j in range(NJ):
                    last = product(nc, banks(r, 4, 2)[:, j * D:(j + 1) * D],
                                   [(part[:, c, j * P:(j + 1) * P], w) for w, c, part in weights("o", 0, D)])
                last.then_inc(out_done, 1)


def load_phase(nc, r, d, src):
    pass


def store_phase(nc, r, out, nb=B):
    with ExitStack() as es:
        stored = new_semaphore(nc, r, ("stored"))
        block = es.enter_context(nc.Block())

        @block.sync
        def _(sp):
            for b in range(nb):
                sp.dma_start(out[b].rearrange("(j p) c -> p j c", p=P),
                             r.X[:, b * BT:(b + 1) * BT].rearrange("p (j c) -> p j c", c=D)).then_inc(stored, 16)
            sp.wait_ge(stored, 16 * nb)


def layout(inp):
    import numpy as np
    f = {k: np.asarray(v) for k, v in inp.items()}
    tr = lambda a: np.ascontiguousarray(np.swapaxes(a, -1, -2))
    a = {"x": f["x"], "ctxT": np.ascontiguousarray(f["ctx_1024"].reshape(B * SKV, D).T)}
    a["w0"] = np.concatenate([tr(f[f"L0_attn_W{n}"]) for n in "qkvp"], axis=1)
    a["wlin"] = np.concatenate([tr(f[f"L0_xattn_W{n}"]) for n in "qkvo"] + [f["L1_attn_w_qkv"], f["L1_attn_w_out"]]
                               + [f[f"L1_xattn_W{n}"] for n in "qkvo"], axis=1)
    for n in "qkvp":
        a[f"a0_b{n}"] = f[f"L0_attn_b{n}"]
    a["a1_bqkv"], a["a1_bout"] = f["L1_attn_b_qkv"], f["L1_attn_b_out"]
    for n in "qkvo":
        a[f"x0_b{n}"], a[f"x1_b{n}"] = f[f"L0_xattn_b{n}"], f[f"L1_xattn_b{n}"]
    a["f_gate"], a["f_up"], a["f_down"] = tr(f["L0_ffn_w_gate"]), tr(f["L0_ffn_w_up"]), tr(f["L0_ffn_w_down"])
    for n, s, w in (("gate", "sg_w", "wg"), ("up", "su_w", "wu"), ("down", "sd_w", "wd")):
        a[f"m_{n}"] = np.concatenate([tr(f[f"L1_ffn_{s}"])[None], tr(f[f"L1_ffn_{w}"])])
    a["m_router"], a["m_bias"] = tr(f["L1_ffn_router_w"]), f["L1_ffn_routing_bias"]
    return a


def build(nc, d, out, phases=("at0", "x0", "ff0", "at1", "x1", "moe"), nb=B):
    r = Core()
    r.semaphores = []
    with ExitStack() as es:
        tensors(nc, es, r)
        setup_phase(nc, r, d)
        end_phase(nc, r)
        for p in phases:
            if p == "at0":
                attention_phase(nc, r, d, 0, nb)
            if p == "at1":
                attention_phase(nc, r, d, 1, nb)
            if p == "x0":
                cross0_phase(nc, r, d, nb)
            if p == "ff0":
                quant_ffn_phase(nc, r, d, nb)
            if p == "x1":
                cross1_phase(nc, r, d, nb)
            if p == "moe":
                experts_phase(nc, r, d, nb)
            end_phase(nc, r)
        store_phase(nc, r, out, nb)


def cross0_phase(nc, r, d, nb=B):
    tag = "x0"
    scale = float(D) ** -0.5
    with ExitStack() as es:
        sb = lambda n, s, t=F32: es.enter_context(nc.sbuf_tensor(f"{tag}_{n}", s, t))
        sem = lambda n: new_semaphore(nc, r, (f"{tag}_{n}"))
        norm = Norm(nc, es, tag, r)
        ctx32, ctxh, ctxl = sb("ctx32", [P, NC, B * SKV]), sb("ctxh", [P, NC, B * SKV], F16), sb("ctxl", [P, NC, B * SKV], F16)
        k32, kh, kl = sb("k32", [P, NC, B * SKV]), sb("kh", [P, NC, B * SKV], F16), sb("kl", [P, NC, B * SKV], F16)
        v_all, vcur = sb("v_all", [SKV, B * D]), sb("vcur", [SKV, D])
        x32, xh, xl = sb("x32", [P, NC, T]), sb("xh", [P, NC, T], F16), sb("xl", [P, NC, T], F16)
        q32, qh, ql = sb("q32", [P, NC, T]), sb("qh", [P, NC, T], F16), sb("ql", [P, NC, T], F16)
        mx, nm, total, rec = sb("mx", [P, NJ]), sb("nm", [P, NJ]), sb("total", [P, NJ]), sb("rec", [P, NJ])
        e, pr, pt = sb("e", [P, NJ, SKV]), sb("pr", [P, NJ, SKV]), sb("pt", [SKV, T])
        z32, zh, zl = sb("z32", [P, NC, T]), sb("zh", [P, NC, T], F16), sb("zl", [P, NC, T], F16)
        bq, bk = sb("bq", [P, NC, 1]), sb("bk", [P, NC, 1])
        bv_row, bias_out = sb("bv_row", [SKV, D]), sb("bias_out", [P, D])
        (w_in, ctxh_ready, ctxl_ready, kps_done, k32_ready, kh_ready, kl_ready, vps_done, v_ready) = (
            sem(n) for n in ("w_in", "ctxh_ready", "ctxl_ready", "kps_done", "k32_ready", "kh_ready", "kl_ready", "vps_done", "v_ready"))
        (xt_done, xh_ready, xl_ready, q_done, q_ready, ql_ready, s_done, nm_ready, e_ready, p_ready, pt_done, pt_ready) = (
            sem(n) for n in ("xt_done", "xh_ready", "xl_ready", "q_done", "q_ready", "ql_ready", "s_done", "nm_ready", "e_ready", "p_ready", "pt_done", "pt_ready"))
        (vcur_ready, att_done, z_ready, zh_ready, zl_ready, out_done, step) = (
            sem(n) for n in ("vcur_ready", "att_done", "z_ready", "zh_ready", "zl_ready", "out_done", "step"))
        flat = lambda t: t[:].rearrange("p c t -> p (c t)")
        block = es.enter_context(nc.Block())

        def three(name, m0, m1, hi, lo):
            at = COL[f"x0{name}"]
            return [(w[:, c, at + m0:at + m1], c, part) for c in range(NC) for w, part in ((r.wh, hi), (r.wh, lo), (r.wl, hi))]

        @block.sync
        def _(sp):
            def const(dst, src):
                sp.dma_start(dst, src, allow_slow_non_contiguous=True).then_inc(w_in, 16)
            const(ctx32[:], d["ctxT"].rearrange("(c p) n -> p c n", p=P))
            const(bq[:], d["x0_bq"].rearrange("(c p) -> p c", p=P).unsqueeze(2))
            const(bk[:], d["x0_bk"].rearrange("(c p) -> p c", p=P).unsqueeze(2))
            const(bv_row[:], d["x0_bv"].partition_broadcast(SKV))
            const(bias_out[:], d["x0_bo"].partition_broadcast(P))

        @block.gpsimd
        def _(pool):
            norm.pool_start(pool)
            with pool.Fori(0, nb) as b:
                norm.pool(pool, b)
                pool.wait_ge(q_ready, b + 1)
                pool.tensor_tensor(ql[:], q32[:], qh[:], ALU.subtract).then_inc(ql_ready, 1)
                pool.wait_ge(zh_ready, b + 1)
                pool.tensor_tensor(zl[:], z32[:], zh[:], ALU.subtract).then_inc(zl_ready, 1)

        @block.scalar
        def _(act):
            act.wait_ge(w_in, 16 * 5)
            act.activation(ctxh[:], ctx32[:], ACT.Copy).then_inc(ctxh_ready, 1)
            act.wait_ge(kps_done, 1)
            for m in range(NC):
                act.activation(k32[:, m, :], banks(r, 2 + m), ACT.Identity, bias=bk[:, m, :], scale=1.0 / WS)
                last = act.activation(kh[:, m, :], banks(r, 2 + m), ACT.Identity, bias=bk[:, m, :], scale=1.0 / WS)
            last.then_inc(kh_ready, 1)
            with act.Fori(0, nb) as b:
                act.wait_ge(xt_done, b + 1)
                act.activation(flat(xh), banks(r, 0, 2), ACT.Copy).then_inc(xh_ready, 1)
                act.activation(flat(x32), banks(r, 0, 2), ACT.Copy).then_inc(xh_ready, 1)
                act.wait_ge(q_done, b + 1)
                for m in range(NC):
                    act.activation(q32[:, m, :], banks(r, 2 + m), ACT.Identity, bias=bq[:, m, :], scale=1.0 / WS)
                    last = act.activation(qh[:, m, :], banks(r, 2 + m), ACT.Identity, bias=bq[:, m, :], scale=1.0 / WS)
                last.then_inc(q_ready, 1)
                act.wait_ge(nm_ready, b + 1)
                for j in range(NJ):
                    last = act.activation(e[:, j, :], banks(r, 4)[:, j * SKV:(j + 1) * SKV], ACT.Exp, bias=nm[:, j:j + 1],
                                          scale=scale, accum_out=total[:, j:j + 1])
                last.then_inc(e_ready, 1)
                act.wait_ge(pt_done, b + 1)
                act.activation(pt[:], banks(r, 5)[0:SKV, :], ACT.Copy).then_inc(pt_ready, 1)
                act.wait_ge(z_ready, b + 1)
                act.activation(zh[:], z32[:], ACT.Copy).then_inc(zh_ready, 1)

        @block.vector
        def _(ve):
            ve.wait_ge(ctxh_ready, 1)
            ve.tensor_tensor(ctxl[:], ctx32[:], ctxh[:], ALU.subtract).then_inc(ctxl_ready, 1)
            ve.wait_ge(kh_ready, 1)
            ve.tensor_tensor(kl[:], k32[:], kh[:], ALU.subtract).then_inc(kl_ready, 1)
            ve.wait_ge(vps_done, 1)
            for s in range(B):
                last = ve.scalar_tensor_tensor(out=v_all[:, s * D:(s + 1) * D], in0=banks(r, 4, 4)[0:SKV, s * D:(s + 1) * D], scalar=1.0 / WS,
                                               in1=bv_row[:], op0=ALU.mult, op1=ALU.add)
            last.then_inc(v_ready, 1)
            ve.wait_ge(v_ready, 1)
            with ve.Fori(0, nb) as b:
                steps = Count(3)
                norm.vector(ve, r, b)
                ve.wait_ge(xh_ready, 2 * (b + 1))
                ve.tensor_tensor(flat(xl), flat(x32), flat(xh), ALU.subtract).then_inc(xl_ready, 1)
                ve.tensor_scalar(vcur[:], v_all[:, bass.ds(b * D, D)], 1.0, None, ALU.mult).then_inc(vcur_ready, 1)
                ve.wait_ge(s_done, b + 1)
                ve.reduce_max(mx[:], banks(r, 4)[:, 0:NJ * SKV].rearrange("p (j s) -> p j s", s=SKV), AX.X).then_inc(step, 1)
                steps.up()
                ve.wait_ge(step, steps.at(b))
                ve.tensor_scalar(nm[:], mx[:], -scale, None, ALU.mult).then_inc(nm_ready, 1)
                ve.wait_ge(e_ready, b + 1)
                ve.reciprocal(rec[:], total[:]).then_inc(step, 1)
                steps.up()
                ve.wait_ge(step, steps.at(b))
                ve.tensor_tensor(pr[:], e[:], rec[:].unsqueeze(2).broadcast_to([P, NJ, SKV]), ALU.mult).then_inc(p_ready, 1)
                ve.wait_ge(att_done, b + 1)
                ve.tensor_tensor(flat(z32), banks(r, 6, 2), flat(x32), ALU.add).then_inc(z_ready, 1)
                ve.wait_ge(out_done, b + 1)
                x = r.X[:, bass.ds(b * BT, BT)]
                ve.scalar_tensor_tensor(out=x, in0=banks(r, 2, 2), scalar=1.0 / WS, in1=x, op0=ALU.mult, op1=ALU.add).then_inc(step, 1)
                steps.up()
                ve.wait_ge(step, steps.at(b))
                xj = x.rearrange("p (j n) -> p j n", n=D)
                ve.tensor_tensor(xj, xj, bias_out[:].unsqueeze(1).broadcast_to([P, NJ, D]), ALU.add)
                steps.done()

        @block.tensor
        def _(pe):
            pe.wait_ge(ctxh_ready, 1)
            pe.wait_ge(ctxl_ready, 1)
            for m in range(NC):
                last = product(nc, banks(r, 2 + m), [(w, part[:, c, :]) for w, c, part in three("k", m * P, (m + 1) * P, ctxh, ctxl)])
            last.then_inc(kps_done, 1)
            for s in range(B):
                last = product(nc, banks(r, 4, 4)[0:SKV, s * D:(s + 1) * D],
                               [(part[:, c, s * SKV:(s + 1) * SKV], w) for w, c, part in three("v", 0, D, ctxh, ctxl)])
            last.then_inc(vps_done, 1)
            pe.wait_ge(kl_ready, 1)
            pe.wait_ge(v_ready, 1)
            with pe.Fori(0, nb) as b:
                pe.wait_ge(norm.xn_ready, b + 1)
                transpose_tiles(nc, r, norm.xn, 0).then_inc(xt_done, 1)
                pe.wait_ge(xl_ready, b + 1)
                for m in range(NC):
                    last = product(nc, banks(r, 2 + m), [(w, part[:, c, :]) for w, c, part in three("q", m * P, (m + 1) * P, xh, xl)])
                last.then_inc(q_done, 1)
                pe.wait_ge(ql_ready, b + 1)
                for j in range(NJ):
                    t = slice(j * P, (j + 1) * P)
                    last = product(nc, banks(r, 4)[:, j * SKV:(j + 1) * SKV],
                                   [(a[:, c, t], k[:, c, bass.ds(b * SKV, SKV)]) for c in range(NC) for a, k in ((qh, kh), (qh, kl), (ql, kh))])
                last.then_inc(s_done, 1)
                pe.wait_ge(p_ready, b + 1)
                nc.tensor.matmul(banks(r, 5)[:, 0:1], r.ident[:], r.ones[:, 0:1], start=True, stop=True)
                for j in range(NJ):
                    last = nc.tensor.transpose(banks(r, 5)[0:SKV, j * P:(j + 1) * P], pr[:, j, :], r.ident[:])
                last.then_inc(pt_done, 1)
                pe.wait_ge(pt_ready, b + 1)
                pe.wait_ge(vcur_ready, b + 1)
                for m in range(NC):
                    last = nc.tensor.matmul(banks(r, 6 + m), vcur[:, m * P:(m + 1) * P], pt[:], start=True, stop=True)
                last.then_inc(att_done, 1)
                pe.wait_ge(zl_ready, b + 1)
                for j in range(NJ):
                    last = product(nc, banks(r, 2, 2)[:, j * D:(j + 1) * D],
                                   [(part[:, c, j * P:(j + 1) * P], w) for w, c, part in three("o", 0, D, zh, zl)])
                last.then_inc(out_done, 1)


def quant_ffn_phase(nc, r, d, nb=B):
    tag = "ff"
    FI = 1024
    NI = FI // P
    with ExitStack() as es:
        sb = lambda n, s, t=F32: es.enter_context(nc.sbuf_tensor(f"{tag}_{n}", s, t))
        sem = lambda n: new_semaphore(nc, r, (f"{tag}_{n}"))
        norm = Norm(nc, es, tag, r)
        NW = NC * FI
        stage = sb("stage", [P, 3, NW])
        tmp = sb("tmp", [P, NW])
        wq = sb("wq", [P, 3, NW], BF16)
        rowsum, wmean, wrec = sb("rowsum", [P, 3]), sb("wmean", [P, 3]), sb("wrec", [P, 3])
        magic = sb("magic", [P, 1])
        amax, arec, ascale, aq = sb("amax", [P, NJ]), sb("arec", [P, NJ]), sb("ascale", [P, NJ]), sb("aq", [P, 2, NJ])
        xr, xq, xqt = sb("xr", [P, NJ, D]), sb("xq", [P, NJ, D], BF16), sb("xqt", [P, NC, T], BF16)
        sg, h, hr, hq, ht = sb("sg", [P, 2, FI]), sb("h", [P, 2, FI]), sb("hr", [P, 2, FI]), sb("hq", [P, 2, FI], BF16), sb("ht", [P, 2, NI, P], BF16)
        hmax, hrec, hscale, hdq = sb("hmax", [P, NJ]), sb("hrec", [P, NJ]), sb("hscale", [P, NJ]), sb("hdq", [P, NJ])
        (w_in, magic_in, abs_ready, tot_done, mean_ready, step, wq_ready, xq_ready, xt_done, xqt_ready) = (
            sem(n) for n in ("w_in", "magic_in", "abs_ready", "tot_done", "mean_ready", "step", "wq_ready", "xq_ready", "xt_done", "xqt_ready"))
        (gate_done, up_done, sg_ready, h_ready, hscale_ready, hr_ready, hq_ready, htps_done, ht_ready, out_done, out_read) = (
            sem(n) for n in ("gate_done", "up_done", "sg_ready", "h_ready", "hscale_ready", "hr_ready", "hq_ready", "htps_done", "ht_ready", "out_done", "out_read"))
        GATE, UP, DOWN, HT = 1, 3, 5, 7
        block = es.enter_context(nc.Block())

        @block.sync
        def _(sp):
            for n, w in enumerate(("f_gate", "f_up", "f_down")):
                k = NI if n == 2 else NC
                sp.dma_start(stage[:, n, :].rearrange("p (c n) -> p c n", c=k), d[w].rearrange("(c p) n -> p c n", p=P)).then_inc(w_in, 16)

        @block.gpsimd
        def _(pool):
            pool.memset(magic[:], MAGIC).then_inc(magic_in, 1)
            norm.pool_start(pool)
            with pool.Fori(0, nb) as b:
                norm.pool(pool, b)
                for j in range(NJ):
                    pool.wait_ge(hr_ready, b * NJ + j + 1)
                    pool.tensor_tensor(hq[:, j % 2, :], hr[:, j % 2, :], magic[:].broadcast_to([P, FI]), ALU.subtract).then_inc(hq_ready, 1)

        @block.scalar
        def _(act):
            act.wait_ge(w_in, 48)
            for n in range(3):
                last = act.activation(h[:].rearrange("p a b -> p (a b)"), stage[:, n, :], ACT.Abs, accum_out=rowsum[:, n:n + 1])
                last.then_inc(abs_ready, 1)
                act.wait_ge(abs_ready, n + 1)
            act.wait_ge(magic_in, 1)
            with act.Fori(0, nb) as b:
                act.wait_ge(xt_done, b + 1)
                act.activation(xqt[:].rearrange("p c t -> p (c t)"), banks(r, 0).bitcast(BF16), ACT.Copy).then_inc(xqt_ready, 1)

                def squash(j):
                    act.wait_ge(gate_done, b * NJ + j + 1)
                    act.activation(sg[:, j % 2, :], banks(r, GATE, 2), ACT.Silu, scale=aq[:, 0, j:j + 1]).then_inc(sg_ready, 1)

                squash(0)
                for j in range(NJ):
                    if j + 1 < NJ:
                        squash(j + 1)
                    act.wait_ge(hscale_ready, b * NJ + j + 1)
                    act.activation(hr[:, j % 2, :], h[:, j % 2, :], ACT.Identity, bias=magic[:], scale=hscale[:, j:j + 1]).then_inc(hr_ready, 1)
                    act.wait_ge(htps_done, b * NJ + j + 1)
                    act.activation(ht[:, j % 2].rearrange("p i t -> p (i t)"), banks(r, HT).bitcast(BF16), ACT.Copy).then_inc(ht_ready, 1)

        @block.vector
        def _(ve):
            ve.wait_ge(tot_done, 1)
            ve.tensor_scalar(wmean[:], banks(r, 0)[:, 0:3], 1.0 / (D * FI), 1e-5, ALU.mult, ALU.max).then_inc(mean_ready, 1)
            ve.wait_ge(mean_ready, 1)
            ve.reciprocal(wrec[:], wmean[:]).then_inc(mean_ready, 1)
            for n in range(3):
                ve.wait_ge(mean_ready, 2 + 3 * n)
                ve.tensor_scalar(tmp[:], stage[:, n, :], wrec[:, n:n + 1], MAGIC, ALU.mult, ALU.add).then_inc(mean_ready, 1)
                ve.wait_ge(mean_ready, 3 + 3 * n)
                ve.tensor_scalar(stage[:, n, :], tmp[:], MAGIC, -1.0, ALU.subtract, ALU.max).then_inc(mean_ready, 1)
                ve.wait_ge(mean_ready, 4 + 3 * n)
                ve.tensor_scalar(wq[:, n, :], stage[:, n, :], 1.0, None, ALU.min).then_inc(mean_ready, 1)
            ve.wait_ge(mean_ready, 11)
            with ve.Fori(0, nb) as b:
                steps = Count(3 + 2 + 1 + 3 * NJ)
                norm.vector(ve, r, b)
                ve.wait_ge(norm.xn_ready, b + 1)
                ve.tensor_reduce(amax[:], norm.xn[:], AX.X, ALU.max, apply_absolute_value=True).then_inc(step, 1)
                steps.up()
                ve.wait_ge(step, steps.at(b))
                ve.tensor_scalar(amax[:], amax[:], 1e-5, None, ALU.max).then_inc(step, 1)
                steps.up()
                ve.wait_ge(step, steps.at(b))
                ve.reciprocal(arec[:], amax[:]).then_inc(step, 1)
                steps.up()
                for n in range(2):
                    ve.tensor_scalar(aq[:, n, :], amax[:], 1.0 / 127.0, wmean[:, n:n + 1], ALU.mult, ALU.mult).then_inc(step, 1)
                    steps.up()
                ve.wait_ge(step, steps.at(b))
                ve.tensor_scalar(ascale[:], arec[:], 127.0, None, ALU.mult).then_inc(step, 1)
                steps.up()
                ve.wait_ge(step, steps.at(b))
                for j in range(NJ):
                    ve.tensor_scalar(xr[:, j, :], norm.xn[:, j, :], ascale[:, j:j + 1], MAGIC, ALU.mult, ALU.add).then_inc(xq_ready, 1)
                ve.wait_ge(xq_ready, b * 5 + 4)
                ve.tensor_scalar(xq[:], xr[:], MAGIC, None, ALU.subtract).then_inc(xq_ready, 1)

                def update(j):
                    ve.wait_ge(out_done, b * NJ + j + 1)
                    x = r.X[:, bass.ds(b * BT + j * D, D)]
                    ve.scalar_tensor_tensor(out=x, in0=banks(r, DOWN + j % 2)[:, 0:D], scalar=hdq[:, j:j + 1], in1=x,
                                            op0=ALU.mult, op1=ALU.add).then_inc(out_read, 1)
                for j in range(NJ):
                    ve.wait_ge(up_done, b * NJ + j + 1)
                    ve.wait_ge(sg_ready, b * NJ + j + 1)
                    ve.scalar_tensor_tensor(out=h[:, j % 2, :], in0=banks(r, UP, 2), scalar=aq[:, 1, j:j + 1], in1=sg[:, j % 2, :],
                                            op0=ALU.mult, op1=ALU.mult).then_inc(h_ready, 1)
                    ve.wait_ge(h_ready, b * NJ + j + 1)
                    ve.tensor_reduce(hmax[:, j:j + 1], h[:, j % 2, :], AX.X, ALU.max, apply_absolute_value=True).then_inc(step, 1)
                    steps.up()
                    ve.wait_ge(step, steps.at(b))
                    ve.tensor_scalar(hmax[:, j:j + 1], hmax[:, j:j + 1], 1e-5, None, ALU.max).then_inc(step, 1)
                    steps.up()
                    ve.wait_ge(step, steps.at(b))
                    ve.reciprocal(hrec[:, j:j + 1], hmax[:, j:j + 1]).then_inc(step, 1)
                    steps.up()
                    ve.wait_ge(step, steps.at(b))
                    ve.tensor_scalar(hdq[:, j:j + 1], hmax[:, j:j + 1], 1.0 / 127.0, wmean[:, 2:3], ALU.mult, ALU.mult)
                    ve.tensor_scalar(hscale[:, j:j + 1], hrec[:, j:j + 1], 127.0, None, ALU.mult).then_inc(hscale_ready, 1)
                    if j:
                        update(j - 1)
                update(NJ - 1)
                steps.done()

        @block.tensor
        def _(pe):
            pe.wait_ge(abs_ready, 3)
            nc.tensor.matmul(banks(r, 0)[:, 0:3], r.ones[:], rowsum[:], start=True, stop=True).then_inc(tot_done, 1)
            pe.wait_ge(mean_ready, 11)
            gate_w, up_w = (wq[:, n, :].rearrange("p (c n) -> p c n", c=NC) for n in range(2))
            down_w = wq[:, 2, :].rearrange("p (c n) -> p c n", c=NI)
            with pe.Fori(0, nb) as b:
                pe.wait_ge(xq_ready, 5 * (b + 1))
                for c in range(NC):
                    for j in range(NJ):
                        last = nc.tensor.transpose(banks(r, 0).bitcast(BF16)[:, c * T + j * P:c * T + (j + 1) * P],
                                                   xq[:, j, c * P:(c + 1) * P], r.identb[:])
                last.then_inc(xt_done, 1)
                pe.wait_ge(xqt_ready, b + 1)

                def inner(j):
                    if j:
                        pe.wait_ge(sg_ready, b * NJ + j)
                    for w, bank, done in ((gate_w, GATE, gate_done), (up_w, UP, up_done)):
                        if w is up_w and j:
                            pe.wait_ge(h_ready, b * NJ + j)
                        for half in range(FI // BANK):
                            last = product(nc, banks(r, bank + half), [(xqt[:, c, j * P:(j + 1) * P], w[:, c, half * BANK:(half + 1) * BANK]) for c in range(NC)])
                        last.then_inc(done, 1)
                inner(0)
                for j in range(NJ):
                    if j + 1 < NJ:
                        inner(j + 1)
                    pe.wait_ge(hq_ready, b * NJ + j + 1)
                    if j:
                        pe.wait_ge(ht_ready, b * NJ + j)
                    for i in range(NI):
                        last = nc.tensor.transpose(banks(r, HT).bitcast(BF16)[:, i * P:(i + 1) * P], hq[:, j % 2, i * P:(i + 1) * P], r.identb[:])
                    last.then_inc(htps_done, 1)
                    pe.wait_ge(ht_ready, b * NJ + j + 1)
                    if j >= 2:
                        pe.wait_ge(out_read, b * NJ + j - 1)
                    product(nc, banks(r, DOWN + j % 2)[:, 0:D], [(ht[:, j % 2, i, :], down_w[:, i, :]) for i in range(NI)]).then_inc(out_done, 1)


def cross1_phase(nc, r, d, nb=B):
    tag = "x1"
    with ExitStack() as es:
        sb = lambda n, s, t=F32: es.enter_context(nc.sbuf_tensor(f"{tag}_{n}", s, t))
        sem = lambda n: new_semaphore(nc, r, (f"{tag}_{n}"))
        norm = Norm(nc, es, tag, r)
        ctx32, ctxh, ctxl = sb("ctx32", [P, NC, B * SKV]), sb("ctxh", [P, NC, B * SKV], F16), sb("ctxl", [P, NC, B * SKV], F16)
        k32, kh, kl = sb("k32", [P, NC, B * SKV]), sb("kh", [P, NC, B * SKV], F16), sb("kl", [P, NC, B * SKV], F16)
        kst, vblk = sb("kst", [P, B, NP_, P], F16), sb("vblk", [P, B, NP_, 64])
        kcur, vcur = sb("kcur", [P, NP_, P], F16), sb("vcur", [P, NP_, 64])
        xh, xl = sb("xh", [P, NC, T], F16), sb("xl", [P, NC, T], F16)
        q32, qh, ql = sb("q32", [P, NC, T]), sb("qh", [P, NC, T], F16), sb("ql", [P, NC, T], F16)
        qs = sb("qs", [P, NP_, T], F16)
        nrow, krow = sb("nrow", [2, NP_, T], F16), sb("krow", [2, T], F16)
        mx, mh, ml = sb("mx", [P, NJ, H]), sb("mh", [H, T], F16), sb("ml", [H, T], F16)
        pexp, ot, rec = sb("pexp", [P, NP_, T]), sb("ot", [P, 4, T]), sb("rec", [P, NJ, H])
        y, yh, yl = norm.xn, xh, xl
        bq, bk = sb("bq", [P, NC, 1]), sb("bk", [P, NC, 1])
        bv_row, bias_out = sb("bv_row", [P, D]), sb("bias_out", [P, D])
        kscratch = nc.dram_tensor(f"{tag}_kscratch", (2, P, NC, B * SKV), F16, kind="Internal").ap()
        qscratch = nc.dram_tensor(f"{tag}_qscratch", (2, P, NC, T), F16, kind="Internal").ap()
        (w_in, consts, ctxh_ready, ctxl_ready, kps_done, kh_ready, kl_ready, vps_done, v_ready, ones_in, ksaved, kstacked) = (
            sem(n) for n in ("w_in", "consts", "ctxh_ready", "ctxl_ready", "kps_done", "kh_ready", "kl_ready", "vps_done", "v_ready", "ones_in", "ksaved", "kstacked"))
        (zeroed, xt_done, xh_ready, xl_ready, q_done, q_ready, ql_ready, saved, stacked, cur_ready, mxs_ready, mx_read, mt_done) = (
            sem(n) for n in ("zeroed", "xt_done", "xh_ready", "xl_ready", "q_done", "q_ready", "ql_ready", "saved", "stacked", "cur_ready", "mxs_ready", "mx_read", "mt_done"))
        (mh_ready, ml_ready, rows_in, st_ready, exp_done, av_done, ot_ready, ott_done, y_ready, yt_done, yh_ready, yl_ready, out_done, step) = (
            sem(n) for n in ("mh_ready", "ml_ready", "rows_in", "st_ready", "exp_done", "av_done", "ot_ready", "ott_done", "y_ready", "yt_done", "yh_ready", "yl_ready", "out_done", "step"))
        flat = lambda t: t[:].rearrange("p c t -> p (c t)")
        MAXB, MAINB = (0, 6), (2, 4)
        NKD = NP_ * 6 + 2 * NP_
        block = es.enter_context(nc.Block())

        def three(name, m0, m1, hi, lo):
            at = COL[f"x1{name}"]
            return [(w[:, c, at + m0:at + m1], c, part) for c in range(NC) for w, part in ((r.wh, hi), (r.wh, lo), (r.wl, hi))]

        @block.sync
        def _(sp):
            def const(dst, src):
                sp.dma_start(dst, src, allow_slow_non_contiguous=True).then_inc(w_in, 16)
            const(ctx32[:], d["ctxT"].rearrange("(c p) n -> p c n", p=P))
            const(bq[:], d["x1_bq"].rearrange("(c p) -> p c", p=P).unsqueeze(2))
            const(bk[:], d["x1_bk"].rearrange("(c p) -> p c", p=P).unsqueeze(2))
            const(bv_row[:], d["x1_bv"].partition_broadcast(P))
            const(bias_out[:], d["x1_bo"].partition_broadcast(P))
            sp.wait_ge(kl_ready, 1)
            sp.dma_start(kscratch[0], kh[:]).then_inc(ksaved, 16)
            sp.dma_start(kscratch[1], kl[:]).then_inc(ksaved, 16)
            sp.wait_ge(consts, 2)
            sp.wait_ge(zeroed, 3)
            sp.wait_ge(ksaved, 32)
            for par in range(2):
                own = slice(par * SKV, (par + 1) * SKV)
                for i in range(NP_):
                    for rep, part in enumerate((0, 1, 0)):
                        at = 64 * par + 16 * rep
                        sp.dma_start(kst[at:at + 16, :, i, own], kscratch[part][i * DH:(i + 1) * DH, par, :].rearrange("d (b s) -> d b s", b=B)).then_inc(kstacked, 16)
                    sp.dma_start(kst[64 * par + 48:64 * par + 50, :, i, own], krow[:].rearrange("p (b s) -> p b s", b=B)).then_inc(kstacked, 16)
            with sp.Fori(0, nb) as b:
                sp.wait_ge(q_ready, b + 1)
                sp.dma_start(qscratch[0], qh[:]).then_inc(saved, 16)
                sp.wait_ge(ql_ready, b + 1)
                sp.dma_start(qscratch[1], ql[:]).then_inc(saved, 16)
                sp.wait_ge(saved, (b + 1) * 32)
                for par in range(2):
                    for rep, part in enumerate((0, 0, 1)):
                        at = 64 * par + 16 * rep
                        sp.dma_start(qs[at:at + 16, :, :], qscratch[part][:, par, :].rearrange("(i d) t -> d i t", d=DH)).then_inc(stacked, 16)
                    sp.dma_start(qs[64 * par + 48:64 * par + 50, :, :], nrow[:]).then_inc(stacked, 16)
                sp.wait_ge(stacked, 16 * 8 * (b + 1))
                sp.wait_ge(ml_ready, b + 1)
                for par in range(2):
                    for row, m in ((48, mh), (49, ml)):
                        sp.dma_start(qs[64 * par + row:64 * par + row + 1, :, :], m[par * NP_:(par + 1) * NP_, :]).then_inc(rows_in, 16)
            sp.wait_ge(rows_in, 16 * 4 * nb)

        @block.gpsimd
        def _(pool):
            pool.memset(krow[:], MS).then_inc(consts, 1)
            pool.memset(nrow[:], 0.0).then_inc(consts, 1)
            norm.pool_start(pool)
            with pool.Fori(0, nb) as b:
                norm.pool(pool, b)
                pool.wait_ge(q_ready, b + 1)
                pool.tensor_tensor(ql[:], q32[:], qh[:], ALU.subtract).then_inc(ql_ready, 1)

        @block.scalar
        def _(act):
            act.wait_ge(w_in, 16 * 5)
            act.activation(ctxh[:], ctx32[:], ACT.Copy).then_inc(ctxh_ready, 1)
            act.wait_ge(kps_done, 1)
            for m in range(NC):
                act.activation(k32[:, m, :], banks(r, 2 + m), ACT.Identity, bias=bk[:, m, :], scale=1.0 / WS)
                last = act.activation(kh[:, m, :], banks(r, 2 + m), ACT.Identity, bias=bk[:, m, :], scale=1.0 / WS)
            last.then_inc(kh_ready, 1)
            with act.Fori(0, nb) as b:
                act.wait_ge(xt_done, b + 1)
                act.activation(flat(xh), banks(r, 0, 2), ACT.Copy).then_inc(xh_ready, 1)
                act.wait_ge(q_done, b + 1)
                for m in range(NC):
                    act.activation(q32[:, m, :], banks(r, 2 + m), ACT.Identity, bias=bq[:, m, :], scale=1.0 / WS)
                    last = act.activation(qh[:, m, :], banks(r, 2 + m), ACT.Identity, bias=bq[:, m, :], scale=1.0 / WS)
                last.then_inc(q_ready, 1)
                act.wait_ge(mt_done, b + 1)
                act.activation(mh[:], banks(r, 0)[0:H, :], ACT.Copy, scale=-1.0 / MS).then_inc(mh_ready, 1)
                for k in range(4):
                    act.wait_ge(st_ready, b * 4 + k + 1)
                    act.activation(pexp[:, 2 * k:2 * k + 2, :].rearrange("p i t -> p (i t)"), banks(r, MAINB[k % 2], 2), ACT.Exp, scale=DH ** -0.5).then_inc(exp_done, 1)
                act.wait_ge(yt_done, b + 1)
                act.activation(flat(yh), banks(r, 2, 2), ACT.Copy).then_inc(yh_ready, 1)

        @block.vector
        def _(ve):
            ve.memset(kst[:], 0.0).then_inc(zeroed, 1)
            ve.memset(vblk[:], 0.0).then_inc(zeroed, 1)
            ve.memset(qs[:], 0.0).then_inc(zeroed, 1)
            ve.wait_ge(zeroed, 3)
            ve.memset(vblk[0:SKV, :, :, DH:DH + 1], 1.0)
            ve.memset(vblk[SKV:P, :, :, 32 + DH:32 + DH + 1], 1.0).then_inc(ones_in, 1)
            ve.wait_ge(ctxh_ready, 1)
            ve.tensor_tensor(ctxl[:], ctx32[:], ctxh[:], ALU.subtract).then_inc(ctxl_ready, 1)
            ve.wait_ge(kh_ready, 1)
            ve.tensor_tensor(kl[:], k32[:], kh[:], ALU.subtract).then_inc(kl_ready, 1)
            ve.wait_ge(vps_done, 1)
            for s in range(B):
                for par in range(2):
                    rows = slice(par * SKV, (par + 1) * SKV)
                    last = ve.scalar_tensor_tensor(out=vblk[rows, s, :, 32 * par:32 * par + DH],
                                                   in0=banks(r, 4, 2)[rows, s * P:(s + 1) * P].rearrange("p (i e) -> p i e", e=DH), scalar=1.0 / WS,
                                                   in1=bv_row[rows, par * P:(par + 1) * P].rearrange("p (i e) -> p i e", e=DH), op0=ALU.mult, op1=ALU.add)
            last.then_inc(v_ready, 1)
            ve.wait_ge(v_ready, 1)
            ve.wait_ge(ones_in, 1)
            ve.wait_ge(kstacked, 16 * NKD)
            with ve.Fori(0, nb) as b:
                steps = Count(NJ + 1)
                norm.vector(ve, r, b)
                ve.wait_ge(xh_ready, b + 1)
                ve.tensor_tensor(flat(xl), banks(r, 0, 2), flat(xh), ALU.subtract).then_inc(xl_ready, 1)
                ve.tensor_scalar(kcur[:], kst[:, bass.ds(b, 1)].rearrange("p o i s -> p (o i) s"), 1.0, None, ALU.mult)
                ve.tensor_scalar(vcur[:], vblk[:, bass.ds(b, 1)].rearrange("p o i s -> p (o i) s"), 1.0, None, ALU.mult).then_inc(cur_ready, 1)
                for j in range(NJ):
                    ve.wait_ge(mxs_ready, b * NJ + j + 1)
                    ve.reduce_max(mx[:, j, :].rearrange("p (par i) -> p i par", par=2), banks(r, MAXB[j % 2], 2).rearrange("p (i par s) -> p i par s", par=2, s=SKV), AX.X).then_inc(mx_read, 1)
                ve.wait_ge(mh_ready, b + 1)
                ve.scalar_tensor_tensor(out=ml[:], in0=banks(r, 0)[0:H, :], scalar=-1.0 / MS, in1=mh[:], op0=ALU.mult, op1=ALU.subtract).then_inc(ml_ready, 1)
                for g in range(4):
                    ve.wait_ge(av_done, b * 4 + g + 1)
                    ve.tensor_copy(ot[:, g, :], banks(r, 6 + g % 2)).then_inc(ot_ready, 1)
                for j in range(NJ):
                    ve.wait_ge(ott_done, b * NJ + j + 1)
                    o = banks(r, j % 2).rearrange("p (i par e) -> p i par e", par=2, e=32)
                    ve.reciprocal(rec[:, j, :], banks(r, j % 2).rearrange("p (h e) -> p h e", e=32)[:, :, DH]).then_inc(step, 1)
                    steps.up()
                    ve.wait_ge(step, steps.at(b))
                    ve.tensor_tensor(y[:, j, :].rearrange("p (par i e) -> p i par e", par=2, e=DH), o[:, :, :, 0:DH],
                                     rec[:, j, :].rearrange("p (i par) -> p i par", par=2).unsqueeze(3).broadcast_to([P, NP_, 2, DH]), ALU.mult).then_inc(y_ready, 1)
                ve.wait_ge(yh_ready, b + 1)
                ve.tensor_tensor(flat(yl), banks(r, 2, 2), flat(yh), ALU.subtract).then_inc(yl_ready, 1)
                ve.wait_ge(out_done, b + 1)
                x = r.X[:, bass.ds(b * BT, BT)]
                ve.scalar_tensor_tensor(out=x, in0=banks(r, 4, 2), scalar=1.0 / WS, in1=x, op0=ALU.mult, op1=ALU.add).then_inc(step, 1)
                steps.up()
                ve.wait_ge(step, steps.at(b))
                xj = x.rearrange("p (j n) -> p j n", n=D)
                ve.tensor_tensor(xj, xj, bias_out[:].unsqueeze(1).broadcast_to([P, NJ, D]), ALU.add)
                steps.done()

        @block.tensor
        def _(pe):
            pe.wait_ge(ctxh_ready, 1)
            pe.wait_ge(ctxl_ready, 1)
            for m in range(NC):
                last = product(nc, banks(r, 2 + m), [(w, part[:, c, :]) for w, c, part in three("k", m * P, (m + 1) * P, ctxh, ctxl)])
            last.then_inc(kps_done, 1)
            for s in range(B):
                for par in range(2):
                    last = product(nc, banks(r, 4, 2)[par * SKV:(par + 1) * SKV, s * P:(s + 1) * P],
                                   [(part[:, c, s * SKV:(s + 1) * SKV], w) for w, c, part in three("v", par * P, (par + 1) * P, ctxh, ctxl)])
            last.then_inc(vps_done, 1)
            pe.wait_ge(kh_ready, 1)
            pe.wait_ge(v_ready, 1)
            with pe.Fori(0, nb) as b:
                pe.wait_ge(norm.xn_ready, b + 1)
                transpose_tiles(nc, r, norm.xn, 0).then_inc(xt_done, 1)
                pe.wait_ge(xl_ready, b + 1)
                for m in range(NC):
                    last = product(nc, banks(r, 2 + m), [(w, part[:, c, :]) for w, c, part in three("q", m * P, (m + 1) * P, xh, xl)])
                last.then_inc(q_done, 1)
                pe.wait_ge(stacked, 16 * 8 * (b + 1))
                pe.wait_ge(cur_ready, b + 1)
                for j in range(NJ):
                    if j >= 2:
                        pe.wait_ge(mx_read, b * NJ + j - 1)
                    for i in range(NP_):
                        last = nc.tensor.matmul(banks(r, MAXB[j % 2], 2)[:, i * P:(i + 1) * P], qs[:, i, j * P:(j + 1) * P], kcur[:, i, :], start=True, stop=True)
                    last.then_inc(mxs_ready, 1)
                pe.wait_ge(mx_read, (b + 1) * NJ)
                for j in range(NJ):
                    last = nc.tensor.transpose(banks(r, 0)[0:H, j * P:(j + 1) * P], mx[:, j, :], r.ident[:])
                last.then_inc(mt_done, 1)
                pe.wait_ge(rows_in, 64 * (b + 1))

                def values(g):
                    pe.wait_ge(exp_done, b * 4 + g + 1)
                    if g >= 2:
                        pe.wait_ge(ot_ready, b * 4 + g - 1)
                    for i in (2 * g, 2 * g + 1):
                        last = nc.tensor.matmul(banks(r, 6 + g % 2)[64 * (i % 2):64 * (i % 2) + 64, :], vcur[:, i, :], pexp[:, i, :], start=True, stop=True)
                    last.then_inc(av_done, 1)

                for k in range(4):
                    if k >= 2:
                        pe.wait_ge(exp_done, b * 4 + k - 1)
                    for i in range(2):
                        last = nc.tensor.matmul(banks(r, MAINB[k % 2] + i), kcur[:, 2 * k + i, :], qs[:, 2 * k + i, :], start=True, stop=True)
                    last.then_inc(st_ready, 1)
                    if k:
                        values(k - 1)
                values(3)
                pe.wait_ge(ot_ready, 4 * (b + 1))
                for j in range(NJ):
                    if j >= 2:
                        pe.wait_ge(y_ready, b * NJ + j - 1)
                    for g in range(4):
                        last = nc.tensor.transpose(banks(r, j % 2)[:, g * P:(g + 1) * P], ot[:, g, j * P:(j + 1) * P], r.ident[:])
                    last.then_inc(ott_done, 1)
                pe.wait_ge(y_ready, NJ * (b + 1))
                transpose_tiles(nc, r, y, 2).then_inc(yt_done, 1)
                pe.wait_ge(yl_ready, b + 1)
                for j in range(NJ):
                    last = product(nc, banks(r, 4, 2)[:, j * D:(j + 1) * D], [(part[:, c, j * P:(j + 1) * P], w) for w, c, part in three("o", 0, D, yh, yl)])
                last.then_inc(out_done, 1)


def experts_phase(nc, r, d, nb=B):
    E, FI = 8, 512
    NI = FI // P
    NE = E + 1
    NW = NC * FI
    with ExitStack() as es0:
        wts = es0.enter_context(nc.sbuf_tensor("mo_wts", [P, B * NJ * NE], F32))
        xth = es0.enter_context(nc.sbuf_tensor("mo_xth", [P, NC, B * T], F16))
        xtl = es0.enter_context(nc.sbuf_tensor("mo_xtl", [P, NC, B * T], F16))
        route(nc, r, d, nb, wts, xth, xtl, E)
        end_phase(nc, r)
        with ExitStack() as es:
            tag = "mo"
            sb = lambda n, s, t=F32: es.enter_context(nc.sbuf_tensor(f"{tag}_{n}", s, t))
            sem = lambda n: new_semaphore(nc, r, (f"{tag}_{n}"))
            stage = sb("stage", [P, 3, NW])
            wh, wl = sb("wh", [P, 3, NW], F16), sb("wl", [P, 3, NW], F16)
            sg, h = sb("sg", [P, 2, FI]), sb("h", [P, 2, NI, T])
            hh, hl = sb("hh", [P, 2, NI, T], F16), sb("hl", [P, 2, NI, T], F16)
            (w_in, wh_ready, wl_ready, gu_done, sg_ready, h_ready, hh_ready, hl_ready, down_done, down_read) = (
                sem(n) for n in ("w_in", "wh_ready", "wl_ready", "gu_done", "sg_ready", "h_ready", "hh_ready", "hl_ready", "down_done", "down_read"))
            GU = ((0, 1), (2, 3))
            DN = (4, 6)
            block = es.enter_context(nc.Block())
            pairs = nb // 2

            @block.sync
            def _(sp):
                with sp.Fori(0, NE) as e:
                    sp.wait_ge(wl_ready, e * 3 + 1)
                    for n, w in enumerate(("m_gate", "m_up", "m_down")):
                        k = NI if n == 2 else NC
                        sp.dma_start(stage[:, n, :].rearrange("p (c n) -> p c n", c=k),
                                     d[w][bass.ds(e, 1)].rearrange("e (c p) n -> p (e c) n", p=P)).then_inc(w_in, 16)

            @block.scalar
            def _(act):
                with act.Fori(0, NE) as e:
                    act.wait_ge(w_in, 48 * (e + 1))
                    act.wait_ge(down_done, nb * e + 1)
                    for n in range(3):
                        act.activation(wh[:, n, :], stage[:, n, :], ACT.Copy, scale=WS).then_inc(wh_ready, 1)

                    def squash(b, par):
                        for i in range(NI):
                            n = (e * nb + b) * NI + i
                            act.wait_ge(gu_done, n + 1)
                            act.activation(sg[:, i % 2, :], banks(r, GU[i % 2][0]), ACT.Silu, scale=1.0 / WS).then_inc(sg_ready, 1)
                            act.wait_ge(h_ready, n + 1)
                            act.activation(hh[:, par, i, :], h[:, par, i, :], ACT.Copy).then_inc(hh_ready, 1)
                    with act.Fori(0, pairs) as k:
                        squash(2 * k, 0)
                        squash(2 * k + 1, 1)

            @block.vector
            def _(ve):
                ve.memset(sg[:, 0, 0:1], 0.0).then_inc(wl_ready, 1)
                ve.memset(sg[:, 0, 1:2], 0.0).then_inc(hl_ready, 1)
                with ve.Fori(0, NE) as e:
                    for n in range(3):
                        ve.wait_ge(wh_ready, 3 * e + n + 1)
                        ve.scalar_tensor_tensor(out=wl[:, n, :], in0=stage[:, n, :], scalar=WS, in1=wh[:, n, :],
                                                op0=ALU.mult, op1=ALU.subtract).then_inc(wl_ready, 1)

                    def hidden(b, par):
                        for i in range(NI):
                            n = (e * nb + b) * NI + i
                            ve.wait_ge(sg_ready, n + 1)
                            ve.scalar_tensor_tensor(out=h[:, par, i, :], in0=banks(r, GU[i % 2][1]), scalar=1.0 / WS, in1=sg[:, i % 2, :],
                                                    op0=ALU.mult, op1=ALU.mult).then_inc(h_ready, 1)
                            ve.wait_ge(hh_ready, n + 1)
                            ve.tensor_tensor(hl[:, par, i, :], h[:, par, i, :], hh[:, par, i, :], ALU.subtract).then_inc(hl_ready, 1)

                    def update(b, par):
                        ve.wait_ge(down_done, e * nb + b + 2)
                        for j in range(NJ):
                            x = r.X[:, bass.ds(b * BT + j * D, D)]
                            last = ve.scalar_tensor_tensor(out=x, in0=banks(r, DN[par], 2)[:, j * D:(j + 1) * D],
                                                           scalar=wts[:, bass.ds(b * NJ * NE + j * NE + e, 1)], in1=x, op0=ALU.mult, op1=ALU.add)
                        last.then_inc(down_read, 1)

                    hidden(0, 0)
                    if pairs > 1:
                        with ve.Fori(0, pairs - 1) as k:
                            hidden(2 * k + 1, 1)
                            update(2 * k, 0)
                            hidden(2 * k + 2, 0)
                            update(2 * k + 1, 1)
                    hidden(nb - 1, 1)
                    update(nb - 2, 0)
                    update(nb - 1, 1)

            @block.tensor
            def _(pe):
                gate, up = (lambda w, n=n: w[:, n, :].rearrange("p (c n) -> p c n", c=NC) for n in range(2))
                down = lambda w: w[:, 2, :].rearrange("p (c n) -> p c n", c=NI)
                nc.tensor.matmul(banks(r, 0)[:, 0:1], r.ones[:], r.ones[:, 0:1], start=True, stop=True).then_inc(down_done, 1)
                with pe.Fori(0, NE) as e:
                    pe.wait_ge(wl_ready, 3 * (e + 1) + 1)

                    def gate_up(b):
                        for i in range(NI):
                            n = (e * nb + b) * NI + i
                            if i >= 2:
                                pe.wait_ge(h_ready, n - 1)
                            else:
                                pe.wait_ge(hl_ready, (e * nb + b) * NI + 1)
                            for w, bank in ((gate, GU[i % 2][0]), (up, GU[i % 2][1])):
                                m = slice(i * P, (i + 1) * P)
                                last = product(nc, banks(r, bank), [(w(a)[:, c, m], x[:, c, bass.ds(b * T, T)]) for c in range(NC)
                                                                    for a, x in ((wh, xth), (wh, xtl), (wl, xth))])
                            last.then_inc(gu_done, 1)

                    def project(b, par):
                        pe.wait_ge(hl_ready, (e * nb + b + 1) * NI + 1)
                        for j in range(NJ):
                            t = slice(j * P, (j + 1) * P)
                            last = product(nc, banks(r, DN[par], 2)[:, j * D:(j + 1) * D],
                                           [(x[:, par, i, t], down(a)[:, i, :]) for i in range(NI) for x, a in ((hh, wh), (hl, wh), (hh, wl))])
                        last.then_inc(down_done, 1)

                    gate_up(0)
                    if pairs > 1:
                        with pe.Fori(0, pairs - 1) as k:
                            gate_up(2 * k + 1)
                            project(2 * k, 0)
                            gate_up(2 * k + 2)
                            project(2 * k + 1, 1)
                    gate_up(nb - 1)
                    project(nb - 2, 0)
                    project(nb - 1, 1)


def route(nc, r, d, nb, wts, xth, xtl, E):
    tag = "ro"
    NE = E + 1
    with ExitStack() as es:
        sb = lambda n, s, t=F32: es.enter_context(nc.sbuf_tensor(f"{tag}_{n}", s, t))
        sem = lambda n: new_semaphore(nc, r, (f"{tag}_{n}"))
        norm = Norm(nc, es, tag, r)
        xh, xl = sb("xh", [P, NC, T], F16), sb("xl", [P, NC, T], F16)
        w32, rwh, rwl = sb("w32", [P, NC, E]), sb("rwh", [P, NC, E], F16), sb("rwl", [P, NC, E], F16)
        bias, iota = sb("bias", [P, E]), sb("iota", [P, E])
        lg, pr = sb("lg", [P, NJ, E]), sb("pr", [P, NJ, E])
        top, idx, idxf = sb("top", [P, NJ, E]), sb("idx", [P, NJ, E], U32), sb("idxf", [P, NJ, E])
        total, rec, share = sb("total", [P, NJ, 1]), sb("rec", [P, NJ, 1]), sb("share", [P, NJ, 2])
        pick, pad = sb("pick", [P, 2, NJ, E]), sb("hold", [P, 1])
        (w_in, iota_in, rwh_ready, rwl_ready, ones_in, xt_done, xh_ready, xl_ready, lg_done, lg_ready, pr_ready, kept, step) = (
            sem(n) for n in ("w_in", "iota_in", "rwh_ready", "rwl_ready", "ones_in", "xt_done", "xh_ready", "xl_ready", "lg_done", "lg_ready", "pr_ready", "kept", "step"))
        flat = lambda t: t[:].rearrange("p c t -> p (c t)")
        block = es.enter_context(nc.Block())

        @block.sync
        def _(sp):
            sp.dma_start(w32[:], d["m_router"].rearrange("(c p) n -> p c n", p=P)).then_inc(w_in, 16)
            sp.dma_start(bias[:], d["m_bias"].partition_broadcast(P)).then_inc(kept, 16)
            with sp.Fori(0, nb) as b:
                sp.wait_ge(xh_ready, b + 1)
                sp.wait_ge(xl_ready, b + 1)
                sp.dma_start(xth[:, :, bass.ds(b * T, T)], xh[:]).then_inc(kept, 16)
                sp.dma_start(xtl[:, :, bass.ds(b * T, T)], xl[:]).then_inc(kept, 16)
            sp.wait_ge(kept, 32 * nb + 16)

        @block.gpsimd
        def _(pool):
            for n in range(E):
                last = pool.memset(iota[:, n:n + 1], float(n))
            last.then_inc(iota_in, 1)
            norm.pool_start(pool)
            with pool.Fori(0, nb) as b:
                norm.pool(pool, b)

        @block.scalar
        def _(act):
            act.wait_ge(w_in, 16)
            act.activation(rwh[:], w32[:], ACT.Copy, scale=WS).then_inc(rwh_ready, 1)
            with act.Fori(0, nb) as b:
                act.wait_ge(xt_done, b + 1)
                act.wait_ge(kept, 32 * b + 16)
                act.activation(flat(xh), banks(r, 0, 2), ACT.Copy).then_inc(xh_ready, 1)
                act.wait_ge(lg_ready, b + 1)
                act.activation(pr[:], lg[:], ACT.Sigmoid).then_inc(pr_ready, 1)

        @block.vector
        def _(ve):
            ve.wait_ge(rwh_ready, 1)
            ve.scalar_tensor_tensor(out=rwl[:], in0=w32[:], scalar=WS, in1=rwh[:], op0=ALU.mult, op1=ALU.subtract).then_inc(rwl_ready, 1)
            ve.memset(wts[:], 1.0 / WS).then_inc(ones_in, 1)
            ve.wait_ge(kept, 16)
            ve.wait_ge(ones_in, 1)
            ve.wait_ge(iota_in, 1)
            with ve.Fori(0, nb) as b:
                steps = Count(2 * NJ + 4 + 2 * NJ)
                norm.vector(ve, r, b)
                ve.wait_ge(xh_ready, b + 1)
                ve.tensor_tensor(flat(xl), banks(r, 0, 2), flat(xh), ALU.subtract).then_inc(xl_ready, 1)
                ve.wait_ge(lg_done, b + 1)
                ve.scalar_tensor_tensor(out=lg[:], in0=banks(r, 2)[:, 0:NJ * E].rearrange("p (j e) -> p j e", e=E), scalar=1.0 / WS,
                                        in1=bias[:].unsqueeze(1).broadcast_to([P, NJ, E]), op0=ALU.mult, op1=ALU.add).then_inc(lg_ready, 1)
                ve.wait_ge(pr_ready, b + 1)
                ve.memset(pad[:], 0.0)
                for j in range(NJ):
                    ve.max(top[:, j, :], pr[:, j, :]).then_inc(step, 1)
                    steps.up()
                ve.wait_ge(step, steps.at(b))
                ve.tensor_tensor(total[:], top[:, :, 0:1], top[:, :, 1:2], ALU.add).then_inc(step, 1)
                for j in range(NJ):
                    ve.max_index(idx[:, j, :], top[:, j, :], pr[:, j, :]).then_inc(step, 1)
                    steps.up()
                steps.up()
                ve.wait_ge(step, steps.at(b))
                ve.tensor_copy(idxf[:], idx[:]).then_inc(step, 1)
                ve.reciprocal(rec[:], total[:]).then_inc(step, 1)
                steps.up()
                steps.up()
                ve.wait_ge(step, steps.at(b))
                ve.scalar_tensor_tensor(out=share[:], in0=top[:, :, 0:2], scalar=1.0 / WS, in1=rec[:].broadcast_to([P, NJ, 2]),
                                        op0=ALU.mult, op1=ALU.mult).then_inc(step, 1)
                steps.up()
                ve.wait_ge(step, steps.at(b))
                for j in range(NJ):
                    for k in range(2):
                        ve.tensor_scalar(pick[:, k, j, :], iota[:], idxf[:, j, k:k + 1], share[:, j, k:k + 1], ALU.is_equal, ALU.mult).then_inc(step, 1)
                        steps.up()
                ve.wait_ge(step, steps.at(b))
                ve.tensor_tensor(wts[:, bass.ds(b * NJ * NE, NJ * NE)].rearrange("p (j e) -> p j e", e=NE)[:, :, 1:NE],
                                 pick[:, 0], pick[:, 1], ALU.add)
                steps.done()

        @block.tensor
        def _(pe):
            pe.wait_ge(rwl_ready, 1)
            with pe.Fori(0, nb) as b:
                pe.wait_ge(norm.xn_ready, b + 1)
                transpose_tiles(nc, r, norm.xn, 0).then_inc(xt_done, 1)
                pe.wait_ge(xl_ready, b + 1)
                for j in range(NJ):
                    t = slice(j * P, (j + 1) * P)
                    last = product(nc, banks(r, 2)[:, j * E:(j + 1) * E],
                                   [(x[:, c, t], w[:, c, :]) for c in range(NC) for x, w in ((xh, rwh), (xl, rwh), (xh, rwl))])
                last.then_inc(lg_done, 1)


def kernel(**inputs):
    import numpy as _np
    import concourse.bacc as _bacc
    from concourse import mybir as _mybir
    from concourse.bass_utils import run_bass_kernel_spmd as _run

    nc = _bacc.Bacc("TRN2", target_bir_lowering=False, num_devices=1)
    arrays, d = {}, {}
    for name, a in layout(inputs).items():
        a = _np.ascontiguousarray(a)
        arrays[f"in_{name}"] = a
        d[name] = nc.dram_tensor(f"in_{name}", a.shape, _mybir.dt.from_np(a.dtype), kind="ExternalInput").ap()
    out = nc.dram_tensor("out_dram", (B, T, D), F32, kind="ExternalOutput").ap()
    build(nc, d, out)
    r = _run(nc, [arrays], core_ids=[0])
    return r.results[0]["out_dram"]
```

```python
from contextlib import ExitStack

import concourse.bass as bass
from concourse import mybir

F32 = mybir.dt.float32
F16 = mybir.dt.float16
BF16 = mybir.dt.bfloat16
U32 = mybir.dt.uint32
ALU = mybir.AluOpType
ACT = mybir.ActivationFunctionType
AX = mybir.AxisListType

B, T, D = 8, 512, 256
P = 128
NJ = T // P
NC = D // P
H, DH = 16, 16
NP_ = H // 2
SKV = 64
BT = NJ * D
LN_EPS = 1e-5
WS = 256.0
MS = 64.0
NEG = -1e30
BANK = 512
MAGIC = 12582912.0

LIN = ["x0q", "x0k", "x0v", "x0o", "a1q", "a1k", "a1v", "a1o", "x1q", "x1k", "x1v", "x1o"]
COL = {n: D * i for i, n in enumerate(LIN)}
NLIN = D * len(LIN)


class Count:

    def __init__(self, per):
        self.per, self.n = per, 0

    def up(self):
        self.n += 1
        return self.n

    def at(self, b):
        return b * self.per + self.n

    def done(self):
        assert self.n == self.per, (self.n, self.per)


class Core:
    pass


def tensors(nc, es, r):
    r.X = es.enter_context(nc.sbuf_tensor("X", [P, B * BT], F32))
    r.ident = es.enter_context(nc.sbuf_tensor("ident", [P, P], F32))
    r.identb = es.enter_context(nc.sbuf_tensor("identb", [P, P], BF16))
    r.ones = es.enter_context(nc.sbuf_tensor("ones", [P, P], F32))
    r.wh = es.enter_context(nc.sbuf_tensor("wh", [P, NC, NLIN], F16))
    r.wl = es.enter_context(nc.sbuf_tensor("wl", [P, NC, NLIN], F16))
    r.ps = es.enter_context(nc.psum_tensor("ps", [P, 8 * BANK], F32))


def new_semaphore(nc, r, name):
    s = nc.alloc_semaphore(name=name)
    r.semaphores.append(s)
    return s


def end_phase(nc, r):
    nc.clear_and_free_semaphores(r.semaphores)
    r.semaphores = []
    nc.all_engine_barrier()


def banks(r, first, n=1):
    return r.ps[:, first * BANK:(first + n) * BANK]


def setup_phase(nc, r, d):
    with ExitStack() as es:
        stage = es.enter_context(nc.sbuf_tensor("stage", [P, NC, NLIN], F32))
        x_in = new_semaphore(nc, r, ("x_in"))
        w_in = new_semaphore(nc, r, ("w_in"))
        w_hi = new_semaphore(nc, r, ("w_hi"))
        w_lo = new_semaphore(nc, r, ("w_lo"))
        consts = new_semaphore(nc, r, ("consts"))
        block = es.enter_context(nc.Block())

        @block.sync
        def _(sp):
            for c in range(NC):
                sp.dma_start(stage[:, c, :], d["wlin"][c * P:(c + 1) * P, :]).then_inc(w_in, 16)
            for b in range(B):
                sp.dma_start(r.X[:, b * BT:(b + 1) * BT].rearrange("p (j c) -> p j c", c=D),
                             d["x"][b].rearrange("(j p) c -> p j c", p=P)).then_inc(x_in, 16)
            sp.wait_ge(x_in, 16 * B)

        @block.gpsimd
        def _(pool):
            pool.memset(r.ones[:], 1.0).then_inc(consts, 1)
            pool.memset(r.ident[:], 0.0).then_inc(consts, 1)
            pool.memset(r.identb[:], 0.0).then_inc(consts, 1)
            pool.wait_ge(consts, 3)
            for m in (r.ident, r.identb):
                pool.affine_select(out=m[:], in_=m[:], compare_op=ALU.not_equal, fill=1.0, base=0,
                                   pattern=[[-1, P]], channel_multiplier=1).then_inc(consts, 1)

        @block.scalar
        def _(act):
            act.wait_ge(w_in, 16 * NC)
            for c in range(NC):
                act.activation(r.wh[:, c, :], stage[:, c, :], ACT.Copy, scale=WS).then_inc(w_hi, 1)

        @block.vector
        def _(ve):
            for c in range(NC):
                ve.wait_ge(w_hi, c + 1)
                ve.scalar_tensor_tensor(out=r.wl[:, c, :], in0=stage[:, c, :], scalar=WS,
                                        in1=r.wh[:, c, :], op0=ALU.mult, op1=ALU.subtract).then_inc(w_lo, 1)


class Norm:

    def __init__(self, nc, es, tag, r):
        sb = lambda n, s: es.enter_context(nc.sbuf_tensor(f"{tag}_{n}", s, F32))
        sem = lambda n: new_semaphore(nc, r, (f"{tag}_{n}"))
        self.stats, self.mv = sb("stats", [P, NJ, 6]), sb("mv", [P, NJ, 2])
        self.var, self.rstd = sb("var", [P, NJ]), sb("rstd", [P, NJ])
        self.power, self.pad = sb("power", [P, NJ]), sb("pad", [P, 1])
        self.xn = sb("xn", [P, NJ, D])
        self.step, self.var_ready, self.rstd_ready = sem("norm_step"), sem("var_ready"), sem("rstd_ready")
        self.power_ready = sem("power_ready")
        self.xn_ready = sem("xn_ready")

    def vector(self, ve, r, b, used=None):
        steps = Count(8)
        x = [r.X[:, bass.ds(b * BT + j * D, D)] for j in range(NJ)]
        for j in range(NJ):
            ve.bn_stats(self.stats[:, j, :], x[j]).then_inc(self.step, 1)
            steps.up()
        ve.wait_ge(self.step, steps.at(b))
        ve.memset(self.pad[:], 0.0)
        for j in range(NJ):
            ve.bn_aggr(self.mv[:, j, :], self.stats[:, j, :]).then_inc(self.step, 1)
            steps.up()
        ve.wait_ge(self.step, steps.at(b))
        ve.tensor_scalar(self.var[:], self.mv[:, :, 1], LN_EPS, None, ALU.add).then_inc(self.var_ready, 1)
        ve.wait_ge(self.rstd_ready, b + 1)
        if used is not None:
            used()
        for j in range(NJ):
            last = ve.tensor_scalar(self.xn[:, j, :], x[j], self.mv[:, j, 0:1], self.rstd[:, j:j + 1],
                                    ALU.subtract, ALU.mult)
        last.then_inc(self.xn_ready, 1)
        steps.done()

    def pool_start(self, pool):
        pool.memset(self.power[:], -0.5).then_inc(self.power_ready, 1)
        pool.wait_ge(self.power_ready, 1)

    def pool(self, pool, b):
        pool.wait_ge(self.var_ready, b + 1)
        pool.tensor_tensor(self.rstd[:], self.var[:], self.power[:], ALU.pow).then_inc(self.rstd_ready, 1)


def transpose_tiles(nc, r, src, bank):
    for c in range(NC):
        for j in range(NJ):
            last = nc.tensor.transpose(banks(r, bank + c)[:, j * P:(j + 1) * P],
                                       src[:, j, c * P:(c + 1) * P], r.ident[:])
    return last


def product(nc, out, terms):
    for n, (lhs, rhs) in enumerate(terms):
        last = nc.tensor.matmul(out, lhs, rhs, start=(n == 0), stop=(n == len(terms) - 1))
    return last


class Piece:

    def __init__(self, at, idx, lo, n, mask=None, mask_at=0, mask_n=0):
        self.at, self.idx, self.lo, self.n = at, idx, lo, n
        self.mask, self.mask_at, self.mask_n = mask, mask_at, mask_n


WIN = 64
LW = P + WIN



def full_max(h):
    return [(h, [Piece(0, j, 0, T)], [(0, 1, BANK, T, j)]) for j in range(NJ)]


def full_main(h, half):
    return (h, [Piece(BANK * k, 2 * half + k, 0, T) for k in range(2)], [(0, 1, BANK, 2 * T, 0)])


def causal_max(h, mask):
    def piece(at, j):
        return Piece(at, j, 0, (j + 1) * P, mask, j * P, P)
    return [(h, [piece(0, 0), piece(P, 1)], [(0, 1, 0, P, 0), (P, 1, 0, 2 * P, 1)])] + \
        [(h, [piece(0, j)], [(0, 1, 0, (j + 1) * P, j)]) for j in (2, 3)]


def causal_main(h, half, mask):
    ps = [Piece(BANK * (s % 2), s, s * P, T - s * P, mask, 0, P) for s in (2 * half, 2 * half + 1)]
    return (h, ps, [(p.at, 1, 0, p.n, 0) for p in ps])


def local_max(h, mask, mask0):
    return [(h, [Piece(256 * (j % 2), j, max(0, j * P - WIN), LW, mask if j else mask0, 0, LW) for j in (2 * half, 2 * half + 1)],
             [(0, 2, 256, LW, 2 * half)]) for half in range(2)]


def local_main(h, mask, mask3):
    return (h, [Piece(256 * s, s, min(s * P, T - LW), LW, mask if s < NJ - 1 else mask3, 0, LW) for s in range(NJ)],
            [(0, NJ, 256, LW, 0)])


def columns(src, at, n, stride, width):
    if n == 1:
        return src[:, at:at + width]
    return src.rearrange("p (n w) -> p n w", w=stride)[:, :n, 0:width]


def attention_phase(nc, r, d, layer, nb=B):
    binary = layer == 0
    tag = f"at{layer}"
    with ExitStack() as es:
        sb = lambda n, s, t=F32: es.enter_context(nc.sbuf_tensor(f"{tag}_{n}", s, t))
        sem = lambda n: new_semaphore(nc, r, f"{tag}_{n}")
        norm = Norm(nc, es, tag, r)
        xh, xl = sb("xh", [P, NC, T], F16), sb("xl", [P, NC, T], F16)
        qk32 = sb("qk32", [P, 4, T])
        qkh, qkl = sb("qkh", [P, 4, T], F16), sb("qkl", [P, 4, T], F16)
        qs = sb("qs", [P, 2, NP_, T], F16)
        ks = sb("ks", [P, 2, H, T], F16)
        vaug = sb("vaug", [P, 2, NJ, H, 32])
        mx = sb("mx", [P, NJ, H])
        mh, ml = sb("mh", [H, T], F16), sb("ml", [H, T], F16)
        pexp = sb("pexp", [P, 2, 4, 2 * BANK])
        ot = sb("ot", [P, 4, T])
        rec = sb("rec", [P, NJ, H])
        y, y32 = sb("y", [P, NJ, D]), sb("y32", [P, NC, T])
        yh, yl = sb("yh", [P, NC, T], F16), sb("yl", [P, NC, T], F16)
        nrow, krow = (y[0:2, i, :].bitcast(F16) for i in range(2))
        bias_out = sb("bias_out", [P, D])
        bqk = sb("bqk", [P, 4, 1])
        if binary:
            stage = pexp[:, 0].rearrange("p a (c n) -> p a c n", c=2)[:, :, :, 0:D]
            wabs = pexp[:, 1].rearrange("p a (c n) -> p a c n", c=2)[:, :, :, 0:D]
            wsign = sb("wsign", [P, 4, NC, D], F16)
            bv = sb("bv", [P, NC, 1])
            alpha = sb("alpha", [P, 6, 1])
            alpha_out = sb("alpha_out", [P, D])
            res = y32[:, 0, :]
        else:
            bv_row = sb("bv_row", [P, D])
            masks = [sb(f"mask{i}", [P, LW], BF16) for i in range(6)]
        scratch = nc.dram_tensor(f"{tag}_scratch", (2, P, 4, T), F16, kind="Internal").ap()
        zrows = nc.dram_tensor(f"{tag}_zrows", (2, NP_, T), F16, kind="Internal").ap()

        w_in, consts, mask_zero, w_abs, alpha_done, alpha_ready = (sem(n) for n in ("w_in", "consts", "mask_zero", "w_abs", "alpha_done", "alpha_ready"))
        zeroed, ones_in, step, xt_done, xh_ready, xl_ready = (sem(n) for n in ("zeroed", "ones_in", "step", "xt_done", "xh_ready", "xl_ready"))
        proj_done, projv_done, qk_ready, qkl_ready, v_ready = (sem(n) for n in ("proj_done", "projv_done", "qk_ready", "qkl_ready", "v_ready"))
        saved, stacked, mxs_ready, mx_read, mt_done = (sem(n) for n in ("saved", "stacked", "mxs_ready", "mx_read", "mt_done"))
        mh_ready, ml_ready, rows_in, st_ready, exp_done = (sem(n) for n in ("mh_ready", "ml_ready", "rows_in", "st_ready", "exp_done"))
        av_done, ot_ready, ott_done, y_ready, yt_done = (sem(n) for n in ("av_done", "ot_ready", "ott_done", "y_ready", "yt_done"))
        yh_ready, yl_ready, out_done, out_read = (sem(n) for n in ("yh_ready", "yl_ready", "out_done", "out_read"))

        NG = 4
        if binary:
            max_slots = [s for h in range(H) for s in full_max(h)]
            units = [(g, [full_main(h, half) for h in range(4 * g, 4 * g + 4)]) for g in range(4) for half in range(2)]
        else:
            max_slots = [s for h in range(H) for s in (causal_max(h, masks[0]) if h < NG else local_max(h, masks[1], masks[2]))]
            units = [(0, [causal_main(h, half, masks[3]) for h in range(NG)]) for half in range(2)] + \
                [(g, [local_main(h, masks[4], masks[5]) for h in range(4 * g, 4 * g + 4)]) for g in range(1, 4)]
        main_slots = [slot for _, slots in units for slot in slots]
        NMAX, NMAIN, NU = len(max_slots), len(main_slots), len(units)
        first_unit = [min(u for u in range(NU) if units[u][0] == g) for g in range(4)]
        last_unit = [max(u for u in range(NU) if units[u][0] == g) for g in range(4)]
        MX, ST, O, TAIL = (0, 1), (2, 4), 6, 7

        MAX_FROM = 5
        share = NMAIN - MAX_FROM

        def max_part(k):
            if k < MAX_FROM:
                return range(0)
            return range((k - MAX_FROM) * NMAX // share, (k + 1 - MAX_FROM) * NMAX // share)
        YT_AT, YH_AT, OUT_AT, X_AT = (6, 7), (7, 8), (11, 15), (12, 16)
        READS = 4 if binary else 2

        block = es.enter_context(nc.Block())

        def turns(eng, turn):
            if nb <= 4:
                for b in range(nb):
                    turn(b, b % 2, b > 0, b + 1 < nb, b + 2 < nb)
                return
            turn(0, 0, False, True, True)
            turn(1, 1, True, True, True)
            with eng.Fori(1, nb // 2 - 1) as k:
                turn(2 * k, 0, True, True, True)
                turn(2 * k + 1, 1, True, True, True)
            turn(nb - 2, 0, True, True, False)
            turn(nb - 1, 1, True, False, False)

        def heads_of(part):
            return part.rearrange("(i d) t -> d i t", d=DH)

        @block.sync
        def _(sp):
            def const(dst, src):
                sp.dma_start(dst, src, allow_slow_non_contiguous=True).then_inc(w_in, 16)
            if binary:
                for a in range(4):
                    const(stage[:, a], d["w0"][:, a * D:(a + 1) * D].rearrange("(c p) n -> p c n", p=P))
                const(bv[:], d["a0_bv"].rearrange("(c p) -> p c", p=P).unsqueeze(2))
                const(bqk[:, 0:2], d["a0_bq"].rearrange("(c p) -> p c", p=P).unsqueeze(2))
                const(bqk[:, 2:4], d["a0_bk"].rearrange("(c p) -> p c", p=P).unsqueeze(2))
                const(bias_out[:], d["a0_bp"].partition_broadcast(P))
            else:
                const(bqk[:], d["a1_bqkv"][0:2 * D].rearrange("(c p) -> p c", p=P).unsqueeze(2))
                const(bv_row[:], d["a1_bqkv"][2 * D:3 * D].partition_broadcast(P))
                const(bias_out[:], d["a1_bout"].partition_broadcast(P))
            sp.wait_ge(consts, 2)
            for i in range(NP_):
                sp.dma_start(zrows[:, i, :], nrow[:]).then_inc(stacked, 16)
            sp.wait_ge(zeroed, 4)
            for h in range(H):
                at = 64 * (h // NP_) + 48
                for p in range(2):
                    sp.dma_start(ks[at:at + 2, p, h, :], krow[:]).then_inc(stacked, 16)
            CONST = NP_ + 2 * H
            sp.wait_ge(stacked, 16 * CONST)

            def save(b):
                sp.wait_ge(qk_ready, 4 * (b + 1))
                sp.dma_start(scratch[0], qkh[:]).then_inc(saved, 16)
                sp.wait_ge(qkl_ready, 4 * (b + 1))
                sp.dma_start(scratch[1], qkl[:]).then_inc(saved, 16)

            def stack(b, p):
                for par in range(2):
                    sp.dma_start(qs[64 * par + 48:64 * par + 50, p], zrows).then_inc(stacked, 16)
                sp.wait_ge(saved, 32 * (b + 1))
                for par in range(2):
                    for rep, (qpart, kpart) in enumerate(((0, 0), (0, 1), (1, 0))):
                        rows = slice(64 * par + 16 * rep, 64 * par + 16 * rep + 16)
                        sp.dma_start(qs[rows, p], heads_of(scratch[qpart][:, par, :])).then_inc(stacked, 16)
                        sp.dma_start(ks[rows, p, par * NP_:(par + 1) * NP_, :], heads_of(scratch[kpart][:, 2 + par, :])).then_inc(stacked, 16)

            def rows(b, p):
                sp.wait_ge(ml_ready, b + 1)
                for par in range(2):
                    for row, m in ((48, mh), (49, ml)):
                        sp.dma_start(qs[64 * par + row:64 * par + row + 1, p], m[par * NP_:(par + 1) * NP_, :]).then_inc(rows_in, 16)

            def turn(b, p, before, after, after2):
                if after:
                    if before:
                        sp.wait_ge(st_ready, b * NMAIN)
                    stack(b + 1, 1 - p)
                    rows(b + 1, 1 - p)
                if after2:
                    save(b + 2)
            save(0)
            stack(0, 0)
            rows(0, 0)
            if nb > 1:
                save(1)
            turns(sp, turn)

        @block.gpsimd
        def _(pool):
            pool.memset(krow[:], MS).then_inc(consts, 1)
            pool.memset(nrow[:], 0.0).then_inc(consts, 1)
            if not binary:
                for m in masks:
                    pool.memset(m[:], 0.0).then_inc(mask_zero, 1)
                pool.wait_ge(mask_zero, 6)

                def keep(m, base, column, row):
                    return pool.affine_select(out=m[:], in_=m[:], compare_op=ALU.is_ge, fill=NEG, base=base,
                                              pattern=[[column, LW]], channel_multiplier=row)
                keep(masks[0], 0, -1, 1).then_inc(w_abs, 1)
                keep(masks[1], WIN, -1, 1).then_inc(w_abs, 1)
                keep(masks[2], 0, -1, 1).then_inc(w_abs, 1)
                keep(masks[3], 0, 1, -1).then_inc(w_abs, 1)
                keep(masks[4], 0, 1, -1).then_inc(w_abs, 1)
                keep(masks[5], -WIN, 1, -1).then_inc(w_abs, 1)
                pool.wait_ge(w_abs, 6)
                keep(masks[1], 0, 1, -1).then_inc(w_abs, 1)
                keep(masks[2], WIN, 1, -1).then_inc(w_abs, 1)
                keep(masks[4], WIN, -1, 1).then_inc(w_abs, 1)
                keep(masks[5], 2 * WIN, -1, 1).then_inc(w_abs, 1)
            norm.pool_start(pool)

            def low_qk(b, first):
                for m in range(4):
                    pool.wait_ge(qk_ready, b * 4 + m + 1)
                    if not first and m == 0:
                        pool.wait_ge(saved, 32 * b)
                    pool.tensor_tensor(qkl[:, m, :], qk32[:, m, :], qkh[:, m, :], ALU.subtract).then_inc(qkl_ready, 1)

            def low_y(b, first):
                for c in range(NC):
                    pool.wait_ge(yh_ready, b * 2 + c + 1)
                    if not first:
                        pool.wait_ge(out_done, 2 * b)
                    pool.tensor_tensor(yl[:, c, :], y32[:, c, :], yh[:, c, :], ALU.subtract).then_inc(yl_ready, 1)

            def turn(b, p, before, after, after2):
                if after2:
                    norm.pool(pool, b + 2)
                if before:
                    low_y(b - 1, not after and nb == 1 or (isinstance(b, int) and b == 1))
                if after2:
                    low_qk(b + 2, False)
            norm.pool(pool, 0)
            low_qk(0, True)
            if nb > 1:
                norm.pool(pool, 1)
                low_qk(1, False)
            turns(pool, turn)
            low_y(nb - 1, nb == 1)

        @block.scalar
        def _(act):
            act.wait_ge(w_in, 16 * (8 if binary else 3))
            if binary:
                act.activation(wsign[:], stage, ACT.Sign).then_inc(w_abs, 1)
                act.activation(wabs, stage, ACT.Abs).then_inc(w_abs, 1)
                act.wait_ge(alpha_done, 1)
                act.activation(alpha[:].rearrange("p a b -> p (a b)"), banks(r, 0)[:, 0:6], ACT.Copy, scale=1.0 / D).then_inc(alpha_ready, 1)
                act.activation(alpha_out[:], banks(r, 1)[:, 0:D], ACT.Copy, scale=1.0 / D).then_inc(alpha_ready, 1)
                act.wait_ge(alpha_ready, 2)

            def project(b, first):
                act.wait_ge(xt_done, b + 1)
                if not first:
                    act.wait_ge(projv_done, b)
                act.activation(xh[:].rearrange("p c t -> p (c t)"), banks(r, MX[0], 2), ACT.Copy).then_inc(xh_ready, 1)
                for m in range(4):
                    act.wait_ge(proj_done, b * 4 + m + 1)
                    if not first and m == 0:
                        act.wait_ge(saved, 32 * b)
                    scale = alpha[:, m, :] if binary else 1.0 / WS
                    act.activation(qk32[:, m, :], banks(r, MX[m % 2]), ACT.Identity, bias=bqk[:, m, :], scale=scale)
                    act.activation(qkh[:, m, :], banks(r, MX[m % 2]), ACT.Identity, bias=bqk[:, m, :], scale=scale).then_inc(qk_ready, 1)

            def max_high(b, first):
                act.wait_ge(mt_done, b + 1)
                if not first:
                    act.wait_ge(rows_in, 64 * b)
                act.activation(mh[:], banks(r, MX[0])[0:H, :], ACT.Copy, scale=-1.0 / MS).then_inc(mh_ready, 1)

            def exps(b, p, k, started):
                act.wait_ge(st_ready, b * NMAIN + k + 1)
                u, hh = k // 4, k % 4
                if hh == 0 and (started or u >= 2):
                    act.wait_ge(av_done, b * NU + u - 1)
                for at, n, stride, width, _ in main_slots[k][2]:
                    last = act.activation(columns(pexp[:, (p * NU + u) % 2, hh], at, n, stride, width),
                                          columns(banks(r, ST[k % 2], 2), at, n, stride, width), ACT.Exp, scale=DH ** -0.5)
                last.then_inc(exp_done, 1)

            def keep_outputs(b, g, started):
                act.wait_ge(av_done, b * NU + last_unit[g] + 1)
                if started and g == 0:
                    act.wait_ge(ott_done, 4 * b)
                act.activation(ot[:, g, :], banks(r, O), ACT.Copy).then_inc(ot_ready, 1)

            def y_high(b, c, started):
                act.wait_ge(yt_done, b * 2 + c + 1)
                if started:
                    act.wait_ge(out_done, 2 * b)
                bias, scale = (bv[:, c, :], alpha[:, 4 + c, :]) if binary else (0.0, 1.0)
                act.activation(y32[:, c, :], banks(r, TAIL), ACT.Identity, bias=bias, scale=scale)
                act.activation(yh[:, c, :], banks(r, TAIL), ACT.Identity, bias=bias, scale=scale).then_inc(yh_ready, 1)

            def turn(b, p, before, after, after2):
                second = isinstance(b, int) and b == 1
                for k in range(NMAIN):
                    exps(b, p, k, before)
                    for g in range(4):
                        if k == 4 * last_unit[g] + 6:
                            keep_outputs(b, g, before)
                    if before and k in YH_AT:
                        y_high(b - 1, YH_AT.index(k), not second)
                for g in range(4):
                    if 4 * last_unit[g] + 6 >= NMAIN:
                        keep_outputs(b, g, before)
                if after:
                    max_high(b + 1, False)
                if after2:
                    project(b + 2, False)
            project(0, True)
            max_high(0, True)
            if nb > 1:
                project(1, False)
            turns(act, turn)
            for c in range(NC):
                y_high(nb - 1, c, nb > 1)

        @block.vector
        def _(ve):
            ve.memset(ks[:, 0], 0.0).then_inc(zeroed, 1)
            ve.memset(ks[:, 1], 0.0).then_inc(zeroed, 1)
            ve.memset(vaug[:], 0.0).then_inc(zeroed, 1)
            ve.memset(qs[:], 0.0).then_inc(zeroed, 1)
            ve.wait_ge(zeroed, 4)
            ve.memset(vaug[:].rearrange("p a s h e -> p (a s h) e")[:, :, DH:DH + 1], 1.0).then_inc(ones_in, 1)
            ve.wait_ge(ones_in, 1)
            ve.wait_ge(w_in, 16 * (8 if binary else 3))
            if binary:
                ve.wait_ge(alpha_ready, 2)

            def low_x(b):
                ve.wait_ge(xh_ready, b + 1)
                ve.tensor_tensor(xl[:].rearrange("p c t -> p (c t)"), banks(r, MX[0], 2), xh[:].rearrange("p c t -> p (c t)"), ALU.subtract).then_inc(xl_ready, 1)

            def values(b, p, started):
                ve.wait_ge(projv_done, b + 1)
                if started:
                    ve.wait_ge(av_done, (b - 1) * NU)
                v_ps = banks(r, MX[0], 2)
                if binary:
                    ve.tensor_copy(vaug[:, p].rearrange("p s h e -> p (s h) e")[:, :, 0:DH], v_ps.rearrange("p (n e) -> p n e", e=DH)).then_inc(v_ready, 1)
                else:
                    for s in range(NJ):
                        last = ve.scalar_tensor_tensor(out=vaug[:, p, s, :, 0:DH], in0=v_ps[:, s * D:(s + 1) * D].rearrange("p (h e) -> p h e", e=DH),
                                                       scalar=1.0 / WS, in1=bv_row[:].rearrange("p (h e) -> p h e", e=DH), op0=ALU.mult, op1=ALU.add)
                    last.then_inc(v_ready, 1)

            def maximum(b, k, first):
                h, _, reads = max_slots[k]
                ve.wait_ge(mxs_ready, b * NMAX + k + 1)
                if k == 0 and not first:
                    ve.wait_ge(mt_done, b)
                for at, n, stride, width, j in reads:
                    last = ve.reduce_max(mx[:, j:j + n, h], columns(banks(r, MX[k % 2]), at, n, stride, width), AX.X)
                last.then_inc(mx_read, 1)

            def max_low(b):
                ve.wait_ge(mh_ready, b + 1)
                ve.scalar_tensor_tensor(out=ml[:], in0=banks(r, MX[0])[0:H, :], scalar=-1.0 / MS, in1=mh[:], op0=ALU.mult, op1=ALU.subtract).then_inc(ml_ready, 1)

            def divide(b, started):
                steps = Count(NJ)
                for j in range(NJ):
                    ve.wait_ge(ott_done, b * NJ + j + 1)
                    o = banks(r, TAIL).rearrange("p (h e) -> p h e", e=32)
                    ve.reciprocal(rec[:, j, :], o[:, :, DH]).then_inc(step, 1)
                    steps.up()
                    ve.wait_ge(step, steps.at(b))
                    if started and j == 0:
                        ve.wait_ge(yt_done, 2 * b)
                    ve.tensor_tensor(y[:, j, :].rearrange("p (h e) -> p h e", e=DH), o[:, :, 0:DH],
                                     rec[:, j, :].unsqueeze(2).broadcast_to([P, H, DH]), ALU.mult).then_inc(y_ready, 1)
                steps.done()

            def residual(b, half):
                ve.wait_ge(out_done, 2 * b + half + 1)
                x = r.X[:, bass.ds(b * BT + half * 2 * D, 2 * D)]
                xj = x.rearrange("p (j n) -> p j n", n=D)
                if binary:
                    ve.tensor_tensor(res.rearrange("p (j n) -> p j n", n=D), banks(r, TAIL).rearrange("p (j n) -> p j n", n=D),
                                     alpha_out[:].unsqueeze(1).broadcast_to([P, 2, D]), ALU.mult).then_inc(out_read, 1)
                    ve.wait_ge(out_read, 4 * b + 2 * half + 1)
                    ve.tensor_tensor(x, x, res, ALU.add).then_inc(out_read, 1)
                    ve.wait_ge(out_read, 4 * b + 2 * half + 2)
                else:
                    ve.scalar_tensor_tensor(out=x, in0=banks(r, TAIL), scalar=1.0 / WS, in1=x, op0=ALU.mult, op1=ALU.add).then_inc(out_read, 1)
                    ve.wait_ge(out_read, 2 * b + half + 1)
                ve.tensor_tensor(xj, xj, bias_out[:].unsqueeze(1).broadcast_to([P, 2, D]), ALU.add)

            def turn(b, p, before, after, after2):
                second = isinstance(b, int) and b == 1
                if before:
                    divide(b - 1, not second)
                if after2:
                    norm.vector(ve, r, b + 2, lambda: ve.wait_ge(xt_done, b + 2))
                if after:
                    values(b + 1, 1 - p, before)
                for k in range(NMAIN):
                    if after:
                        for i in max_part(k):
                            maximum(b + 1, i, False)
                    if before and k in X_AT:
                        residual(b - 1, X_AT.index(k))
                if after:
                    max_low(b + 1)
                if after2:
                    low_x(b + 2)
            norm.vector(ve, r, 0)
            low_x(0)
            values(0, 0, False)
            for k in range(NMAX):
                maximum(0, k, True)
            max_low(0)
            if nb > 1:
                norm.vector(ve, r, 1, lambda: ve.wait_ge(xt_done, 1))
                low_x(1)
            turns(ve, turn)
            divide(nb - 1, nb > 1)
            for half in range(2):
                residual(nb - 1, half)

        @block.tensor
        def _(pe):
            if binary:
                pe.wait_ge(w_abs, 2)
                for a in range(6):
                    for c in range(NC):
                        nc.tensor.matmul(banks(r, 0)[:, a:a + 1], wabs[:, a // 2, c, (a % 2) * P:(a % 2 + 1) * P], r.ones[:, 0:1],
                                         start=(c == 0), stop=(c == NC - 1))
                for c in range(NC):
                    last = nc.tensor.matmul(banks(r, 1)[:, 0:D], r.ones[:], wabs[:, 3, c, :], start=(c == 0), stop=(c == NC - 1))
                last.then_inc(alpha_done, 1)
                pe.wait_ge(alpha_ready, 2)
            else:
                pe.wait_ge(w_abs, 10)

            def weights(name, m0, m1, hi, lo):
                if binary:
                    a = "qkvo".index(name)
                    return [(wsign[:, a, c, m0:m1], c, part) for c in range(NC) for part in (hi, lo)]
                at = COL[f"a1{name}"]
                return [(w[:, c, at + m0:at + m1], c, part) for c in range(NC) for w, part in ((r.wh, hi), (r.wh, lo), (r.wl, hi))]

            def project(b):
                pe.wait_ge(norm.xn_ready, b + 1)
                transpose_tiles(nc, r, norm.xn, MX[0]).then_inc(xt_done, 1)
                pe.wait_ge(xh_ready, b + 1)
                pe.wait_ge(xl_ready, b + 1)
                for m in range(4):
                    if m >= 2:
                        pe.wait_ge(qk_ready, b * 4 + m - 1)
                    product(nc, banks(r, MX[m % 2]), [(w, part[:, c, :]) for w, c, part in weights("qk"[m // 2], (m % 2) * P, (m % 2 + 1) * P, xh, xl)]).then_inc(proj_done, 1)

            def project_values(b):
                pe.wait_ge(qk_ready, 4 * (b + 1))
                for s in range(NJ):
                    last = product(nc, banks(r, MX[0], 2)[:, s * D:(s + 1) * D],
                                   [(part[:, c, s * P:(s + 1) * P], w) for w, c, part in weights("v", 0, D, xh, xl)])
                last.then_inc(projv_done, 1)

            def masked(out, lhs, rhs, piece):
                last = nc.tensor.matmul(out, lhs, rhs, start=True, stop=True)
                if piece.mask is not None:
                    last = nc.tensor.matmul(out[:, piece.mask_at:piece.mask_at + piece.mask_n], r.identb[:], piece.mask[:, 0:piece.mask_n],
                                            start=False, stop=True, skip_group_check=True)
                return last

            def maximum(b, p, k):
                h, pieces, _ = max_slots[k]
                if k == 0:
                    pe.wait_ge(stacked, 16 * (14 * (b + 1) + NP_ + 2 * H))
                    pe.wait_ge(v_ready, b + 1)
                if k >= 2:
                    pe.wait_ge(mx_read, b * NMAX + k - 1)
                for piece in pieces:
                    last = masked(banks(r, MX[k % 2])[:, piece.at:piece.at + piece.n], qs[:, p, h % NP_, piece.idx * P:(piece.idx + 1) * P],
                                  ks[:, p, h, piece.lo:piece.lo + piece.n], piece)
                last.then_inc(mxs_ready, 1)

            def transpose_max(b):
                pe.wait_ge(mx_read, (b + 1) * NMAX)
                for j in range(NJ):
                    last = nc.tensor.transpose(banks(r, MX[0])[0:H, j * P:(j + 1) * P], mx[:, j, :], r.ident[:])
                last.then_inc(mt_done, 1)

            def scores(b, p, k, started):
                h, pieces, _ = main_slots[k]
                if k == 0:
                    pe.wait_ge(rows_in, 64 * (b + 1))
                if started or k >= 2:
                    pe.wait_ge(exp_done, b * NMAIN + k - 1)
                for piece in pieces:
                    last = masked(banks(r, ST[k % 2], 2)[:, piece.at:piece.at + piece.n], ks[:, p, h, piece.idx * P:(piece.idx + 1) * P],
                                  qs[:, p, h % NP_, piece.lo:piece.lo + piece.n], piece)
                last.then_inc(st_ready, 1)

            def weigh(b, p, u, started):
                g, slots = units[u]
                pe.wait_ge(exp_done, b * NMAIN + 4 * (u + 1))
                if u == first_unit[g] and (started or g):
                    pe.wait_ge(ot_ready, b * 4 + g)
                for n in range(len(slots[0][1])):
                    for hh, (h, pieces, _) in enumerate(slots):
                        piece = pieces[n]
                        last = nc.tensor.matmul(banks(r, O)[32 * hh:32 * hh + 32, piece.lo:piece.lo + piece.n], vaug[:, p, piece.idx, h, :],
                                                pexp[:, (p * NU + u) % 2, hh, piece.at:piece.at + piece.n],
                                                start=(u == first_unit[g] and n == 0), stop=True, skip_group_check=True)
                last.then_inc(av_done, 1)

            def transpose_outputs(b, j, started):
                if j == 0:
                    pe.wait_ge(ot_ready, 4 * (b + 1))
                    if started:
                        pe.wait_ge(out_read, READS * b)
                else:
                    pe.wait_ge(y_ready, b * NJ + j)
                for g in range(4):
                    last = nc.tensor.transpose(banks(r, TAIL)[:, g * P:(g + 1) * P], ot[:, g, j * P:(j + 1) * P], r.ident[:])
                last.then_inc(ott_done, 1)

            def transpose_y(b, c):
                pe.wait_ge(y_ready, NJ * (b + 1))
                if c:
                    pe.wait_ge(yh_ready, 2 * b + 1)
                for j in range(NJ):
                    last = nc.tensor.transpose(banks(r, TAIL)[:, j * P:(j + 1) * P], y[:, j, c * P:(c + 1) * P], r.ident[:])
                last.then_inc(yt_done, 1)

            def output(b, half):
                pe.wait_ge(yl_ready, 2 * (b + 1))
                if half:
                    pe.wait_ge(out_read, READS * b + READS // 2)
                for j in range(2):
                    t = slice((2 * half + j) * P, (2 * half + j + 1) * P)
                    last = product(nc, banks(r, TAIL)[:, j * D:(j + 1) * D], [(part[:, c, t], w) for w, c, part in weights("o", 0, D, yh, yl)])
                last.then_inc(out_done, 1)

            def turn(b, p, before, after, after2):
                second = isinstance(b, int) and b == 1
                for k in range(NMAIN):
                    scores(b, p, k, before)
                    if k >= 5 and (k - 5) % 4 == 0:
                        weigh(b, p, (k - 5) // 4, before)
                    if before and k < NJ:
                        transpose_outputs(b - 1, k, not second)
                    if before and k in YT_AT:
                        transpose_y(b - 1, YT_AT.index(k))
                    if before and k in OUT_AT:
                        output(b - 1, OUT_AT.index(k))
                    if after and k == 4:
                        project_values(b + 1)
                    if after:
                        for i in max_part(k):
                            maximum(b + 1, 1 - p, i)
                weigh(b, p, NU - 1, before)
                if after:
                    transpose_max(b + 1)
                if after2:
                    pe.wait_ge(ml_ready, b + 2)
                    project(b + 2)
            project(0)
            project_values(0)
            for k in range(NMAX):
                maximum(0, 0, k)
            transpose_max(0)
            if nb > 1:
                pe.wait_ge(ml_ready, 1)
                project(1)
            turns(pe, turn)
            for j in range(NJ):
                transpose_outputs(nb - 1, j, nb > 1)
            for c in range(NC):
                transpose_y(nb - 1, c)
            for half in range(2):
                output(nb - 1, half)


def store_phase(nc, r, out, nb=B):
    with ExitStack() as es:
        stored = new_semaphore(nc, r, ("stored"))
        block = es.enter_context(nc.Block())

        @block.sync
        def _(sp):
            for b in range(nb):
                sp.dma_start(out[b].rearrange("(j p) c -> p j c", p=P),
                             r.X[:, b * BT:(b + 1) * BT].rearrange("p (j c) -> p j c", c=D)).then_inc(stored, 16)
            sp.wait_ge(stored, 16 * nb)


def layout(inp):
    import numpy as np
    f = {k: np.asarray(v) for k, v in inp.items()}
    tr = lambda a: np.ascontiguousarray(np.swapaxes(a, -1, -2))
    a = {"x": f["x"], "ctxT": np.ascontiguousarray(f["ctx_1024"].reshape(B * SKV, D).T)}
    a["w0"] = np.concatenate([tr(f[f"L0_attn_W{n}"]) for n in "qkvp"], axis=1)
    a["wlin"] = np.concatenate([tr(f[f"L0_xattn_W{n}"]) for n in "qkvo"] + [f["L1_attn_w_qkv"], f["L1_attn_w_out"]]
                               + [f[f"L1_xattn_W{n}"] for n in "qkvo"], axis=1)
    for n in "qkvp":
        a[f"a0_b{n}"] = f[f"L0_attn_b{n}"]
    a["a1_bqkv"], a["a1_bout"] = f["L1_attn_b_qkv"], f["L1_attn_b_out"]
    for n in "qkvo":
        a[f"x0_b{n}"], a[f"x1_b{n}"] = f[f"L0_xattn_b{n}"], f[f"L1_xattn_b{n}"]
    a["f_gate"], a["f_up"], a["f_down"] = tr(f["L0_ffn_w_gate"]), tr(f["L0_ffn_w_up"]), tr(f["L0_ffn_w_down"])
    for n, s, w in (("gate", "sg_w", "wg"), ("up", "su_w", "wu"), ("down", "sd_w", "wd")):
        a[f"m_{n}"] = np.concatenate([tr(f[f"L1_ffn_{s}"])[None], tr(f[f"L1_ffn_{w}"])])
    a["m_router"], a["m_bias"] = tr(f["L1_ffn_router_w"]), f["L1_ffn_routing_bias"]
    return a


def build(nc, d, out, phases=("at0", "x0", "ff0", "at1", "x1", "moe"), nb=B):
    r = Core()
    r.semaphores = []
    with ExitStack() as es:
        tensors(nc, es, r)
        setup_phase(nc, r, d)
        end_phase(nc, r)
        for p in phases:
            if p == "at0":
                attention_phase(nc, r, d, 0, nb)
            if p == "at1":
                attention_phase(nc, r, d, 1, nb)
            if p == "x0":
                cross0_phase(nc, r, d, nb)
            if p == "ff0":
                quant_ffn_phase(nc, r, d, nb)
            if p == "x1":
                cross1_phase(nc, r, d, nb)
            if p == "moe":
                experts_phase(nc, r, d, nb)
            end_phase(nc, r)
        store_phase(nc, r, out, nb)


def cross0_phase(nc, r, d, nb=B):
    tag = "x0"
    scale = float(D) ** -0.5
    with ExitStack() as es:
        sb = lambda n, s, t=F32: es.enter_context(nc.sbuf_tensor(f"{tag}_{n}", s, t))
        sem = lambda n: new_semaphore(nc, r, (f"{tag}_{n}"))
        norm = Norm(nc, es, tag, r)
        ctx32, ctxh, ctxl = sb("ctx32", [P, NC, B * SKV]), sb("ctxh", [P, NC, B * SKV], F16), sb("ctxl", [P, NC, B * SKV], F16)
        k32, kh, kl = sb("k32", [P, NC, B * SKV]), sb("kh", [P, NC, B * SKV], F16), sb("kl", [P, NC, B * SKV], F16)
        v_all, vcur = sb("v_all", [SKV, B * D]), sb("vcur", [SKV, D])
        x32, xh, xl = sb("x32", [P, NC, T]), sb("xh", [P, NC, T], F16), sb("xl", [P, NC, T], F16)
        q32, qh, ql = sb("q32", [P, NC, T]), sb("qh", [P, NC, T], F16), sb("ql", [P, NC, T], F16)
        mx, nm, total, rec = sb("mx", [P, NJ]), sb("nm", [P, NJ]), sb("total", [P, NJ]), sb("rec", [P, NJ])
        e, pr, pt = sb("e", [P, NJ, SKV]), sb("pr", [P, NJ, SKV]), sb("pt", [SKV, T])
        z32, zh, zl = sb("z32", [P, NC, T]), sb("zh", [P, NC, T], F16), sb("zl", [P, NC, T], F16)
        bq, bk = sb("bq", [P, NC, 1]), sb("bk", [P, NC, 1])
        bv_row, bias_out = sb("bv_row", [SKV, D]), sb("bias_out", [P, D])
        (w_in, ctxh_ready, ctxl_ready, kps_done, k32_ready, kh_ready, kl_ready, vps_done, v_ready) = (
            sem(n) for n in ("w_in", "ctxh_ready", "ctxl_ready", "kps_done", "k32_ready", "kh_ready", "kl_ready", "vps_done", "v_ready"))
        (xt_done, xh_ready, xl_ready, q_done, q_ready, ql_ready, s_done, nm_ready, e_ready, p_ready, pt_done, pt_ready) = (
            sem(n) for n in ("xt_done", "xh_ready", "xl_ready", "q_done", "q_ready", "ql_ready", "s_done", "nm_ready", "e_ready", "p_ready", "pt_done", "pt_ready"))
        (vcur_ready, att_done, z_ready, zh_ready, zl_ready, out_done, step) = (
            sem(n) for n in ("vcur_ready", "att_done", "z_ready", "zh_ready", "zl_ready", "out_done", "step"))
        flat = lambda t: t[:].rearrange("p c t -> p (c t)")
        block = es.enter_context(nc.Block())

        def three(name, m0, m1, hi, lo):
            at = COL[f"x0{name}"]
            return [(w[:, c, at + m0:at + m1], c, part) for c in range(NC) for w, part in ((r.wh, hi), (r.wh, lo), (r.wl, hi))]

        @block.sync
        def _(sp):
            def const(dst, src):
                sp.dma_start(dst, src, allow_slow_non_contiguous=True).then_inc(w_in, 16)
            const(ctx32[:], d["ctxT"].rearrange("(c p) n -> p c n", p=P))
            const(bq[:], d["x0_bq"].rearrange("(c p) -> p c", p=P).unsqueeze(2))
            const(bk[:], d["x0_bk"].rearrange("(c p) -> p c", p=P).unsqueeze(2))
            const(bv_row[:], d["x0_bv"].partition_broadcast(SKV))
            const(bias_out[:], d["x0_bo"].partition_broadcast(P))

        @block.gpsimd
        def _(pool):
            norm.pool_start(pool)
            with pool.Fori(0, nb) as b:
                norm.pool(pool, b)
                pool.wait_ge(q_ready, b + 1)
                pool.tensor_tensor(ql[:], q32[:], qh[:], ALU.subtract).then_inc(ql_ready, 1)
                pool.wait_ge(zh_ready, b + 1)
                pool.tensor_tensor(zl[:], z32[:], zh[:], ALU.subtract).then_inc(zl_ready, 1)

        @block.scalar
        def _(act):
            act.wait_ge(w_in, 16 * 5)
            act.activation(ctxh[:], ctx32[:], ACT.Copy).then_inc(ctxh_ready, 1)
            act.wait_ge(kps_done, 1)
            for m in range(NC):
                act.activation(k32[:, m, :], banks(r, 2 + m), ACT.Identity, bias=bk[:, m, :], scale=1.0 / WS)
                last = act.activation(kh[:, m, :], banks(r, 2 + m), ACT.Identity, bias=bk[:, m, :], scale=1.0 / WS)
            last.then_inc(kh_ready, 1)
            with act.Fori(0, nb) as b:
                act.wait_ge(xt_done, b + 1)
                act.activation(flat(xh), banks(r, 0, 2), ACT.Copy).then_inc(xh_ready, 1)
                act.activation(flat(x32), banks(r, 0, 2), ACT.Copy).then_inc(xh_ready, 1)
                act.wait_ge(q_done, b + 1)
                for m in range(NC):
                    act.activation(q32[:, m, :], banks(r, 2 + m), ACT.Identity, bias=bq[:, m, :], scale=1.0 / WS)
                    last = act.activation(qh[:, m, :], banks(r, 2 + m), ACT.Identity, bias=bq[:, m, :], scale=1.0 / WS)
                last.then_inc(q_ready, 1)
                act.wait_ge(nm_ready, b + 1)
                for j in range(NJ):
                    last = act.activation(e[:, j, :], banks(r, 4)[:, j * SKV:(j + 1) * SKV], ACT.Exp, bias=nm[:, j:j + 1],
                                          scale=scale, accum_out=total[:, j:j + 1])
                last.then_inc(e_ready, 1)
                act.wait_ge(pt_done, b + 1)
                act.activation(pt[:], banks(r, 5)[0:SKV, :], ACT.Copy).then_inc(pt_ready, 1)
                act.wait_ge(z_ready, b + 1)
                act.activation(zh[:], z32[:], ACT.Copy).then_inc(zh_ready, 1)

        @block.vector
        def _(ve):
            ve.wait_ge(ctxh_ready, 1)
            ve.tensor_tensor(ctxl[:], ctx32[:], ctxh[:], ALU.subtract).then_inc(ctxl_ready, 1)
            ve.wait_ge(kh_ready, 1)
            ve.tensor_tensor(kl[:], k32[:], kh[:], ALU.subtract).then_inc(kl_ready, 1)
            ve.wait_ge(vps_done, 1)
            for s in range(B):
                last = ve.scalar_tensor_tensor(out=v_all[:, s * D:(s + 1) * D], in0=banks(r, 4, 4)[0:SKV, s * D:(s + 1) * D], scalar=1.0 / WS,
                                               in1=bv_row[:], op0=ALU.mult, op1=ALU.add)
            last.then_inc(v_ready, 1)
            ve.wait_ge(v_ready, 1)
            with ve.Fori(0, nb) as b:
                steps = Count(3)
                norm.vector(ve, r, b)
                ve.wait_ge(xh_ready, 2 * (b + 1))
                ve.tensor_tensor(flat(xl), flat(x32), flat(xh), ALU.subtract).then_inc(xl_ready, 1)
                ve.tensor_scalar(vcur[:], v_all[:, bass.ds(b * D, D)], 1.0, None, ALU.mult).then_inc(vcur_ready, 1)
                ve.wait_ge(s_done, b + 1)
                ve.reduce_max(mx[:], banks(r, 4)[:, 0:NJ * SKV].rearrange("p (j s) -> p j s", s=SKV), AX.X).then_inc(step, 1)
                steps.up()
                ve.wait_ge(step, steps.at(b))
                ve.tensor_scalar(nm[:], mx[:], -scale, None, ALU.mult).then_inc(nm_ready, 1)
                ve.wait_ge(e_ready, b + 1)
                ve.reciprocal(rec[:], total[:]).then_inc(step, 1)
                steps.up()
                ve.wait_ge(step, steps.at(b))
                ve.tensor_tensor(pr[:], e[:], rec[:].unsqueeze(2).broadcast_to([P, NJ, SKV]), ALU.mult).then_inc(p_ready, 1)
                ve.wait_ge(att_done, b + 1)
                ve.tensor_tensor(flat(z32), banks(r, 6, 2), flat(x32), ALU.add).then_inc(z_ready, 1)
                ve.wait_ge(out_done, b + 1)
                x = r.X[:, bass.ds(b * BT, BT)]
                ve.scalar_tensor_tensor(out=x, in0=banks(r, 2, 2), scalar=1.0 / WS, in1=x, op0=ALU.mult, op1=ALU.add).then_inc(step, 1)
                steps.up()
                ve.wait_ge(step, steps.at(b))
                xj = x.rearrange("p (j n) -> p j n", n=D)
                ve.tensor_tensor(xj, xj, bias_out[:].unsqueeze(1).broadcast_to([P, NJ, D]), ALU.add)
                steps.done()

        @block.tensor
        def _(pe):
            pe.wait_ge(ctxh_ready, 1)
            pe.wait_ge(ctxl_ready, 1)
            for m in range(NC):
                last = product(nc, banks(r, 2 + m), [(w, part[:, c, :]) for w, c, part in three("k", m * P, (m + 1) * P, ctxh, ctxl)])
            last.then_inc(kps_done, 1)
            for s in range(B):
                last = product(nc, banks(r, 4, 4)[0:SKV, s * D:(s + 1) * D],
                               [(part[:, c, s * SKV:(s + 1) * SKV], w) for w, c, part in three("v", 0, D, ctxh, ctxl)])
            last.then_inc(vps_done, 1)
            pe.wait_ge(kl_ready, 1)
            pe.wait_ge(v_ready, 1)
            with pe.Fori(0, nb) as b:
                pe.wait_ge(norm.xn_ready, b + 1)
                transpose_tiles(nc, r, norm.xn, 0).then_inc(xt_done, 1)
                pe.wait_ge(xl_ready, b + 1)
                for m in range(NC):
                    last = product(nc, banks(r, 2 + m), [(w, part[:, c, :]) for w, c, part in three("q", m * P, (m + 1) * P, xh, xl)])
                last.then_inc(q_done, 1)
                pe.wait_ge(ql_ready, b + 1)
                for j in range(NJ):
                    t = slice(j * P, (j + 1) * P)
                    last = product(nc, banks(r, 4)[:, j * SKV:(j + 1) * SKV],
                                   [(a[:, c, t], k[:, c, bass.ds(b * SKV, SKV)]) for c in range(NC) for a, k in ((qh, kh), (qh, kl), (ql, kh))])
                last.then_inc(s_done, 1)
                pe.wait_ge(p_ready, b + 1)
                nc.tensor.matmul(banks(r, 5)[:, 0:1], r.ident[:], r.ones[:, 0:1], start=True, stop=True)
                for j in range(NJ):
                    last = nc.tensor.transpose(banks(r, 5)[0:SKV, j * P:(j + 1) * P], pr[:, j, :], r.ident[:])
                last.then_inc(pt_done, 1)
                pe.wait_ge(pt_ready, b + 1)
                pe.wait_ge(vcur_ready, b + 1)
                for m in range(NC):
                    last = nc.tensor.matmul(banks(r, 6 + m), vcur[:, m * P:(m + 1) * P], pt[:], start=True, stop=True)
                last.then_inc(att_done, 1)
                pe.wait_ge(zl_ready, b + 1)
                for j in range(NJ):
                    last = product(nc, banks(r, 2, 2)[:, j * D:(j + 1) * D],
                                   [(part[:, c, j * P:(j + 1) * P], w) for w, c, part in three("o", 0, D, zh, zl)])
                last.then_inc(out_done, 1)


def quant_ffn_phase(nc, r, d, nb=B):
    tag = "ff"
    FI = 1024
    NI = FI // P
    with ExitStack() as es:
        sb = lambda n, s, t=F32: es.enter_context(nc.sbuf_tensor(f"{tag}_{n}", s, t))
        sem = lambda n: new_semaphore(nc, r, (f"{tag}_{n}"))
        norm = Norm(nc, es, tag, r)
        NW = NC * FI
        stage = sb("stage", [P, 3, NW])
        tmp = sb("tmp", [P, NW])
        wq = sb("wq", [P, 3, NW], BF16)
        rowsum, wmean, wrec = sb("rowsum", [P, 3]), sb("wmean", [P, 3]), sb("wrec", [P, 3])
        magic = sb("magic", [P, 1])
        amax, arec, ascale, aq = sb("amax", [P, NJ]), sb("arec", [P, NJ]), sb("ascale", [P, NJ]), sb("aq", [P, 2, NJ])
        xr, xq, xqt = sb("xr", [P, NJ, D]), sb("xq", [P, NJ, D], BF16), sb("xqt", [P, NC, T], BF16)
        sg, h, hr, hq, ht = sb("sg", [P, 2, FI]), sb("h", [P, 2, FI]), sb("hr", [P, 2, FI]), sb("hq", [P, 2, FI], BF16), sb("ht", [P, 2, NI, P], BF16)
        hmax, hrec, hscale, hdq = sb("hmax", [P, NJ]), sb("hrec", [P, NJ]), sb("hscale", [P, NJ]), sb("hdq", [P, NJ])
        (w_in, magic_in, abs_ready, tot_done, mean_ready, step, wq_ready, xq_ready, xt_done, xqt_ready) = (
            sem(n) for n in ("w_in", "magic_in", "abs_ready", "tot_done", "mean_ready", "step", "wq_ready", "xq_ready", "xt_done", "xqt_ready"))
        (gate_done, up_done, sg_ready, h_ready, hscale_ready, hr_ready, hq_ready, htps_done, ht_ready, out_done, out_read) = (
            sem(n) for n in ("gate_done", "up_done", "sg_ready", "h_ready", "hscale_ready", "hr_ready", "hq_ready", "htps_done", "ht_ready", "out_done", "out_read"))
        GATE, UP, DOWN, HT = 1, 3, 5, 7
        block = es.enter_context(nc.Block())

        @block.sync
        def _(sp):
            for n, w in enumerate(("f_gate", "f_up", "f_down")):
                k = NI if n == 2 else NC
                sp.dma_start(stage[:, n, :].rearrange("p (c n) -> p c n", c=k), d[w].rearrange("(c p) n -> p c n", p=P)).then_inc(w_in, 16)

        @block.gpsimd
        def _(pool):
            pool.memset(magic[:], MAGIC).then_inc(magic_in, 1)
            norm.pool_start(pool)
            with pool.Fori(0, nb) as b:
                norm.pool(pool, b)
                for j in range(NJ):
                    pool.wait_ge(hr_ready, b * NJ + j + 1)
                    pool.tensor_tensor(hq[:, j % 2, :], hr[:, j % 2, :], magic[:].broadcast_to([P, FI]), ALU.subtract).then_inc(hq_ready, 1)

        @block.scalar
        def _(act):
            act.wait_ge(w_in, 48)
            for n in range(3):
                last = act.activation(h[:].rearrange("p a b -> p (a b)"), stage[:, n, :], ACT.Abs, accum_out=rowsum[:, n:n + 1])
                last.then_inc(abs_ready, 1)
                act.wait_ge(abs_ready, n + 1)
            act.wait_ge(magic_in, 1)
            with act.Fori(0, nb) as b:
                act.wait_ge(xt_done, b + 1)
                act.activation(xqt[:].rearrange("p c t -> p (c t)"), banks(r, 0).bitcast(BF16), ACT.Copy).then_inc(xqt_ready, 1)

                def squash(j):
                    act.wait_ge(gate_done, b * NJ + j + 1)
                    act.activation(sg[:, j % 2, :], banks(r, GATE, 2), ACT.Silu, scale=aq[:, 0, j:j + 1]).then_inc(sg_ready, 1)

                squash(0)
                for j in range(NJ):
                    if j + 1 < NJ:
                        squash(j + 1)
                    act.wait_ge(hscale_ready, b * NJ + j + 1)
                    act.activation(hr[:, j % 2, :], h[:, j % 2, :], ACT.Identity, bias=magic[:], scale=hscale[:, j:j + 1]).then_inc(hr_ready, 1)
                    act.wait_ge(htps_done, b * NJ + j + 1)
                    act.activation(ht[:, j % 2].rearrange("p i t -> p (i t)"), banks(r, HT).bitcast(BF16), ACT.Copy).then_inc(ht_ready, 1)

        @block.vector
        def _(ve):
            ve.wait_ge(tot_done, 1)
            ve.tensor_scalar(wmean[:], banks(r, 0)[:, 0:3], 1.0 / (D * FI), 1e-5, ALU.mult, ALU.max).then_inc(mean_ready, 1)
            ve.wait_ge(mean_ready, 1)
            ve.reciprocal(wrec[:], wmean[:]).then_inc(mean_ready, 1)
            for n in range(3):
                ve.wait_ge(mean_ready, 2 + 3 * n)
                ve.tensor_scalar(tmp[:], stage[:, n, :], wrec[:, n:n + 1], MAGIC, ALU.mult, ALU.add).then_inc(mean_ready, 1)
                ve.wait_ge(mean_ready, 3 + 3 * n)
                ve.tensor_scalar(stage[:, n, :], tmp[:], MAGIC, -1.0, ALU.subtract, ALU.max).then_inc(mean_ready, 1)
                ve.wait_ge(mean_ready, 4 + 3 * n)
                ve.tensor_scalar(wq[:, n, :], stage[:, n, :], 1.0, None, ALU.min).then_inc(mean_ready, 1)
            ve.wait_ge(mean_ready, 11)
            with ve.Fori(0, nb) as b:
                steps = Count(3 + 2 + 1 + 3 * NJ)
                norm.vector(ve, r, b)
                ve.wait_ge(norm.xn_ready, b + 1)
                ve.tensor_reduce(amax[:], norm.xn[:], AX.X, ALU.max, apply_absolute_value=True).then_inc(step, 1)
                steps.up()
                ve.wait_ge(step, steps.at(b))
                ve.tensor_scalar(amax[:], amax[:], 1e-5, None, ALU.max).then_inc(step, 1)
                steps.up()
                ve.wait_ge(step, steps.at(b))
                ve.reciprocal(arec[:], amax[:]).then_inc(step, 1)
                steps.up()
                for n in range(2):
                    ve.tensor_scalar(aq[:, n, :], amax[:], 1.0 / 127.0, wmean[:, n:n + 1], ALU.mult, ALU.mult).then_inc(step, 1)
                    steps.up()
                ve.wait_ge(step, steps.at(b))
                ve.tensor_scalar(ascale[:], arec[:], 127.0, None, ALU.mult).then_inc(step, 1)
                steps.up()
                ve.wait_ge(step, steps.at(b))
                for j in range(NJ):
                    ve.tensor_scalar(xr[:, j, :], norm.xn[:, j, :], ascale[:, j:j + 1], MAGIC, ALU.mult, ALU.add).then_inc(xq_ready, 1)
                ve.wait_ge(xq_ready, b * 5 + 4)
                ve.tensor_scalar(xq[:], xr[:], MAGIC, None, ALU.subtract).then_inc(xq_ready, 1)

                def update(j):
                    ve.wait_ge(out_done, b * NJ + j + 1)
                    x = r.X[:, bass.ds(b * BT + j * D, D)]
                    ve.scalar_tensor_tensor(out=x, in0=banks(r, DOWN + j % 2)[:, 0:D], scalar=hdq[:, j:j + 1], in1=x,
                                            op0=ALU.mult, op1=ALU.add).then_inc(out_read, 1)
                for j in range(NJ):
                    ve.wait_ge(up_done, b * NJ + j + 1)
                    ve.wait_ge(sg_ready, b * NJ + j + 1)
                    ve.scalar_tensor_tensor(out=h[:, j % 2, :], in0=banks(r, UP, 2), scalar=aq[:, 1, j:j + 1], in1=sg[:, j % 2, :],
                                            op0=ALU.mult, op1=ALU.mult).then_inc(h_ready, 1)
                    ve.wait_ge(h_ready, b * NJ + j + 1)
                    ve.tensor_reduce(hmax[:, j:j + 1], h[:, j % 2, :], AX.X, ALU.max, apply_absolute_value=True).then_inc(step, 1)
                    steps.up()
                    ve.wait_ge(step, steps.at(b))
                    ve.tensor_scalar(hmax[:, j:j + 1], hmax[:, j:j + 1], 1e-5, None, ALU.max).then_inc(step, 1)
                    steps.up()
                    ve.wait_ge(step, steps.at(b))
                    ve.reciprocal(hrec[:, j:j + 1], hmax[:, j:j + 1]).then_inc(step, 1)
                    steps.up()
                    ve.wait_ge(step, steps.at(b))
                    ve.tensor_scalar(hdq[:, j:j + 1], hmax[:, j:j + 1], 1.0 / 127.0, wmean[:, 2:3], ALU.mult, ALU.mult)
                    ve.tensor_scalar(hscale[:, j:j + 1], hrec[:, j:j + 1], 127.0, None, ALU.mult).then_inc(hscale_ready, 1)
                    if j:
                        update(j - 1)
                update(NJ - 1)
                steps.done()

        @block.tensor
        def _(pe):
            pe.wait_ge(abs_ready, 3)
            nc.tensor.matmul(banks(r, 0)[:, 0:3], r.ones[:], rowsum[:], start=True, stop=True).then_inc(tot_done, 1)
            pe.wait_ge(mean_ready, 11)
            gate_w, up_w = (wq[:, n, :].rearrange("p (c n) -> p c n", c=NC) for n in range(2))
            down_w = wq[:, 2, :].rearrange("p (c n) -> p c n", c=NI)
            with pe.Fori(0, nb) as b:
                pe.wait_ge(xq_ready, 5 * (b + 1))
                for c in range(NC):
                    for j in range(NJ):
                        last = nc.tensor.transpose(banks(r, 0).bitcast(BF16)[:, c * T + j * P:c * T + (j + 1) * P],
                                                   xq[:, j, c * P:(c + 1) * P], r.identb[:])
                last.then_inc(xt_done, 1)
                pe.wait_ge(xqt_ready, b + 1)

                def inner(j):
                    if j:
                        pe.wait_ge(sg_ready, b * NJ + j)
                    for w, bank, done in ((gate_w, GATE, gate_done), (up_w, UP, up_done)):
                        if w is up_w and j:
                            pe.wait_ge(h_ready, b * NJ + j)
                        for half in range(FI // BANK):
                            last = product(nc, banks(r, bank + half), [(xqt[:, c, j * P:(j + 1) * P], w[:, c, half * BANK:(half + 1) * BANK]) for c in range(NC)])
                        last.then_inc(done, 1)
                inner(0)
                for j in range(NJ):
                    if j + 1 < NJ:
                        inner(j + 1)
                    pe.wait_ge(hq_ready, b * NJ + j + 1)
                    if j:
                        pe.wait_ge(ht_ready, b * NJ + j)
                    for i in range(NI):
                        last = nc.tensor.transpose(banks(r, HT).bitcast(BF16)[:, i * P:(i + 1) * P], hq[:, j % 2, i * P:(i + 1) * P], r.identb[:])
                    last.then_inc(htps_done, 1)
                    pe.wait_ge(ht_ready, b * NJ + j + 1)
                    if j >= 2:
                        pe.wait_ge(out_read, b * NJ + j - 1)
                    product(nc, banks(r, DOWN + j % 2)[:, 0:D], [(ht[:, j % 2, i, :], down_w[:, i, :]) for i in range(NI)]).then_inc(out_done, 1)


def cross1_phase(nc, r, d, nb=B):
    tag = "x1"
    with ExitStack() as es:
        sb = lambda n, s, t=F32: es.enter_context(nc.sbuf_tensor(f"{tag}_{n}", s, t))
        sem = lambda n: new_semaphore(nc, r, (f"{tag}_{n}"))
        norm = Norm(nc, es, tag, r)
        ctx32, ctxh, ctxl = sb("ctx32", [P, NC, B * SKV]), sb("ctxh", [P, NC, B * SKV], F16), sb("ctxl", [P, NC, B * SKV], F16)
        k32, kh, kl = sb("k32", [P, NC, B * SKV]), sb("kh", [P, NC, B * SKV], F16), sb("kl", [P, NC, B * SKV], F16)
        kst, vblk = sb("kst", [P, B, NP_, P], F16), sb("vblk", [P, B, NP_, 64])
        kcur, vcur = sb("kcur", [P, NP_, P], F16), sb("vcur", [P, NP_, 64])
        xh, xl = sb("xh", [P, NC, T], F16), sb("xl", [P, NC, T], F16)
        q32, qh, ql = sb("q32", [P, NC, T]), sb("qh", [P, NC, T], F16), sb("ql", [P, NC, T], F16)
        qs = sb("qs", [P, NP_, T], F16)
        nrow, krow = sb("nrow", [2, NP_, T], F16), sb("krow", [2, T], F16)
        mx, mh, ml = sb("mx", [P, NJ, H]), sb("mh", [H, T], F16), sb("ml", [H, T], F16)
        pexp, ot, rec = sb("pexp", [P, NP_, T]), sb("ot", [P, 4, T]), sb("rec", [P, NJ, H])
        y, yh, yl = norm.xn, xh, xl
        bq, bk = sb("bq", [P, NC, 1]), sb("bk", [P, NC, 1])
        bv_row, bias_out = sb("bv_row", [P, D]), sb("bias_out", [P, D])
        kscratch = nc.dram_tensor(f"{tag}_kscratch", (2, P, NC, B * SKV), F16, kind="Internal").ap()
        qscratch = nc.dram_tensor(f"{tag}_qscratch", (2, P, NC, T), F16, kind="Internal").ap()
        (w_in, consts, ctxh_ready, ctxl_ready, kps_done, kh_ready, kl_ready, vps_done, v_ready, ones_in, ksaved, kstacked) = (
            sem(n) for n in ("w_in", "consts", "ctxh_ready", "ctxl_ready", "kps_done", "kh_ready", "kl_ready", "vps_done", "v_ready", "ones_in", "ksaved", "kstacked"))
        (zeroed, xt_done, xh_ready, xl_ready, q_done, q_ready, ql_ready, saved, stacked, cur_ready, mxs_ready, mx_read, mt_done) = (
            sem(n) for n in ("zeroed", "xt_done", "xh_ready", "xl_ready", "q_done", "q_ready", "ql_ready", "saved", "stacked", "cur_ready", "mxs_ready", "mx_read", "mt_done"))
        (mh_ready, ml_ready, rows_in, st_ready, exp_done, av_done, ot_ready, ott_done, y_ready, yt_done, yh_ready, yl_ready, out_done, step) = (
            sem(n) for n in ("mh_ready", "ml_ready", "rows_in", "st_ready", "exp_done", "av_done", "ot_ready", "ott_done", "y_ready", "yt_done", "yh_ready", "yl_ready", "out_done", "step"))
        flat = lambda t: t[:].rearrange("p c t -> p (c t)")
        MAXB, MAINB = (0, 6), (2, 4)
        NKD = NP_ * 6 + 2 * NP_
        block = es.enter_context(nc.Block())

        def three(name, m0, m1, hi, lo):
            at = COL[f"x1{name}"]
            return [(w[:, c, at + m0:at + m1], c, part) for c in range(NC) for w, part in ((r.wh, hi), (r.wh, lo), (r.wl, hi))]

        @block.sync
        def _(sp):
            def const(dst, src):
                sp.dma_start(dst, src, allow_slow_non_contiguous=True).then_inc(w_in, 16)
            const(ctx32[:], d["ctxT"].rearrange("(c p) n -> p c n", p=P))
            const(bq[:], d["x1_bq"].rearrange("(c p) -> p c", p=P).unsqueeze(2))
            const(bk[:], d["x1_bk"].rearrange("(c p) -> p c", p=P).unsqueeze(2))
            const(bv_row[:], d["x1_bv"].partition_broadcast(P))
            const(bias_out[:], d["x1_bo"].partition_broadcast(P))
            sp.wait_ge(kl_ready, 1)
            sp.dma_start(kscratch[0], kh[:]).then_inc(ksaved, 16)
            sp.dma_start(kscratch[1], kl[:]).then_inc(ksaved, 16)
            sp.wait_ge(consts, 2)
            sp.wait_ge(zeroed, 3)
            sp.wait_ge(ksaved, 32)
            for par in range(2):
                own = slice(par * SKV, (par + 1) * SKV)
                for i in range(NP_):
                    for rep, part in enumerate((0, 1, 0)):
                        at = 64 * par + 16 * rep
                        sp.dma_start(kst[at:at + 16, :, i, own], kscratch[part][i * DH:(i + 1) * DH, par, :].rearrange("d (b s) -> d b s", b=B)).then_inc(kstacked, 16)
                    sp.dma_start(kst[64 * par + 48:64 * par + 50, :, i, own], krow[:].rearrange("p (b s) -> p b s", b=B)).then_inc(kstacked, 16)
            with sp.Fori(0, nb) as b:
                sp.wait_ge(q_ready, b + 1)
                sp.dma_start(qscratch[0], qh[:]).then_inc(saved, 16)
                sp.wait_ge(ql_ready, b + 1)
                sp.dma_start(qscratch[1], ql[:]).then_inc(saved, 16)
                sp.wait_ge(saved, (b + 1) * 32)
                for par in range(2):
                    for rep, part in enumerate((0, 0, 1)):
                        at = 64 * par + 16 * rep
                        sp.dma_start(qs[at:at + 16, :, :], qscratch[part][:, par, :].rearrange("(i d) t -> d i t", d=DH)).then_inc(stacked, 16)
                    sp.dma_start(qs[64 * par + 48:64 * par + 50, :, :], nrow[:]).then_inc(stacked, 16)
                sp.wait_ge(stacked, 16 * 8 * (b + 1))
                sp.wait_ge(ml_ready, b + 1)
                for par in range(2):
                    for row, m in ((48, mh), (49, ml)):
                        sp.dma_start(qs[64 * par + row:64 * par + row + 1, :, :], m[par * NP_:(par + 1) * NP_, :]).then_inc(rows_in, 16)
            sp.wait_ge(rows_in, 16 * 4 * nb)

        @block.gpsimd
        def _(pool):
            pool.memset(krow[:], MS).then_inc(consts, 1)
            pool.memset(nrow[:], 0.0).then_inc(consts, 1)
            norm.pool_start(pool)
            with pool.Fori(0, nb) as b:
                norm.pool(pool, b)
                pool.wait_ge(q_ready, b + 1)
                pool.tensor_tensor(ql[:], q32[:], qh[:], ALU.subtract).then_inc(ql_ready, 1)

        @block.scalar
        def _(act):
            act.wait_ge(w_in, 16 * 5)
            act.activation(ctxh[:], ctx32[:], ACT.Copy).then_inc(ctxh_ready, 1)
            act.wait_ge(kps_done, 1)
            for m in range(NC):
                act.activation(k32[:, m, :], banks(r, 2 + m), ACT.Identity, bias=bk[:, m, :], scale=1.0 / WS)
                last = act.activation(kh[:, m, :], banks(r, 2 + m), ACT.Identity, bias=bk[:, m, :], scale=1.0 / WS)
            last.then_inc(kh_ready, 1)
            with act.Fori(0, nb) as b:
                act.wait_ge(xt_done, b + 1)
                act.activation(flat(xh), banks(r, 0, 2), ACT.Copy).then_inc(xh_ready, 1)
                act.wait_ge(q_done, b + 1)
                for m in range(NC):
                    act.activation(q32[:, m, :], banks(r, 2 + m), ACT.Identity, bias=bq[:, m, :], scale=1.0 / WS)
                    last = act.activation(qh[:, m, :], banks(r, 2 + m), ACT.Identity, bias=bq[:, m, :], scale=1.0 / WS)
                last.then_inc(q_ready, 1)
                act.wait_ge(mt_done, b + 1)
                act.activation(mh[:], banks(r, 0)[0:H, :], ACT.Copy, scale=-1.0 / MS).then_inc(mh_ready, 1)
                for k in range(4):
                    act.wait_ge(st_ready, b * 4 + k + 1)
                    act.activation(pexp[:, 2 * k:2 * k + 2, :].rearrange("p i t -> p (i t)"), banks(r, MAINB[k % 2], 2), ACT.Exp, scale=DH ** -0.5).then_inc(exp_done, 1)
                act.wait_ge(yt_done, b + 1)
                act.activation(flat(yh), banks(r, 2, 2), ACT.Copy).then_inc(yh_ready, 1)

        @block.vector
        def _(ve):
            ve.memset(kst[:], 0.0).then_inc(zeroed, 1)
            ve.memset(vblk[:], 0.0).then_inc(zeroed, 1)
            ve.memset(qs[:], 0.0).then_inc(zeroed, 1)
            ve.wait_ge(zeroed, 3)
            ve.memset(vblk[0:SKV, :, :, DH:DH + 1], 1.0)
            ve.memset(vblk[SKV:P, :, :, 32 + DH:32 + DH + 1], 1.0).then_inc(ones_in, 1)
            ve.wait_ge(ctxh_ready, 1)
            ve.tensor_tensor(ctxl[:], ctx32[:], ctxh[:], ALU.subtract).then_inc(ctxl_ready, 1)
            ve.wait_ge(kh_ready, 1)
            ve.tensor_tensor(kl[:], k32[:], kh[:], ALU.subtract).then_inc(kl_ready, 1)
            ve.wait_ge(vps_done, 1)
            for s in range(B):
                for par in range(2):
                    rows = slice(par * SKV, (par + 1) * SKV)
                    last = ve.scalar_tensor_tensor(out=vblk[rows, s, :, 32 * par:32 * par + DH],
                                                   in0=banks(r, 4, 2)[rows, s * P:(s + 1) * P].rearrange("p (i e) -> p i e", e=DH), scalar=1.0 / WS,
                                                   in1=bv_row[rows, par * P:(par + 1) * P].rearrange("p (i e) -> p i e", e=DH), op0=ALU.mult, op1=ALU.add)
            last.then_inc(v_ready, 1)
            ve.wait_ge(v_ready, 1)
            ve.wait_ge(ones_in, 1)
            ve.wait_ge(kstacked, 16 * NKD)
            with ve.Fori(0, nb) as b:
                steps = Count(NJ + 1)
                norm.vector(ve, r, b)
                ve.wait_ge(xh_ready, b + 1)
                ve.tensor_tensor(flat(xl), banks(r, 0, 2), flat(xh), ALU.subtract).then_inc(xl_ready, 1)
                ve.tensor_scalar(kcur[:], kst[:, bass.ds(b, 1)].rearrange("p o i s -> p (o i) s"), 1.0, None, ALU.mult)
                ve.tensor_scalar(vcur[:], vblk[:, bass.ds(b, 1)].rearrange("p o i s -> p (o i) s"), 1.0, None, ALU.mult).then_inc(cur_ready, 1)
                for j in range(NJ):
                    ve.wait_ge(mxs_ready, b * NJ + j + 1)
                    ve.reduce_max(mx[:, j, :].rearrange("p (par i) -> p i par", par=2), banks(r, MAXB[j % 2], 2).rearrange("p (i par s) -> p i par s", par=2, s=SKV), AX.X).then_inc(mx_read, 1)
                ve.wait_ge(mh_ready, b + 1)
                ve.scalar_tensor_tensor(out=ml[:], in0=banks(r, 0)[0:H, :], scalar=-1.0 / MS, in1=mh[:], op0=ALU.mult, op1=ALU.subtract).then_inc(ml_ready, 1)
                for g in range(4):
                    ve.wait_ge(av_done, b * 4 + g + 1)
                    ve.tensor_copy(ot[:, g, :], banks(r, 6 + g % 2)).then_inc(ot_ready, 1)
                for j in range(NJ):
                    ve.wait_ge(ott_done, b * NJ + j + 1)
                    o = banks(r, j % 2).rearrange("p (i par e) -> p i par e", par=2, e=32)
                    ve.reciprocal(rec[:, j, :], banks(r, j % 2).rearrange("p (h e) -> p h e", e=32)[:, :, DH]).then_inc(step, 1)
                    steps.up()
                    ve.wait_ge(step, steps.at(b))
                    ve.tensor_tensor(y[:, j, :].rearrange("p (par i e) -> p i par e", par=2, e=DH), o[:, :, :, 0:DH],
                                     rec[:, j, :].rearrange("p (i par) -> p i par", par=2).unsqueeze(3).broadcast_to([P, NP_, 2, DH]), ALU.mult).then_inc(y_ready, 1)
                ve.wait_ge(yh_ready, b + 1)
                ve.tensor_tensor(flat(yl), banks(r, 2, 2), flat(yh), ALU.subtract).then_inc(yl_ready, 1)
                ve.wait_ge(out_done, b + 1)
                x = r.X[:, bass.ds(b * BT, BT)]
                ve.scalar_tensor_tensor(out=x, in0=banks(r, 4, 2), scalar=1.0 / WS, in1=x, op0=ALU.mult, op1=ALU.add).then_inc(step, 1)
                steps.up()
                ve.wait_ge(step, steps.at(b))
                xj = x.rearrange("p (j n) -> p j n", n=D)
                ve.tensor_tensor(xj, xj, bias_out[:].unsqueeze(1).broadcast_to([P, NJ, D]), ALU.add)
                steps.done()

        @block.tensor
        def _(pe):
            pe.wait_ge(ctxh_ready, 1)
            pe.wait_ge(ctxl_ready, 1)
            for m in range(NC):
                last = product(nc, banks(r, 2 + m), [(w, part[:, c, :]) for w, c, part in three("k", m * P, (m + 1) * P, ctxh, ctxl)])
            last.then_inc(kps_done, 1)
            for s in range(B):
                for par in range(2):
                    last = product(nc, banks(r, 4, 2)[par * SKV:(par + 1) * SKV, s * P:(s + 1) * P],
                                   [(part[:, c, s * SKV:(s + 1) * SKV], w) for w, c, part in three("v", par * P, (par + 1) * P, ctxh, ctxl)])
            last.then_inc(vps_done, 1)
            pe.wait_ge(kh_ready, 1)
            pe.wait_ge(v_ready, 1)
            with pe.Fori(0, nb) as b:
                pe.wait_ge(norm.xn_ready, b + 1)
                transpose_tiles(nc, r, norm.xn, 0).then_inc(xt_done, 1)
                pe.wait_ge(xl_ready, b + 1)
                for m in range(NC):
                    last = product(nc, banks(r, 2 + m), [(w, part[:, c, :]) for w, c, part in three("q", m * P, (m + 1) * P, xh, xl)])
                last.then_inc(q_done, 1)
                pe.wait_ge(stacked, 16 * 8 * (b + 1))
                pe.wait_ge(cur_ready, b + 1)
                for j in range(NJ):
                    if j >= 2:
                        pe.wait_ge(mx_read, b * NJ + j - 1)
                    for i in range(NP_):
                        last = nc.tensor.matmul(banks(r, MAXB[j % 2], 2)[:, i * P:(i + 1) * P], qs[:, i, j * P:(j + 1) * P], kcur[:, i, :], start=True, stop=True)
                    last.then_inc(mxs_ready, 1)
                pe.wait_ge(mx_read, (b + 1) * NJ)
                for j in range(NJ):
                    last = nc.tensor.transpose(banks(r, 0)[0:H, j * P:(j + 1) * P], mx[:, j, :], r.ident[:])
                last.then_inc(mt_done, 1)
                pe.wait_ge(rows_in, 64 * (b + 1))

                def values(g):
                    pe.wait_ge(exp_done, b * 4 + g + 1)
                    if g >= 2:
                        pe.wait_ge(ot_ready, b * 4 + g - 1)
                    for i in (2 * g, 2 * g + 1):
                        last = nc.tensor.matmul(banks(r, 6 + g % 2)[64 * (i % 2):64 * (i % 2) + 64, :], vcur[:, i, :], pexp[:, i, :], start=True, stop=True)
                    last.then_inc(av_done, 1)

                for k in range(4):
                    if k >= 2:
                        pe.wait_ge(exp_done, b * 4 + k - 1)
                    for i in range(2):
                        last = nc.tensor.matmul(banks(r, MAINB[k % 2] + i), kcur[:, 2 * k + i, :], qs[:, 2 * k + i, :], start=True, stop=True)
                    last.then_inc(st_ready, 1)
                    if k:
                        values(k - 1)
                values(3)
                pe.wait_ge(ot_ready, 4 * (b + 1))
                for j in range(NJ):
                    if j >= 2:
                        pe.wait_ge(y_ready, b * NJ + j - 1)
                    for g in range(4):
                        last = nc.tensor.transpose(banks(r, j % 2)[:, g * P:(g + 1) * P], ot[:, g, j * P:(j + 1) * P], r.ident[:])
                    last.then_inc(ott_done, 1)
                pe.wait_ge(y_ready, NJ * (b + 1))
                transpose_tiles(nc, r, y, 2).then_inc(yt_done, 1)
                pe.wait_ge(yl_ready, b + 1)
                for j in range(NJ):
                    last = product(nc, banks(r, 4, 2)[:, j * D:(j + 1) * D], [(part[:, c, j * P:(j + 1) * P], w) for w, c, part in three("o", 0, D, yh, yl)])
                last.then_inc(out_done, 1)


def experts_phase(nc, r, d, nb=B):
    E, FI = 8, 512
    NI = FI // P
    NE = E + 1
    NW = NC * FI
    with ExitStack() as es0:
        wts = es0.enter_context(nc.sbuf_tensor("mo_wts", [P, B * NJ * NE], F32))
        xth = es0.enter_context(nc.sbuf_tensor("mo_xth", [P, NC, B * T], F16))
        xtl = es0.enter_context(nc.sbuf_tensor("mo_xtl", [P, NC, B * T], F16))
        route(nc, r, d, nb, wts, xth, xtl, E)
        end_phase(nc, r)
        with ExitStack() as es:
            tag = "mo"
            sb = lambda n, s, t=F32: es.enter_context(nc.sbuf_tensor(f"{tag}_{n}", s, t))
            sem = lambda n: new_semaphore(nc, r, (f"{tag}_{n}"))
            stage = sb("stage", [P, 3, NW])
            wh, wl = sb("wh", [P, 3, NW], F16), sb("wl", [P, 3, NW], F16)
            sg, h = sb("sg", [P, 2, FI]), sb("h", [P, 2, NI, T])
            hh, hl = sb("hh", [P, 2, NI, T], F16), sb("hl", [P, 2, NI, T], F16)
            (w_in, wh_ready, wl_ready, gu_done, sg_ready, h_ready, hh_ready, hl_ready, down_done, down_read) = (
                sem(n) for n in ("w_in", "wh_ready", "wl_ready", "gu_done", "sg_ready", "h_ready", "hh_ready", "hl_ready", "down_done", "down_read"))
            GU = ((0, 1), (2, 3))
            DN = (4, 6)
            block = es.enter_context(nc.Block())
            pairs = nb // 2

            @block.sync
            def _(sp):
                with sp.Fori(0, NE) as e:
                    sp.wait_ge(wl_ready, e * 3 + 1)
                    for n, w in enumerate(("m_gate", "m_up", "m_down")):
                        k = NI if n == 2 else NC
                        sp.dma_start(stage[:, n, :].rearrange("p (c n) -> p c n", c=k),
                                     d[w][bass.ds(e, 1)].rearrange("e (c p) n -> p (e c) n", p=P)).then_inc(w_in, 16)

            @block.scalar
            def _(act):
                with act.Fori(0, NE) as e:
                    act.wait_ge(w_in, 48 * (e + 1))
                    act.wait_ge(down_done, nb * e + 1)
                    for n in range(3):
                        act.activation(wh[:, n, :], stage[:, n, :], ACT.Copy, scale=WS).then_inc(wh_ready, 1)

                    def squash(b, par):
                        for i in range(NI):
                            n = (e * nb + b) * NI + i
                            act.wait_ge(gu_done, n + 1)
                            act.activation(sg[:, i % 2, :], banks(r, GU[i % 2][0]), ACT.Silu, scale=1.0 / WS).then_inc(sg_ready, 1)
                            act.wait_ge(h_ready, n + 1)
                            act.activation(hh[:, par, i, :], h[:, par, i, :], ACT.Copy).then_inc(hh_ready, 1)
                    with act.Fori(0, pairs) as k:
                        squash(2 * k, 0)
                        squash(2 * k + 1, 1)

            @block.vector
            def _(ve):
                ve.memset(sg[:, 0, 0:1], 0.0).then_inc(wl_ready, 1)
                ve.memset(sg[:, 0, 1:2], 0.0).then_inc(hl_ready, 1)
                with ve.Fori(0, NE) as e:
                    for n in range(3):
                        ve.wait_ge(wh_ready, 3 * e + n + 1)
                        ve.scalar_tensor_tensor(out=wl[:, n, :], in0=stage[:, n, :], scalar=WS, in1=wh[:, n, :],
                                                op0=ALU.mult, op1=ALU.subtract).then_inc(wl_ready, 1)

                    def hidden(b, par):
                        for i in range(NI):
                            n = (e * nb + b) * NI + i
                            ve.wait_ge(sg_ready, n + 1)
                            ve.scalar_tensor_tensor(out=h[:, par, i, :], in0=banks(r, GU[i % 2][1]), scalar=1.0 / WS, in1=sg[:, i % 2, :],
                                                    op0=ALU.mult, op1=ALU.mult).then_inc(h_ready, 1)
                            ve.wait_ge(hh_ready, n + 1)
                            ve.tensor_tensor(hl[:, par, i, :], h[:, par, i, :], hh[:, par, i, :], ALU.subtract).then_inc(hl_ready, 1)

                    def update(b, par):
                        ve.wait_ge(down_done, e * nb + b + 2)
                        for j in range(NJ):
                            x = r.X[:, bass.ds(b * BT + j * D, D)]
                            last = ve.scalar_tensor_tensor(out=x, in0=banks(r, DN[par], 2)[:, j * D:(j + 1) * D],
                                                           scalar=wts[:, bass.ds(b * NJ * NE + j * NE + e, 1)], in1=x, op0=ALU.mult, op1=ALU.add)
                        last.then_inc(down_read, 1)

                    hidden(0, 0)
                    if pairs > 1:
                        with ve.Fori(0, pairs - 1) as k:
                            hidden(2 * k + 1, 1)
                            update(2 * k, 0)
                            hidden(2 * k + 2, 0)
                            update(2 * k + 1, 1)
                    hidden(nb - 1, 1)
                    update(nb - 2, 0)
                    update(nb - 1, 1)

            @block.tensor
            def _(pe):
                gate, up = (lambda w, n=n: w[:, n, :].rearrange("p (c n) -> p c n", c=NC) for n in range(2))
                down = lambda w: w[:, 2, :].rearrange("p (c n) -> p c n", c=NI)
                nc.tensor.matmul(banks(r, 0)[:, 0:1], r.ones[:], r.ones[:, 0:1], start=True, stop=True).then_inc(down_done, 1)
                with pe.Fori(0, NE) as e:
                    pe.wait_ge(wl_ready, 3 * (e + 1) + 1)

                    def gate_up(b):
                        for i in range(NI):
                            n = (e * nb + b) * NI + i
                            if i >= 2:
                                pe.wait_ge(h_ready, n - 1)
                            else:
                                pe.wait_ge(hl_ready, (e * nb + b) * NI + 1)
                            for w, bank in ((gate, GU[i % 2][0]), (up, GU[i % 2][1])):
                                m = slice(i * P, (i + 1) * P)
                                last = product(nc, banks(r, bank), [(w(a)[:, c, m], x[:, c, bass.ds(b * T, T)]) for c in range(NC)
                                                                    for a, x in ((wh, xth), (wh, xtl), (wl, xth))])
                            last.then_inc(gu_done, 1)

                    def project(b, par):
                        pe.wait_ge(hl_ready, (e * nb + b + 1) * NI + 1)
                        for j in range(NJ):
                            t = slice(j * P, (j + 1) * P)
                            last = product(nc, banks(r, DN[par], 2)[:, j * D:(j + 1) * D],
                                           [(x[:, par, i, t], down(a)[:, i, :]) for i in range(NI) for x, a in ((hh, wh), (hl, wh), (hh, wl))])
                        last.then_inc(down_done, 1)

                    gate_up(0)
                    if pairs > 1:
                        with pe.Fori(0, pairs - 1) as k:
                            gate_up(2 * k + 1)
                            project(2 * k, 0)
                            gate_up(2 * k + 2)
                            project(2 * k + 1, 1)
                    gate_up(nb - 1)
                    project(nb - 2, 0)
                    project(nb - 1, 1)


def route(nc, r, d, nb, wts, xth, xtl, E):
    tag = "ro"
    NE = E + 1
    with ExitStack() as es:
        sb = lambda n, s, t=F32: es.enter_context(nc.sbuf_tensor(f"{tag}_{n}", s, t))
        sem = lambda n: new_semaphore(nc, r, (f"{tag}_{n}"))
        norm = Norm(nc, es, tag, r)
        xh, xl = sb("xh", [P, NC, T], F16), sb("xl", [P, NC, T], F16)
        w32, rwh, rwl = sb("w32", [P, NC, E]), sb("rwh", [P, NC, E], F16), sb("rwl", [P, NC, E], F16)
        bias, iota = sb("bias", [P, E]), sb("iota", [P, E])
        lg, pr = sb("lg", [P, NJ, E]), sb("pr", [P, NJ, E])
        top, idx, idxf = sb("top", [P, NJ, E]), sb("idx", [P, NJ, E], U32), sb("idxf", [P, NJ, E])
        total, rec, share = sb("total", [P, NJ, 1]), sb("rec", [P, NJ, 1]), sb("share", [P, NJ, 2])
        pick, pad = sb("pick", [P, 2, NJ, E]), sb("hold", [P, 1])
        (w_in, iota_in, rwh_ready, rwl_ready, ones_in, xt_done, xh_ready, xl_ready, lg_done, lg_ready, pr_ready, kept, step) = (
            sem(n) for n in ("w_in", "iota_in", "rwh_ready", "rwl_ready", "ones_in", "xt_done", "xh_ready", "xl_ready", "lg_done", "lg_ready", "pr_ready", "kept", "step"))
        flat = lambda t: t[:].rearrange("p c t -> p (c t)")
        block = es.enter_context(nc.Block())

        @block.sync
        def _(sp):
            sp.dma_start(w32[:], d["m_router"].rearrange("(c p) n -> p c n", p=P)).then_inc(w_in, 16)
            sp.dma_start(bias[:], d["m_bias"].partition_broadcast(P)).then_inc(kept, 16)
            with sp.Fori(0, nb) as b:
                sp.wait_ge(xh_ready, b + 1)
                sp.wait_ge(xl_ready, b + 1)
                sp.dma_start(xth[:, :, bass.ds(b * T, T)], xh[:]).then_inc(kept, 16)
                sp.dma_start(xtl[:, :, bass.ds(b * T, T)], xl[:]).then_inc(kept, 16)
            sp.wait_ge(kept, 32 * nb + 16)

        @block.gpsimd
        def _(pool):
            for n in range(E):
                last = pool.memset(iota[:, n:n + 1], float(n))
            last.then_inc(iota_in, 1)
            norm.pool_start(pool)
            with pool.Fori(0, nb) as b:
                norm.pool(pool, b)

        @block.scalar
        def _(act):
            act.wait_ge(w_in, 16)
            act.activation(rwh[:], w32[:], ACT.Copy, scale=WS).then_inc(rwh_ready, 1)
            with act.Fori(0, nb) as b:
                act.wait_ge(xt_done, b + 1)
                act.wait_ge(kept, 32 * b + 16)
                act.activation(flat(xh), banks(r, 0, 2), ACT.Copy).then_inc(xh_ready, 1)
                act.wait_ge(lg_ready, b + 1)
                act.activation(pr[:], lg[:], ACT.Sigmoid).then_inc(pr_ready, 1)

        @block.vector
        def _(ve):
            ve.wait_ge(rwh_ready, 1)
            ve.scalar_tensor_tensor(out=rwl[:], in0=w32[:], scalar=WS, in1=rwh[:], op0=ALU.mult, op1=ALU.subtract).then_inc(rwl_ready, 1)
            ve.memset(wts[:], 1.0 / WS).then_inc(ones_in, 1)
            ve.wait_ge(kept, 16)
            ve.wait_ge(ones_in, 1)
            ve.wait_ge(iota_in, 1)
            with ve.Fori(0, nb) as b:
                steps = Count(2 * NJ + 4 + 2 * NJ)
                norm.vector(ve, r, b)
                ve.wait_ge(xh_ready, b + 1)
                ve.tensor_tensor(flat(xl), banks(r, 0, 2), flat(xh), ALU.subtract).then_inc(xl_ready, 1)
                ve.wait_ge(lg_done, b + 1)
                ve.scalar_tensor_tensor(out=lg[:], in0=banks(r, 2)[:, 0:NJ * E].rearrange("p (j e) -> p j e", e=E), scalar=1.0 / WS,
                                        in1=bias[:].unsqueeze(1).broadcast_to([P, NJ, E]), op0=ALU.mult, op1=ALU.add).then_inc(lg_ready, 1)
                ve.wait_ge(pr_ready, b + 1)
                ve.memset(pad[:], 0.0)
                for j in range(NJ):
                    ve.max(top[:, j, :], pr[:, j, :]).then_inc(step, 1)
                    steps.up()
                ve.wait_ge(step, steps.at(b))
                ve.tensor_tensor(total[:], top[:, :, 0:1], top[:, :, 1:2], ALU.add).then_inc(step, 1)
                for j in range(NJ):
                    ve.max_index(idx[:, j, :], top[:, j, :], pr[:, j, :]).then_inc(step, 1)
                    steps.up()
                steps.up()
                ve.wait_ge(step, steps.at(b))
                ve.tensor_copy(idxf[:], idx[:]).then_inc(step, 1)
                ve.reciprocal(rec[:], total[:]).then_inc(step, 1)
                steps.up()
                steps.up()
                ve.wait_ge(step, steps.at(b))
                ve.scalar_tensor_tensor(out=share[:], in0=top[:, :, 0:2], scalar=1.0 / WS, in1=rec[:].broadcast_to([P, NJ, 2]),
                                        op0=ALU.mult, op1=ALU.mult).then_inc(step, 1)
                steps.up()
                ve.wait_ge(step, steps.at(b))
                for j in range(NJ):
                    for k in range(2):
                        ve.tensor_scalar(pick[:, k, j, :], iota[:], idxf[:, j, k:k + 1], share[:, j, k:k + 1], ALU.is_equal, ALU.mult).then_inc(step, 1)
                        steps.up()
                ve.wait_ge(step, steps.at(b))
                ve.tensor_tensor(wts[:, bass.ds(b * NJ * NE, NJ * NE)].rearrange("p (j e) -> p j e", e=NE)[:, :, 1:NE],
                                 pick[:, 0], pick[:, 1], ALU.add)
                steps.done()

        @block.tensor
        def _(pe):
            pe.wait_ge(rwl_ready, 1)
            with pe.Fori(0, nb) as b:
                pe.wait_ge(norm.xn_ready, b + 1)
                transpose_tiles(nc, r, norm.xn, 0).then_inc(xt_done, 1)
                pe.wait_ge(xl_ready, b + 1)
                for j in range(NJ):
                    t = slice(j * P, (j + 1) * P)
                    last = product(nc, banks(r, 2)[:, j * E:(j + 1) * E],
                                   [(x[:, c, t], w[:, c, :]) for c in range(NC) for x, w in ((xh, rwh), (xl, rwh), (xh, rwl))])
                last.then_inc(lg_done, 1)


def kernel(**inputs):
    import numpy as _np
    import concourse.bacc as _bacc
    from concourse import mybir as _mybir
    from concourse.bass_utils import run_bass_kernel_spmd as _run

    nc = _bacc.Bacc("TRN2", target_bir_lowering=False, num_devices=1)
    arrays, d = {}, {}
    for name, a in layout(inputs).items():
        a = _np.ascontiguousarray(a)
        arrays[f"in_{name}"] = a
        d[name] = nc.dram_tensor(f"in_{name}", a.shape, _mybir.dt.from_np(a.dtype), kind="ExternalInput").ap()
    out = nc.dram_tensor("out_dram", (B, T, D), F32, kind="ExternalOutput").ap()
    build(nc, d, out)
    r = _run(nc, [arrays], core_ids=[0])
    return r.results[0]["out_dram"]
```

```python
from contextlib import ExitStack

import concourse.bass as bass
from concourse import mybir

F32 = mybir.dt.float32
F16 = mybir.dt.float16
BF16 = mybir.dt.bfloat16
U32 = mybir.dt.uint32
ALU = mybir.AluOpType
ACT = mybir.ActivationFunctionType
AX = mybir.AxisListType

B, T, D = 8, 512, 256
P = 128
NJ = T // P
NC = D // P
H, DH = 16, 16
NP_ = H // 2
SKV = 64
BT = NJ * D
LN_EPS = 1e-5
WS = 256.0
MS = 64.0
NEG = -1e30
FF_WIDTH = D * 1024 // P
BANK = 512
MAGIC = 12582912.0

LIN = ["x0q", "x0k", "x0v", "x0o", "a1q", "a1k", "a1v", "a1o", "x1q", "x1k", "x1v", "x1o"]
COL = {n: D * i for i, n in enumerate(LIN)}
NLIN = D * len(LIN)


class Count:

    def __init__(self, per):
        self.per, self.n = per, 0

    def up(self):
        self.n += 1
        return self.n

    def at(self, b):
        return b * self.per + self.n

    def done(self):
        assert self.n == self.per, (self.n, self.per)


class Core:
    pass


def tensors(nc, es, r):
    r.X = es.enter_context(nc.sbuf_tensor("X", [P, B * BT], F32))
    r.ident = es.enter_context(nc.sbuf_tensor("ident", [P, P], F32))
    r.identb = es.enter_context(nc.sbuf_tensor("identb", [P, P], BF16))
    r.ones = es.enter_context(nc.sbuf_tensor("ones", [P, P], F32))
    r.wh = es.enter_context(nc.sbuf_tensor("wh", [P, NC, NLIN], F16))
    r.wl = es.enter_context(nc.sbuf_tensor("wl", [P, NC, NLIN], F16))
    r.ps = es.enter_context(nc.psum_tensor("ps", [P, 8 * BANK], F32))


def new_semaphore(nc, r, name):
    s = nc.alloc_semaphore(name=name)
    r.semaphores.append(s)
    return s


def end_phase(nc, r):
    nc.clear_and_free_semaphores(r.semaphores)
    r.semaphores = []
    nc.all_engine_barrier()


def banks(r, first, n=1):
    return r.ps[:, first * BANK:(first + n) * BANK]


def setup_phase(nc, r, d):
    with ExitStack() as es:
        stage = es.enter_context(nc.sbuf_tensor("stage", [P, NC, NLIN], F32))
        x_in = new_semaphore(nc, r, ("x_in"))
        w_in = new_semaphore(nc, r, ("w_in"))
        w_hi = new_semaphore(nc, r, ("w_hi"))
        w_lo = new_semaphore(nc, r, ("w_lo"))
        consts = new_semaphore(nc, r, ("consts"))
        block = es.enter_context(nc.Block())

        @block.sync
        def _(sp):
            for c in range(NC):
                sp.dma_start(stage[:, c, :], d["wlin"][c * P:(c + 1) * P, :]).then_inc(w_in, 16)
            for b in range(B):
                sp.dma_start(r.X[:, b * BT:(b + 1) * BT].rearrange("p (j c) -> p j c", c=D),
                             d["x"][b].rearrange("(j p) c -> p j c", p=P)).then_inc(x_in, 16)
            sp.wait_ge(x_in, 16 * B)

        @block.gpsimd
        def _(pool):
            pool.memset(r.ones[:], 1.0).then_inc(consts, 1)
            pool.memset(r.ident[:], 0.0).then_inc(consts, 1)
            pool.memset(r.identb[:], 0.0).then_inc(consts, 1)
            pool.wait_ge(consts, 3)
            for m in (r.ident, r.identb):
                pool.affine_select(out=m[:], in_=m[:], compare_op=ALU.not_equal, fill=1.0, base=0,
                                   pattern=[[-1, P]], channel_multiplier=1).then_inc(consts, 1)

        @block.scalar
        def _(act):
            act.wait_ge(w_in, 16 * NC)
            for c in range(NC):
                act.activation(r.wh[:, c, :], stage[:, c, :], ACT.Copy, scale=WS).then_inc(w_hi, 1)

        @block.vector
        def _(ve):
            for c in range(NC):
                ve.wait_ge(w_hi, c + 1)
                ve.scalar_tensor_tensor(out=r.wl[:, c, :], in0=stage[:, c, :], scalar=WS,
                                        in1=r.wh[:, c, :], op0=ALU.mult, op1=ALU.subtract).then_inc(w_lo, 1)


class Norm:

    def __init__(self, nc, es, tag, r):
        sb = lambda n, s: es.enter_context(nc.sbuf_tensor(f"{tag}_{n}", s, F32))
        sem = lambda n: new_semaphore(nc, r, (f"{tag}_{n}"))
        self.stats, self.mv = sb("stats", [P, NJ, 6]), sb("mv", [P, NJ, 2])
        self.var, self.rstd = sb("var", [P, NJ]), sb("rstd", [P, NJ])
        self.power, self.pad = sb("power", [P, NJ]), sb("pad", [P, 1])
        self.xn = sb("xn", [P, NJ, D])
        self.step, self.var_ready, self.rstd_ready = sem("norm_step"), sem("var_ready"), sem("rstd_ready")
        self.power_ready = sem("power_ready")
        self.xn_ready = sem("xn_ready")

    def statistics(self, ve, r, b):
        steps = Count(8)
        for j in range(NJ):
            ve.bn_stats(self.stats[:, j, :], r.X[:, bass.ds(b * BT + j * D, D)]).then_inc(self.step, 1)
            steps.up()
        ve.wait_ge(self.step, steps.at(b))
        ve.memset(self.pad[:], 0.0)
        for j in range(NJ):
            ve.bn_aggr(self.mv[:, j, :], self.stats[:, j, :]).then_inc(self.step, 1)
            steps.up()
        ve.wait_ge(self.step, steps.at(b))
        ve.tensor_scalar(self.var[:], self.mv[:, :, 1], LN_EPS, None, ALU.add).then_inc(self.var_ready, 1)
        steps.done()

    def apply(self, ve, r, b, used=None):
        ve.wait_ge(self.rstd_ready, b + 1)
        if used is not None:
            used()
        for j in range(NJ):
            last = ve.tensor_scalar(self.xn[:, j, :], r.X[:, bass.ds(b * BT + j * D, D)], self.mv[:, j, 0:1], self.rstd[:, j:j + 1],
                                    ALU.subtract, ALU.mult)
        last.then_inc(self.xn_ready, 1)

    def vector(self, ve, r, b, used=None):
        self.statistics(ve, r, b)
        self.apply(ve, r, b, used)

    def pool_start(self, pool):
        pool.memset(self.power[:], -0.5).then_inc(self.power_ready, 1)
        pool.wait_ge(self.power_ready, 1)

    def pool(self, pool, b):
        pool.wait_ge(self.var_ready, b + 1)
        pool.tensor_tensor(self.rstd[:], self.var[:], self.power[:], ALU.pow).then_inc(self.rstd_ready, 1)


def transpose_tiles(nc, r, src, bank):
    for c in range(NC):
        for j in range(NJ):
            last = nc.tensor.transpose(banks(r, bank + c)[:, j * P:(j + 1) * P],
                                       src[:, j, c * P:(c + 1) * P], r.ident[:])
    return last


def staggered(eng, nb, turn):
    turn(0, 0, False, True)
    turn(1, 1, True, True)
    with eng.Fori(1, nb // 2 - 1) as k:
        turn(2 * k, 0, True, True)
        turn(2 * k + 1, 1, True, True)
    turn(nb - 2, 0, True, True)
    turn(nb - 1, 1, True, False)


def product(nc, out, terms):
    for n, (lhs, rhs) in enumerate(terms):
        last = nc.tensor.matmul(out, lhs, rhs, start=(n == 0), stop=(n == len(terms) - 1))
    return last


class Piece:

    def __init__(self, at, idx, lo, n, mask=None, mask_at=0, mask_n=0):
        self.at, self.idx, self.lo, self.n = at, idx, lo, n
        self.mask, self.mask_at, self.mask_n = mask, mask_at, mask_n


WIN = 64
LW = P + WIN



def full_max(h):
    return [(h, [Piece(0, j, 0, T)], [(0, 1, BANK, T, j)]) for j in range(NJ)]


def full_main(h, half):
    return (h, [Piece(BANK * k, 2 * half + k, 0, T) for k in range(2)], [(0, 1, BANK, 2 * T, 0)])


def causal_max(h, mask):
    def piece(at, j):
        return Piece(at, j, 0, (j + 1) * P, mask, j * P, P)
    return [(h, [piece(0, 0), piece(P, 1)], [(0, 1, 0, P, 0), (P, 1, 0, 2 * P, 1)])] + \
        [(h, [piece(0, j)], [(0, 1, 0, (j + 1) * P, j)]) for j in (2, 3)]


def causal_main(h, half, mask):
    ps = [Piece(BANK * (s % 2), s, s * P, T - s * P, mask, 0, P) for s in (2 * half, 2 * half + 1)]
    return (h, ps, [(p.at, 1, 0, p.n, 0) for p in ps])


def local_max(h, mask, mask0):
    return [(h, [Piece(256 * (j % 2), j, max(0, j * P - WIN), LW, mask if j else mask0, 0, LW) for j in (2 * half, 2 * half + 1)],
             [(0, 2, 256, LW, 2 * half)]) for half in range(2)]


def local_main(h, mask, mask3):
    return (h, [Piece(256 * s, s, min(s * P, T - LW), LW, mask if s < NJ - 1 else mask3, 0, LW) for s in range(NJ)],
            [(0, NJ, 256, LW, 0)])


def columns(src, at, n, stride, width):
    if n == 1:
        return src[:, at:at + width]
    return src.rearrange("p (n w) -> p n w", w=stride)[:, :n, 0:width]


def attention_phase(nc, r, d, layer, nb=B):
    binary = layer == 0
    tag = f"at{layer}"
    with ExitStack() as es:
        sb = lambda n, s, t=F32: es.enter_context(nc.sbuf_tensor(f"{tag}_{n}", s, t))
        sem = lambda n: new_semaphore(nc, r, f"{tag}_{n}")
        norm = Norm(nc, es, tag, r)
        xh, xl = sb("xh", [P, NC, T], F16), sb("xl", [P, NC, T], F16)
        qk32 = sb("qk32", [P, 4, T])
        qkh, qkl = sb("qkh", [P, 4, T], F16), sb("qkl", [P, 4, T], F16)
        qs = sb("qs", [P, 2, NP_, T], F16)
        ks = sb("ks", [P, 2, H, T], F16)
        vaug = sb("vaug", [P, 2, NJ, H, 32])
        mx = sb("mx", [P, NJ, H])
        mh, ml = sb("mh", [H, T], F16), sb("ml", [H, T], F16)
        pexp = sb("pexp", [P, 2, 4, 2 * BANK])
        ot = sb("ot", [P, 4, T])
        rec = sb("rec", [P, NJ, H])
        y, y32 = sb("y", [P, NJ, D]), sb("y32", [P, NC, T])
        yh, yl = sb("yh", [P, NC, T], F16), sb("yl", [P, NC, T], F16)
        nrow, krow = (y[0:2, i, :].bitcast(F16) for i in range(2))
        bias_out = sb("bias_out", [P, D])
        bqk = sb("bqk", [P, 4, 1])
        if binary:
            stage = pexp[:, 0].rearrange("p a (c n) -> p a c n", c=2)[:, :, :, 0:D]
            wabs = pexp[:, 1].rearrange("p a (c n) -> p a c n", c=2)[:, :, :, 0:D]
            wsign = sb("wsign", [P, 4, NC, D], F16)
            bv = sb("bv", [P, NC, 1])
            alpha = sb("alpha", [P, 6, 1])
            alpha_out = sb("alpha_out", [P, D])
            res = y32[:, 0, :]
        else:
            bv_row = sb("bv_row", [P, D])
            masks = [sb(f"mask{i}", [P, LW], BF16) for i in range(6)]
        scratch = nc.dram_tensor(f"{tag}_scratch", (2, P, 4, T), F16, kind="Internal").ap()
        zrows = nc.dram_tensor(f"{tag}_zrows", (2, NP_, T), F16, kind="Internal").ap()

        w_in, consts, mask_zero, masks_ready, w_abs, alpha_done, alpha_ready = (
            sem(n) for n in ("w_in", "consts", "mask_zero", "masks_ready", "w_abs", "alpha_done", "alpha_ready"))
        zeroed, ones_in, step, xt_done, xh_ready, xl_ready = (sem(n) for n in ("zeroed", "ones_in", "step", "xt_done", "xh_ready", "xl_ready"))
        proj_done, projv_done, qk_ready, qkl_ready, v_ready = (sem(n) for n in ("proj_done", "projv_done", "qk_ready", "qkl_ready", "v_ready"))
        saved, stacked, mxs_ready, mx_read, mt_done = (sem(n) for n in ("saved", "stacked", "mxs_ready", "mx_read", "mt_done"))
        mh_ready, ml_ready, rows_in, st_ready, exp_done = (sem(n) for n in ("mh_ready", "ml_ready", "rows_in", "st_ready", "exp_done"))
        av_done, ot_ready, ott_done, y_ready, yt_done = (sem(n) for n in ("av_done", "ot_ready", "ott_done", "y_ready", "yt_done"))
        yh_ready, yl_ready, out_done, out_read = (sem(n) for n in ("yh_ready", "yl_ready", "out_done", "out_read"))

        NG = 4
        if binary:
            max_slots = [s for h in range(H) for s in full_max(h)]
            units = [(g, [full_main(h, half) for h in range(4 * g, 4 * g + 4)]) for g in range(4) for half in range(2)]
        else:
            max_slots = [s for h in range(H) for s in (causal_max(h, masks[0]) if h < NG else local_max(h, masks[1], masks[2]))]
            units = [(0, [causal_main(h, half, masks[3]) for h in range(NG)]) for half in range(2)] + \
                [(g, [local_main(h, masks[4], masks[5]) for h in range(4 * g, 4 * g + 4)]) for g in range(1, 4)]
        main_slots = [slot for _, slots in units for slot in slots]
        NMAX, NMAIN, NU = len(max_slots), len(main_slots), len(units)
        first_unit = [min(u for u in range(NU) if units[u][0] == g) for g in range(4)]
        last_unit = [max(u for u in range(NU) if units[u][0] == g) for g in range(4)]
        MX, ST, O, TAIL = (0, 1), (2, 4), 6, 7

        MAX_FROM = 5
        share = NMAIN - MAX_FROM

        def max_part(k):
            if k < MAX_FROM:
                return range(0)
            return range((k - MAX_FROM) * NMAX // share, (k + 1 - MAX_FROM) * NMAX // share)
        if binary:
            STATS_AT, NORM_AT, YT_AT, OUT_AT, XT_AT, QK_AT = 4, 9, (6, 8), (12, 16), (20, 21), (24, 27, 30)
        else:
            STATS_AT, NORM_AT, YT_AT, OUT_AT, XT_AT, QK_AT = 2, 5, (4, 6), (8, 10), (11, 12), (13, 15, 17)
        CONST = 5
        READS = 4 if binary else 2

        block = es.enter_context(nc.Block())

        def turns(eng, turn):
            turn(0, 0, False, True, True)
            turn(1, 1, True, True, True)
            with eng.Fori(1, nb // 2 - 1) as k:
                turn(2 * k, 0, True, True, True)
                turn(2 * k + 1, 1, True, True, True)
            turn(nb - 2, 0, True, True, False)
            turn(nb - 1, 1, True, False, False)

        def heads_of(part):
            return part.rearrange("(i d) t -> d i t", d=DH)

        @block.sync
        def _(sp):
            def const(dst, src):
                sp.dma_start(dst, src, allow_slow_non_contiguous=True).then_inc(w_in, 16)
            if binary:
                for a in range(4):
                    const(stage[:, a], d["w0"][:, a * D:(a + 1) * D].rearrange("(c p) n -> p c n", p=P))
                const(bv[:], d["a0_bv"].rearrange("(c p) -> p c", p=P).unsqueeze(2))
                const(bqk[:, 0:2], d["a0_bq"].rearrange("(c p) -> p c", p=P).unsqueeze(2))
                const(bqk[:, 2:4], d["a0_bk"].rearrange("(c p) -> p c", p=P).unsqueeze(2))
                const(bias_out[:], d["a0_bp"].partition_broadcast(P))
            else:
                const(bqk[:], d["a1_bqkv"][0:2 * D].rearrange("(c p) -> p c", p=P).unsqueeze(2))
                const(bv_row[:], d["a1_bqkv"][2 * D:3 * D].partition_broadcast(P))
                const(bias_out[:], d["a1_bout"].partition_broadcast(P))
            sp.wait_ge(consts, 2)
            sp.dma_start(zrows, nrow[:].unsqueeze(1).broadcast_to([2, NP_, T])).then_inc(stacked, 16)
            sp.wait_ge(zeroed, 3)
            for par in range(2):
                for p in range(2):
                    sp.dma_start(ks[64 * par + 48:64 * par + 50, p, par * NP_:(par + 1) * NP_, :],
                                 krow[:].unsqueeze(1).broadcast_to([2, NP_, T])).then_inc(stacked, 16)
            sp.wait_ge(stacked, 16 * CONST)

            def save(b):
                sp.wait_ge(qk_ready, 4 * (b + 1))
                sp.dma_start(scratch[0], qkh[:]).then_inc(saved, 16)
                sp.wait_ge(qkl_ready, 4 * (b + 1))
                sp.dma_start(scratch[1], qkl[:]).then_inc(saved, 16)

            def stack(b, p):
                for par in range(2):
                    sp.dma_start(qs[64 * par + 48:64 * par + 50, p], zrows).then_inc(stacked, 16)
                sp.wait_ge(saved, 32 * (b + 1))
                for par in range(2):
                    for rep, (qpart, kpart) in enumerate(((0, 0), (0, 1), (1, 0))):
                        rows = slice(64 * par + 16 * rep, 64 * par + 16 * rep + 16)
                        sp.dma_start(qs[rows, p], heads_of(scratch[qpart][:, par, :])).then_inc(stacked, 16)
                        sp.dma_start(ks[rows, p, par * NP_:(par + 1) * NP_, :], heads_of(scratch[kpart][:, 2 + par, :])).then_inc(stacked, 16)

            def rows(b, p):
                sp.wait_ge(ml_ready, b + 1)
                for par in range(2):
                    for row, m in ((48, mh), (49, ml)):
                        sp.dma_start(qs[64 * par + row:64 * par + row + 1, p], m[par * NP_:(par + 1) * NP_, :]).then_inc(rows_in, 16)

            def turn(b, p, before, after, after2):
                if after:
                    rows(b + 1, 1 - p)
                if after2:
                    save(b + 2)
                    sp.wait_ge(st_ready, (b + 1) * NMAIN)
                    stack(b + 2, p)
            save(0)
            stack(0, 0)
            rows(0, 0)
            save(1)
            stack(1, 1)
            turns(sp, turn)

        @block.gpsimd
        def _(pool):
            pool.memset(krow[:], MS).then_inc(consts, 1)
            pool.memset(nrow[:], 0.0).then_inc(consts, 1)
            norm.pool_start(pool)
            norm.pool(pool, 0)
            if not binary:
                for m in masks:
                    pool.memset(m[:], 0.0).then_inc(mask_zero, 1)
                pool.wait_ge(mask_zero, 6)

                def keep(m, base, column, row):
                    return pool.affine_select(out=m[:], in_=m[:], compare_op=ALU.is_ge, fill=NEG, base=base,
                                              pattern=[[column, LW]], channel_multiplier=row)
                keep(masks[0], 0, -1, 1).then_inc(masks_ready, 1)
                keep(masks[1], WIN, -1, 1).then_inc(masks_ready, 1)
                keep(masks[2], 0, -1, 1).then_inc(masks_ready, 1)
                keep(masks[3], 0, 1, -1).then_inc(masks_ready, 1)
                keep(masks[4], 0, 1, -1).then_inc(masks_ready, 1)
                keep(masks[5], -WIN, 1, -1).then_inc(masks_ready, 1)
                pool.wait_ge(masks_ready, 6)
                keep(masks[1], 0, 1, -1).then_inc(masks_ready, 1)
                keep(masks[2], WIN, 1, -1).then_inc(masks_ready, 1)
                keep(masks[4], WIN, -1, 1).then_inc(masks_ready, 1)
                keep(masks[5], 2 * WIN, -1, 1).then_inc(masks_ready, 1)

            def low_qk(b, first):
                for m in range(4):
                    pool.wait_ge(qk_ready, b * 4 + m + 1)
                    if not first and m == 0:
                        pool.wait_ge(saved, 32 * b)
                    pool.tensor_tensor(qkl[:, m, :], qk32[:, m, :], qkh[:, m, :], ALU.subtract).then_inc(qkl_ready, 1)

            def low_y(b, first):
                for c in range(NC):
                    pool.wait_ge(yh_ready, b * 2 + c + 1)
                    if not first:
                        pool.wait_ge(out_done, 2 * b)
                    pool.tensor_tensor(yl[:, c, :], y32[:, c, :], yh[:, c, :], ALU.subtract).then_inc(yl_ready, 1)

            def turn(b, p, before, after, after2):
                if after2:
                    norm.pool(pool, b + 2)
                if before:
                    low_y(b - 1, isinstance(b, int) and b == 1)
                if after2:
                    low_qk(b + 2, False)
            pool.memset(qs[:], 0.0).then_inc(zeroed, 1)
            pool.memset(ks[:, 1], 0.0).then_inc(zeroed, 1)
            low_qk(0, True)
            norm.pool(pool, 1)
            low_qk(1, False)
            turns(pool, turn)
            low_y(nb - 1, False)

        @block.scalar
        def _(act):
            act.wait_ge(w_in, 16 * (8 if binary else 3))
            if binary:
                act.activation(wsign[:], stage, ACT.Sign).then_inc(w_abs, 1)
                act.activation(wabs, stage, ACT.Abs).then_inc(w_abs, 1)
                act.wait_ge(alpha_done, 1)
                act.activation(alpha[:].rearrange("p a b -> p (a b)"), banks(r, 0)[:, 0:6], ACT.Copy, scale=1.0 / D).then_inc(alpha_ready, 1)
                act.activation(alpha_out[:], banks(r, 1)[:, 0:D], ACT.Copy, scale=1.0 / D).then_inc(alpha_ready, 1)
                act.wait_ge(alpha_ready, 2)

            def high_x(b, c, first=False):
                act.wait_ge(xt_done, b * 2 + c + 1)
                if not first:
                    act.wait_ge(projv_done, b)
                act.activation(xh[:, c, :], banks(r, TAIL), ACT.Copy).then_inc(xh_ready, 1)

            def queries_keys(b, m, first=False):
                act.wait_ge(proj_done, b * 4 + m + 1)
                if not first and m == 0:
                    act.wait_ge(saved, 32 * b)
                scale = alpha[:, m, :] if binary else 1.0 / WS
                act.activation(qk32[:, m, :], banks(r, TAIL), ACT.Identity, bias=bqk[:, m, :], scale=scale)
                act.activation(qkh[:, m, :], banks(r, TAIL), ACT.Identity, bias=bqk[:, m, :], scale=scale).then_inc(qk_ready, 1)

            def project(b, first):
                for c in range(NC):
                    high_x(b, c, first)
                for m in range(4):
                    queries_keys(b, m, first)

            def max_high(b, first):
                act.wait_ge(mt_done, b + 1)
                if not first:
                    act.wait_ge(rows_in, 64 * b)
                act.activation(mh[:], banks(r, MX[0])[0:H, :], ACT.Copy, scale=-1.0 / MS).then_inc(mh_ready, 1)

            def exps(b, p, k, started):
                act.wait_ge(st_ready, b * NMAIN + k + 1)
                u, hh = k // 4, k % 4
                if hh == 0 and (started or u >= 2):
                    act.wait_ge(av_done, b * NU + u - 1)
                for at, n, stride, width, _ in main_slots[k][2]:
                    last = act.activation(columns(pexp[:, (p * NU + u) % 2, hh], at, n, stride, width),
                                          columns(banks(r, ST[k % 2], 2), at, n, stride, width), ACT.Exp, scale=DH ** -0.5)
                last.then_inc(exp_done, 1)

            def keep_outputs(b, g, started):
                act.wait_ge(av_done, b * NU + last_unit[g] + 1)
                if started and g == 0:
                    act.wait_ge(ott_done, 4 * b)
                act.activation(ot[:, g, :], banks(r, O), ACT.Copy).then_inc(ot_ready, 1)

            def y_high(b, c, started):
                act.wait_ge(yt_done, b * 2 + c + 1)
                if started:
                    act.wait_ge(out_done, 2 * b)
                bias, scale = (bv[:, c, :], alpha[:, 4 + c, :]) if binary else (0.0, 1.0)
                act.activation(y32[:, c, :], banks(r, TAIL), ACT.Identity, bias=bias, scale=scale)
                act.activation(yh[:, c, :], banks(r, TAIL), ACT.Identity, bias=bias, scale=scale).then_inc(yh_ready, 1)

            def turn(b, p, before, after, after2):
                second = isinstance(b, int) and b == 1
                for k in range(NMAIN):
                    exps(b, p, k, before)
                    for g in range(4):
                        if k == 4 * last_unit[g] + 6:
                            keep_outputs(b, g, before)
                    if before and k in YT_AT:
                        y_high(b - 1, YT_AT.index(k), not second)
                    if after2 and k in XT_AT:
                        high_x(b + 2, XT_AT.index(k))
                    if after2 and k in QK_AT:
                        queries_keys(b + 2, QK_AT.index(k))
                for g in range(4):
                    if 4 * last_unit[g] + 6 >= NMAIN:
                        keep_outputs(b, g, before)
                if after:
                    max_high(b + 1, False)
                if after2:
                    queries_keys(b + 2, 3)
            project(0, True)
            project(1, False)
            max_high(0, True)
            turns(act, turn)
            for c in range(NC):
                y_high(nb - 1, c, True)

        @block.vector
        def _(ve):
            def low_x(b, c):
                ve.wait_ge(xh_ready, b * 2 + c + 1)
                ve.tensor_tensor(xl[:, c, :], banks(r, TAIL), xh[:, c, :], ALU.subtract).then_inc(xl_ready, 1)

            def values(b, p, started):
                ve.wait_ge(projv_done, b + 1)
                if started:
                    ve.wait_ge(av_done, (b - 1) * NU)
                v_ps = banks(r, MX[0], 2)
                if binary:
                    ve.tensor_copy(vaug[:, p].rearrange("p s h e -> p (s h) e")[:, :, 0:DH], v_ps.rearrange("p (n e) -> p n e", e=DH)).then_inc(v_ready, 1)
                else:
                    for s in range(NJ):
                        last = ve.scalar_tensor_tensor(out=vaug[:, p, s, :, 0:DH], in0=v_ps[:, s * D:(s + 1) * D].rearrange("p (h e) -> p h e", e=DH),
                                                       scalar=1.0 / WS, in1=bv_row[:].rearrange("p (h e) -> p h e", e=DH), op0=ALU.mult, op1=ALU.add)
                    last.then_inc(v_ready, 1)

            def maximum(b, k, first):
                h, _, reads = max_slots[k]
                ve.wait_ge(mxs_ready, b * NMAX + k + 1)
                if k == 0 and not first:
                    ve.wait_ge(mt_done, b)
                for at, n, stride, width, j in reads:
                    last = ve.reduce_max(mx[:, j:j + n, h], columns(banks(r, MX[k % 2]), at, n, stride, width), AX.X)
                last.then_inc(mx_read, 1)

            def max_low(b):
                ve.wait_ge(mh_ready, b + 1)
                ve.scalar_tensor_tensor(out=ml[:], in0=banks(r, MX[0])[0:H, :], scalar=-1.0 / MS, in1=mh[:], op0=ALU.mult, op1=ALU.subtract).then_inc(ml_ready, 1)

            def divide(b, j, started):
                ve.wait_ge(ott_done, b * NJ + j + 1)
                o = banks(r, TAIL).rearrange("p (h e) -> p h e", e=32)
                ve.reciprocal(rec[:, j, :], o[:, :, DH]).then_inc(step, 1)
                ve.wait_ge(step, b * NJ + j + 1)
                if started and j == 0:
                    ve.wait_ge(yt_done, 2 * b)
                ve.tensor_tensor(y[:, j, :].rearrange("p (h e) -> p h e", e=DH), o[:, :, 0:DH],
                                 rec[:, j, :].unsqueeze(2).broadcast_to([P, H, DH]), ALU.mult).then_inc(y_ready, 1)

            def residual(b, half):
                ve.wait_ge(out_done, 2 * b + half + 1)
                x = r.X[:, bass.ds(b * BT + half * 2 * D, 2 * D)]
                xj = x.rearrange("p (j n) -> p j n", n=D)
                if binary:
                    ve.tensor_tensor(res.rearrange("p (j n) -> p j n", n=D), banks(r, TAIL).rearrange("p (j n) -> p j n", n=D),
                                     alpha_out[:].unsqueeze(1).broadcast_to([P, 2, D]), ALU.mult).then_inc(out_read, 1)
                    ve.wait_ge(out_read, 4 * b + 2 * half + 1)
                    ve.tensor_tensor(x, x, res, ALU.add).then_inc(out_read, 1)
                    ve.wait_ge(out_read, 4 * b + 2 * half + 2)
                else:
                    ve.scalar_tensor_tensor(out=x, in0=banks(r, TAIL), scalar=1.0 / WS, in1=x, op0=ALU.mult, op1=ALU.add).then_inc(out_read, 1)
                    ve.wait_ge(out_read, 2 * b + half + 1)
                ve.tensor_tensor(xj, xj, bias_out[:].unsqueeze(1).broadcast_to([P, 2, D]), ALU.add)

            def turn(b, p, before, after, after2):
                second = isinstance(b, int) and b == 1
                if after:
                    values(b + 1, 1 - p, before)
                for k in range(NMAIN):
                    if before and k < NJ:
                        divide(b - 1, k, not second)
                    if after2 and k == STATS_AT:
                        norm.statistics(ve, r, b + 2)
                    if after2 and k == NORM_AT:
                        norm.apply(ve, r, b + 2, lambda: ve.wait_ge(xt_done, 2 * (b + 2)))
                    if after2 and k in XT_AT:
                        low_x(b + 2, XT_AT.index(k))
                    if before and k in OUT_AT:
                        residual(b - 1, OUT_AT.index(k))
                    if after:
                        for i in max_part(k):
                            maximum(b + 1, i, False)
                if after:
                    max_low(b + 1)
            norm.vector(ve, r, 0)
            for c in range(NC):
                low_x(0, c)
            ve.memset(ks[:, 0], 0.0).then_inc(zeroed, 1)
            ve.memset(vaug[:], 0.0).then_inc(ones_in, 1)
            ve.wait_ge(ones_in, 1)
            ve.memset(vaug[:].rearrange("p a s h e -> p (a s h) e")[:, :, DH:DH + 1], 1.0).then_inc(ones_in, 1)
            ve.wait_ge(ones_in, 2)
            ve.wait_ge(w_in, 16 * (8 if binary else 3))
            if binary:
                ve.wait_ge(alpha_ready, 2)
            values(0, 0, False)
            norm.vector(ve, r, 1, lambda: ve.wait_ge(xt_done, 2))
            for c in range(NC):
                low_x(1, c)
            for k in range(NMAX):
                maximum(0, k, True)
            max_low(0)
            turns(ve, turn)
            for j in range(NJ):
                divide(nb - 1, j, True)
            for half in range(2):
                residual(nb - 1, half)

        @block.tensor
        def _(pe):
            if binary:
                pe.wait_ge(w_abs, 2)
                for a in range(6):
                    for c in range(NC):
                        nc.tensor.matmul(banks(r, 0)[:, a:a + 1], wabs[:, a // 2, c, (a % 2) * P:(a % 2 + 1) * P], r.ones[:, 0:1],
                                         start=(c == 0), stop=(c == NC - 1))
                for c in range(NC):
                    last = nc.tensor.matmul(banks(r, 1)[:, 0:D], r.ones[:], wabs[:, 3, c, :], start=(c == 0), stop=(c == NC - 1))
                last.then_inc(alpha_done, 1)
                pe.wait_ge(alpha_ready, 2)

            def weights(name, m0, m1, hi, lo):
                if binary:
                    a = "qkvo".index(name)
                    return [(wsign[:, a, c, m0:m1], c, part) for c in range(NC) for part in (hi, lo)]
                at = COL[f"a1{name}"]
                return [(w[:, c, at + m0:at + m1], c, part) for c in range(NC) for w, part in ((r.wh, hi), (r.wh, lo), (r.wl, hi))]

            def transpose_x(b, c, started):
                if c == 0:
                    pe.wait_ge(norm.xn_ready, b + 1)
                    if started:
                        pe.wait_ge(out_read, READS * (b - 2))
                    elif isinstance(b, int) and b == 1:
                        pe.wait_ge(qk_ready, 4)
                else:
                    pe.wait_ge(xl_ready, b * 2 + 1)
                for j in range(NJ):
                    last = nc.tensor.transpose(banks(r, TAIL)[:, j * P:(j + 1) * P], norm.xn[:, j, c * P:(c + 1) * P], r.ident[:])
                last.then_inc(xt_done, 1)

            def queries_keys(b, m):
                if m == 0:
                    pe.wait_ge(xl_ready, 2 * (b + 1))
                else:
                    pe.wait_ge(qk_ready, b * 4 + m)
                product(nc, banks(r, TAIL), [(w, part[:, c, :]) for w, c, part in weights("qk"[m // 2], (m % 2) * P, (m % 2 + 1) * P, xh, xl)]).then_inc(proj_done, 1)

            def project(b):
                for c in range(NC):
                    transpose_x(b, c, False)
                for m in range(4):
                    queries_keys(b, m)

            def project_values(b):
                for s in range(NJ):
                    last = product(nc, banks(r, MX[0], 2)[:, s * D:(s + 1) * D],
                                   [(part[:, c, s * P:(s + 1) * P], w) for w, c, part in weights("v", 0, D, xh, xl)])
                last.then_inc(projv_done, 1)

            def masked(out, lhs, rhs, piece):
                last = nc.tensor.matmul(out, lhs, rhs, start=True, stop=True)
                if piece.mask is not None:
                    last = nc.tensor.matmul(out[:, piece.mask_at:piece.mask_at + piece.mask_n], r.identb[:], piece.mask[:, 0:piece.mask_n],
                                            start=False, stop=True, skip_group_check=True)
                return last

            def maximum(b, p, k):
                h, pieces, _ = max_slots[k]
                if k == 0:
                    pe.wait_ge(stacked, 16 * (14 * (b + 1) + CONST))
                    pe.wait_ge(v_ready, b + 1)
                if k >= 2:
                    pe.wait_ge(mx_read, b * NMAX + k - 1)
                for piece in pieces:
                    last = masked(banks(r, MX[k % 2])[:, piece.at:piece.at + piece.n], qs[:, p, h % NP_, piece.idx * P:(piece.idx + 1) * P],
                                  ks[:, p, h, piece.lo:piece.lo + piece.n], piece)
                last.then_inc(mxs_ready, 1)

            def transpose_max(b):
                pe.wait_ge(mx_read, (b + 1) * NMAX)
                for j in range(NJ):
                    last = nc.tensor.transpose(banks(r, MX[0])[0:H, j * P:(j + 1) * P], mx[:, j, :], r.ident[:])
                last.then_inc(mt_done, 1)

            def scores(b, p, k, started):
                h, pieces, _ = main_slots[k]
                if k == 0:
                    pe.wait_ge(rows_in, 64 * (b + 1))
                if started or k >= 2:
                    pe.wait_ge(exp_done, b * NMAIN + k - 1)
                for piece in pieces:
                    last = masked(banks(r, ST[k % 2], 2)[:, piece.at:piece.at + piece.n], ks[:, p, h, piece.idx * P:(piece.idx + 1) * P],
                                  qs[:, p, h % NP_, piece.lo:piece.lo + piece.n], piece)
                last.then_inc(st_ready, 1)

            def weigh(b, p, u, started):
                g, slots = units[u]
                pe.wait_ge(exp_done, b * NMAIN + 4 * (u + 1))
                if u == first_unit[g] and (started or g):
                    pe.wait_ge(ot_ready, b * 4 + g)
                for n in range(len(slots[0][1])):
                    for hh, (h, pieces, _) in enumerate(slots):
                        piece = pieces[n]
                        last = nc.tensor.matmul(banks(r, O)[32 * hh:32 * hh + 32, piece.lo:piece.lo + piece.n], vaug[:, p, piece.idx, h, :],
                                                pexp[:, (p * NU + u) % 2, hh, piece.at:piece.at + piece.n],
                                                start=(u == first_unit[g] and n == 0), stop=True, skip_group_check=True)
                last.then_inc(av_done, 1)

            def transpose_outputs(b, j, started, projected=False):
                if j == 0:
                    pe.wait_ge(ot_ready, 4 * (b + 1))
                    if projected:
                        pe.wait_ge(qk_ready, 4 * (b + 3))
                    elif started:
                        pe.wait_ge(out_read, READS * b)
                else:
                    pe.wait_ge(y_ready, b * NJ + j)
                for g in range(4):
                    last = nc.tensor.transpose(banks(r, TAIL)[:, g * P:(g + 1) * P], ot[:, g, j * P:(j + 1) * P], r.ident[:])
                last.then_inc(ott_done, 1)

            def transpose_y(b, c):
                pe.wait_ge(y_ready, NJ * (b + 1))
                if c:
                    pe.wait_ge(yh_ready, 2 * b + 1)
                for j in range(NJ):
                    last = nc.tensor.transpose(banks(r, TAIL)[:, j * P:(j + 1) * P], y[:, j, c * P:(c + 1) * P], r.ident[:])
                last.then_inc(yt_done, 1)

            def output(b, half):
                pe.wait_ge(yl_ready, 2 * (b + 1))
                if half:
                    pe.wait_ge(out_read, READS * b + READS // 2)
                for j in range(2):
                    t = slice((2 * half + j) * P, (2 * half + j + 1) * P)
                    last = product(nc, banks(r, TAIL)[:, j * D:(j + 1) * D], [(part[:, c, t], w) for w, c, part in weights("o", 0, D, yh, yl)])
                last.then_inc(out_done, 1)

            def turn(b, p, before, after, after2):
                second = isinstance(b, int) and b == 1
                if after:
                    pe.wait_ge(ml_ready, b + 1)
                    project_values(b + 1)
                for k in range(NMAIN):
                    scores(b, p, k, before)
                    if k >= 5 and (k - 5) % 4 == 0:
                        weigh(b, p, (k - 5) // 4, before)
                    if before and k < NJ:
                        transpose_outputs(b - 1, k, not second, after)
                    if before and k in YT_AT:
                        transpose_y(b - 1, YT_AT.index(k))
                    if before and k in OUT_AT:
                        output(b - 1, OUT_AT.index(k))
                    if after2 and k in XT_AT:
                        transpose_x(b + 2, XT_AT.index(k), before)
                    if after2 and k in QK_AT:
                        queries_keys(b + 2, QK_AT.index(k))
                    if after:
                        for i in max_part(k):
                            maximum(b + 1, 1 - p, i)
                weigh(b, p, NU - 1, before)
                if after:
                    transpose_max(b + 1)
                if after2:
                    queries_keys(b + 2, 3)
            project(0)
            project_values(0)
            project(1)
            if not binary:
                pe.wait_ge(masks_ready, 10)
            for k in range(NMAX):
                maximum(0, 0, k)
            transpose_max(0)
            turns(pe, turn)
            for j in range(NJ):
                transpose_outputs(nb - 1, j, True)
            for c in range(NC):
                transpose_y(nb - 1, c)
            for half in range(2):
                output(nb - 1, half)


def layout(inp):
    import numpy as np
    f = {k: np.asarray(v) for k, v in inp.items()}
    tr = lambda a: np.ascontiguousarray(np.swapaxes(a, -1, -2))
    a = {"x": f["x"], "ctxT": np.ascontiguousarray(f["ctx_1024"].reshape(B * SKV, D).T)}
    a["w0"] = np.concatenate([tr(f[f"L0_attn_W{n}"]) for n in "qkvp"], axis=1)
    a["wlin"] = np.concatenate([tr(f[f"L0_xattn_W{n}"]) for n in "qkvo"] + [f["L1_attn_w_qkv"], f["L1_attn_w_out"]]
                               + [f[f"L1_xattn_W{n}"] for n in "qkvo"], axis=1)
    for n in "qkvp":
        a[f"a0_b{n}"] = f[f"L0_attn_b{n}"]
    a["a1_bqkv"], a["a1_bout"] = f["L1_attn_b_qkv"], f["L1_attn_b_out"]
    for n in "qkvo":
        a[f"x0_b{n}"], a[f"x1_b{n}"] = f[f"L0_xattn_b{n}"], f[f"L1_xattn_b{n}"]
    a["f_gate"], a["f_up"], a["f_down"] = tr(f["L0_ffn_w_gate"]), tr(f["L0_ffn_w_up"]), tr(f["L0_ffn_w_down"])
    for n, s, w in (("gate", "sg_w", "wg"), ("up", "su_w", "wu"), ("down", "sd_w", "wd")):
        a[f"m_{n}"] = np.concatenate([tr(f[f"L1_ffn_{s}"])[None], tr(f[f"L1_ffn_{w}"])])
    a["m_router"], a["m_bias"] = tr(f["L1_ffn_router_w"]), f["L1_ffn_routing_bias"]
    return a


def build(nc, d, out):
    r = Core()
    r.semaphores = []
    with ExitStack() as es:
        tensors(nc, es, r)
        setup_phase(nc, r, d)
        end_phase(nc, r)
        attention_phase(nc, r, d, 0)
        end_phase(nc, r)
        with nc.sbuf_tensor("ff_stage", [P, 3, FF_WIDTH], F32) as stage:
            cross0_phase(nc, r, d, stage)
            end_phase(nc, r)
            quant_ffn_phase(nc, r, stage)
            end_phase(nc, r)
        attention_phase(nc, r, d, 1)
        end_phase(nc, r)
        cross1_phase(nc, r, d)
        end_phase(nc, r)
        experts_phase(nc, r, d, out)


def cross0_phase(nc, r, d, ff_stage, nb=B):
    tag = "x0"
    scale = float(D) ** -0.5
    with ExitStack() as es:
        sb = lambda n, s, t=F32: es.enter_context(nc.sbuf_tensor(f"{tag}_{n}", s, t))
        sem = lambda n: new_semaphore(nc, r, (f"{tag}_{n}"))
        norm = Norm(nc, es, tag, r)
        ctx32, ctxh, ctxl = sb("ctx32", [P, NC, B * SKV]), sb("ctxh", [P, NC, B * SKV], F16), sb("ctxl", [P, NC, B * SKV], F16)
        k32, kh, kl = sb("k32", [P, NC, B * SKV]), sb("kh", [P, NC, B * SKV], F16), sb("kl", [P, NC, B * SKV], F16)
        v_all, vcur = sb("v_all", [SKV, B * D]), sb("vcur", [SKV, D])
        x32, xh, xl = sb("x32", [P, NC, T]), sb("xh", [P, NC, T], F16), sb("xl", [P, NC, T], F16)
        q32, qh, ql = sb("q32", [P, NC, T]), sb("qh", [P, NC, T], F16), sb("ql", [P, NC, T], F16)
        mx, nm, total, rec = sb("mx", [P, NJ]), sb("nm", [P, NJ]), sb("total", [P, NJ]), sb("rec", [P, NJ])
        e, pr, pt = sb("e", [P, NJ, SKV]), sb("pr", [P, NJ, SKV]), sb("pt", [SKV, T])
        z32, zh, zl = sb("z32", [P, NC, T]), sb("zh", [P, NC, T], F16), sb("zl", [P, NC, T], F16)
        bq, bk = sb("bq", [P, NC, 1]), sb("bk", [P, NC, 1])
        bv_row, bias_out = sb("bv_row", [SKV, D]), sb("bias_out", [P, D])
        (w_in, ctxh_ready, ctxl_ready, kps_done, x32_ready, kh_ready, kl_ready, vps_done, v_ready) = (
            sem(n) for n in ("w_in", "ctxh_ready", "ctxl_ready", "kps_done", "x32_ready", "kh_ready", "kl_ready", "vps_done", "v_ready"))
        (xt_done, xh_ready, xl_ready, q_done, q_ready, ql_ready, s_done, nm_ready, e_ready, p_ready, pt_done, pt_ready) = (
            sem(n) for n in ("xt_done", "xh_ready", "xl_ready", "q_done", "q_ready", "ql_ready", "s_done", "nm_ready", "e_ready", "p_ready", "pt_done", "pt_ready"))
        (vcur_ready, att_done, z_ready, zh_ready, zl_ready, out_done, step) = (
            sem(n) for n in ("vcur_ready", "att_done", "z_ready", "zh_ready", "zl_ready", "out_done", "step"))
        ff_in = sem("ff_in")
        flat = lambda t: t[:].rearrange("p c t -> p (c t)")
        block = es.enter_context(nc.Block())

        def three(name, m0, m1, hi, lo):
            at = COL[f"x0{name}"]
            return [(w[:, c, at + m0:at + m1], c, part) for c in range(NC) for w, part in ((r.wh, hi), (r.wh, lo), (r.wl, hi))]

        @block.sync
        def _(sp):
            def const(dst, src):
                sp.dma_start(dst, src, allow_slow_non_contiguous=True).then_inc(w_in, 16)
            const(ctx32[:], d["ctxT"].rearrange("(c p) n -> p c n", p=P))
            const(bq[:], d["x0_bq"].rearrange("(c p) -> p c", p=P).unsqueeze(2))
            const(bk[:], d["x0_bk"].rearrange("(c p) -> p c", p=P).unsqueeze(2))
            const(bv_row[:], d["x0_bv"].partition_broadcast(SKV))
            const(bias_out[:], d["x0_bo"].partition_broadcast(P))
            for n, w in enumerate(("f_gate", "f_up", "f_down")):
                c = FF_WIDTH // d[w].shape[1]
                sp.dma_start(ff_stage[:, n, :].rearrange("p (c n) -> p c n", c=c), d[w].rearrange("(c p) n -> p c n", p=P)).then_inc(ff_in, 16)
            sp.wait_ge(ff_in, 48)

        @block.gpsimd
        def _(pool):
            norm.pool_start(pool)

            def low_q(b):
                pool.wait_ge(q_ready, b + 1)
                pool.tensor_tensor(ql[:], q32[:], qh[:], ALU.subtract).then_inc(ql_ready, 1)

            def turn(b, after):
                if after:
                    norm.pool(pool, b + 1)
                pool.wait_ge(zh_ready, b + 1)
                pool.tensor_tensor(zl[:], z32[:], zh[:], ALU.subtract).then_inc(zl_ready, 1)
                if after:
                    low_q(b + 1)
            norm.pool(pool, 0)
            low_q(0)
            with pool.Fori(0, nb - 1) as b:
                turn(b, True)
            turn(nb - 1, False)

        @block.scalar
        def _(act):
            act.wait_ge(w_in, 16 * 5)
            act.activation(ctxh[:], ctx32[:], ACT.Copy).then_inc(ctxh_ready, 1)
            act.wait_ge(kps_done, 1)
            for m in range(NC):
                act.activation(k32[:, m, :], banks(r, 2 + m), ACT.Identity, bias=bk[:, m, :], scale=1.0 / WS)
                last = act.activation(kh[:, m, :], banks(r, 2 + m), ACT.Identity, bias=bk[:, m, :], scale=1.0 / WS)
            last.then_inc(kh_ready, 1)

            def high_x(b):
                act.wait_ge(xt_done, b + 1)
                act.activation(flat(xh), banks(r, 0, 2), ACT.Copy).then_inc(xh_ready, 1)

            def queries(b):
                act.wait_ge(q_done, b + 1)
                for m in range(NC):
                    act.activation(q32[:, m, :], banks(r, 2 + m), ACT.Identity, bias=bq[:, m, :], scale=1.0 / WS)
                    last = act.activation(qh[:, m, :], banks(r, 2 + m), ACT.Identity, bias=bq[:, m, :], scale=1.0 / WS)
                last.then_inc(q_ready, 1)

            def turn(b, after):
                act.wait_ge(nm_ready, b + 1)
                for j in range(NJ):
                    last = act.activation(e[:, j, :], banks(r, 4)[:, j * SKV:(j + 1) * SKV], ACT.Exp, bias=nm[:, j:j + 1],
                                          scale=scale, accum_out=total[:, j:j + 1])
                last.then_inc(e_ready, 1)
                if after:
                    high_x(b + 1)
                act.wait_ge(pt_done, b + 1)
                act.activation(pt[:], banks(r, 5)[0:SKV, :], ACT.Copy).then_inc(pt_ready, 1)
                act.wait_ge(z_ready, b + 1)
                act.activation(zh[:], z32[:], ACT.Copy).then_inc(zh_ready, 1)
                if after:
                    act.activation(flat(x32), banks(r, 0, 2), ACT.Copy).then_inc(x32_ready, 1)
                    queries(b + 1)
            high_x(0)
            act.wait_ge(xl_ready, 1)
            act.activation(flat(x32), banks(r, 0, 2), ACT.Copy).then_inc(x32_ready, 1)
            queries(0)
            with act.Fori(0, nb - 1) as b:
                turn(b, True)
            turn(nb - 1, False)

        @block.vector
        def _(ve):
            ve.wait_ge(ctxh_ready, 1)
            ve.tensor_tensor(ctxl[:], ctx32[:], ctxh[:], ALU.subtract).then_inc(ctxl_ready, 1)
            ve.wait_ge(kh_ready, 1)
            ve.tensor_tensor(kl[:], k32[:], kh[:], ALU.subtract).then_inc(kl_ready, 1)
            ve.wait_ge(vps_done, 1)
            for s in range(B):
                last = ve.scalar_tensor_tensor(out=v_all[:, s * D:(s + 1) * D], in0=banks(r, 4, 4)[0:SKV, s * D:(s + 1) * D], scalar=1.0 / WS,
                                               in1=bv_row[:], op0=ALU.mult, op1=ALU.add)
            last.then_inc(v_ready, 1)
            ve.wait_ge(v_ready, 1)

            def low_x(b):
                ve.wait_ge(xh_ready, b + 1)
                ve.tensor_tensor(flat(xl), banks(r, 0, 2), flat(xh), ALU.subtract).then_inc(xl_ready, 1)

            def turn(b, after, after2):
                steps = Count(3)
                ve.tensor_scalar(vcur[:], v_all[:, bass.ds(b * D, D)], 1.0, None, ALU.mult).then_inc(vcur_ready, 1)
                ve.wait_ge(s_done, b + 1)
                ve.reduce_max(mx[:], banks(r, 4)[:, 0:NJ * SKV].rearrange("p (j s) -> p j s", s=SKV), AX.X).then_inc(step, 1)
                steps.up()
                ve.wait_ge(step, steps.at(b))
                ve.tensor_scalar(nm[:], mx[:], -scale, None, ALU.mult).then_inc(nm_ready, 1)
                if after:
                    norm.apply(ve, r, b + 1)
                ve.wait_ge(e_ready, b + 1)
                ve.reciprocal(rec[:], total[:]).then_inc(step, 1)
                steps.up()
                ve.wait_ge(step, steps.at(b))
                ve.tensor_tensor(pr[:], e[:], rec[:].unsqueeze(2).broadcast_to([P, NJ, SKV]), ALU.mult).then_inc(p_ready, 1)
                if after:
                    low_x(b + 1)
                ve.wait_ge(att_done, b + 1)
                ve.wait_ge(x32_ready, b + 1)
                ve.tensor_tensor(flat(z32), banks(r, 6, 2), flat(x32), ALU.add).then_inc(z_ready, 1)
                if after2:
                    norm.statistics(ve, r, b + 2)
                ve.wait_ge(out_done, b + 1)
                x = r.X[:, bass.ds(b * BT, BT)]
                ve.scalar_tensor_tensor(out=x, in0=banks(r, 6, 2), scalar=1.0 / WS, in1=x, op0=ALU.mult, op1=ALU.add).then_inc(step, 1)
                steps.up()
                ve.wait_ge(step, steps.at(b))
                xj = x.rearrange("p (j n) -> p j n", n=D)
                ve.tensor_tensor(xj, xj, bias_out[:].unsqueeze(1).broadcast_to([P, NJ, D]), ALU.add)
                steps.done()
            norm.vector(ve, r, 0)
            low_x(0)
            norm.statistics(ve, r, 1)
            with ve.Fori(0, nb - 2) as b:
                turn(b, True, True)
            turn(nb - 2, True, False)
            turn(nb - 1, False, False)

        @block.tensor
        def _(pe):
            pe.wait_ge(ctxh_ready, 1)
            pe.wait_ge(ctxl_ready, 1)
            for m in range(NC):
                last = product(nc, banks(r, 2 + m), [(w, part[:, c, :]) for w, c, part in three("k", m * P, (m + 1) * P, ctxh, ctxl)])
            last.then_inc(kps_done, 1)
            for s in range(B):
                last = product(nc, banks(r, 4, 4)[0:SKV, s * D:(s + 1) * D],
                               [(part[:, c, s * SKV:(s + 1) * SKV], w) for w, c, part in three("v", 0, D, ctxh, ctxl)])
            last.then_inc(vps_done, 1)
            pe.wait_ge(kl_ready, 1)
            pe.wait_ge(v_ready, 1)

            def transpose_x(b):
                pe.wait_ge(norm.xn_ready, b + 1)
                transpose_tiles(nc, r, norm.xn, 0).then_inc(xt_done, 1)

            def queries(b):
                pe.wait_ge(xl_ready, b + 1)
                for m in range(NC):
                    last = product(nc, banks(r, 2 + m), [(w, part[:, c, :]) for w, c, part in three("q", m * P, (m + 1) * P, xh, xl)])
                last.then_inc(q_done, 1)

            def scores(b):
                pe.wait_ge(ql_ready, b + 1)
                for j in range(NJ):
                    t = slice(j * P, (j + 1) * P)
                    last = product(nc, banks(r, 4)[:, j * SKV:(j + 1) * SKV],
                                   [(a[:, c, t], k[:, c, bass.ds(b * SKV, SKV)]) for c in range(NC) for a, k in ((qh, kh), (qh, kl), (ql, kh))])
                last.then_inc(s_done, 1)

            def turn(b, after):
                if after:
                    pe.wait_ge(x32_ready, b + 1)
                    transpose_x(b + 1)
                pe.wait_ge(p_ready, b + 1)
                nc.tensor.matmul(banks(r, 5)[:, 0:1], r.ident[:], r.ones[:, 0:1], start=True, stop=True)
                for j in range(NJ):
                    last = nc.tensor.transpose(banks(r, 5)[0:SKV, j * P:(j + 1) * P], pr[:, j, :], r.ident[:])
                last.then_inc(pt_done, 1)
                if after:
                    queries(b + 1)
                pe.wait_ge(pt_ready, b + 1)
                pe.wait_ge(vcur_ready, b + 1)
                for m in range(NC):
                    last = nc.tensor.matmul(banks(r, 6 + m), vcur[:, m * P:(m + 1) * P], pt[:], start=True, stop=True)
                last.then_inc(att_done, 1)
                pe.wait_ge(zl_ready, b + 1)
                for j in range(NJ):
                    last = product(nc, banks(r, 6, 2)[:, j * D:(j + 1) * D],
                                   [(part[:, c, j * P:(j + 1) * P], w) for w, c, part in three("o", 0, D, zh, zl)])
                last.then_inc(out_done, 1)
                if after:
                    scores(b + 1)
            transpose_x(0)
            queries(0)
            scores(0)
            with pe.Fori(0, nb - 1) as b:
                turn(b, True)
            turn(nb - 1, False)


def quant_ffn_phase(nc, r, stage, nb=B):
    tag = "ff"
    FI = 1024
    NI = FI // P
    with ExitStack() as es:
        sb = lambda n, s, t=F32: es.enter_context(nc.sbuf_tensor(f"{tag}_{n}", s, t))
        sem = lambda n: new_semaphore(nc, r, (f"{tag}_{n}"))
        norm = Norm(nc, es, tag, r)
        NW = NC * FI
        tmp = sb("tmp", [P, NW])
        wq = sb("wq", [P, 3, NW], BF16)
        rowsum, wmean, wrec = sb("rowsum", [P, 3]), sb("wmean", [P, 3]), sb("wrec", [P, 3])
        magic = sb("magic", [P, 1])
        amax, arec, ascale, aq = sb("amax", [P, NJ]), sb("arec", [P, NJ]), sb("ascale", [P, NJ]), sb("aq", [P, 2, 2, NJ])
        xr, xq, xqt = sb("xr", [P, NJ, D]), sb("xq", [P, NJ, D], BF16), sb("xqt", [P, NC, T], BF16)
        sg, h, hr, hq, ht = sb("sg", [P, 2, FI]), sb("h", [P, 2, FI]), sb("hr", [P, 2, FI]), sb("hq", [P, 2, FI], BF16), sb("ht", [P, 2, NI, P], BF16)
        hmax, hrec, hscale, hdq = sb("hmax", [P, NJ]), sb("hrec", [P, NJ]), sb("hscale", [P, NJ]), sb("hdq", [P, NJ])
        (magic_in, abs_ready, tot_done, mean_ready, step, xq_ready, xt_done, xqt_ready) = (
            sem(n) for n in ("magic_in", "abs_ready", "tot_done", "mean_ready", "step", "xq_ready", "xt_done", "xqt_ready"))
        (gate_done, up_done, sg_ready, h_ready, hscale_ready, hr_ready, hq_ready, htps_done, ht_ready, out_done, out_read) = (
            sem(n) for n in ("gate_done", "up_done", "sg_ready", "h_ready", "hscale_ready", "hr_ready", "hq_ready", "htps_done", "ht_ready", "out_done", "out_read"))
        token_step = sem("token_step")
        GATE, UP, DOWN, HT = 1, 3, 5, 7
        block = es.enter_context(nc.Block())

        @block.gpsimd
        def _(pool):
            pool.memset(magic[:], MAGIC).then_inc(magic_in, 1)
            norm.pool_start(pool)
            norm.pool(pool, 0)

            def turn(b, p, before, after):
                for j in range(NJ):
                    if after and j == 1:
                        norm.pool(pool, b + 1)
                    pool.wait_ge(hr_ready, b * NJ + j + 1)
                    pool.tensor_tensor(hq[:, j % 2, :], hr[:, j % 2, :], magic[:].broadcast_to([P, FI]), ALU.subtract).then_inc(hq_ready, 1)
            staggered(pool, nb, turn)

        @block.scalar
        def _(act):
            for n in range(3):
                last = act.activation(h[:].rearrange("p a b -> p (a b)"), stage[:, n, :], ACT.Abs, accum_out=rowsum[:, n:n + 1])
                last.then_inc(abs_ready, 1)
                act.wait_ge(abs_ready, n + 1)
            act.wait_ge(magic_in, 1)

            def keep_x(b):
                act.wait_ge(xt_done, b + 1)
                act.activation(xqt[:].rearrange("p c t -> p (c t)"), banks(r, 0).bitcast(BF16), ACT.Copy).then_inc(xqt_ready, 1)

            def squash(b, p, j):
                act.wait_ge(gate_done, b * NJ + j + 1)
                act.activation(sg[:, j % 2, :], banks(r, GATE, 2), ACT.Silu, scale=aq[:, p, 0, j:j + 1]).then_inc(sg_ready, 1)

            def turn(b, p, before, after):
                for j in range(NJ):
                    act.wait_ge(hscale_ready, b * NJ + j + 1)
                    act.activation(hr[:, j % 2, :], h[:, j % 2, :], ACT.Identity, bias=magic[:], scale=hscale[:, j:j + 1]).then_inc(hr_ready, 1)
                    if j < 2:
                        squash(b, p, j + 2)
                    elif after:
                        squash(b + 1, 1 - p, j - 2)
                    act.wait_ge(htps_done, b * NJ + j + 1)
                    act.activation(ht[:, j % 2].rearrange("p i t -> p (i t)"), banks(r, HT).bitcast(BF16), ACT.Copy).then_inc(ht_ready, 1)
                    if after and j == 1:
                        keep_x(b + 1)
            keep_x(0)
            squash(0, 0, 0)
            squash(0, 0, 1)
            staggered(act, nb, turn)

        @block.vector
        def _(ve):
            norm.statistics(ve, r, 0)
            ve.wait_ge(tot_done, 1)
            ve.tensor_scalar(wmean[:], banks(r, 0)[:, 0:3], 1.0 / (D * FI), 1e-5, ALU.mult, ALU.max).then_inc(mean_ready, 1)
            ve.wait_ge(mean_ready, 1)
            ve.reciprocal(wrec[:], wmean[:]).then_inc(mean_ready, 1)
            for n in range(3):
                ve.wait_ge(mean_ready, 2 + 3 * n)
                ve.tensor_scalar(tmp[:], stage[:, n, :], wrec[:, n:n + 1], MAGIC, ALU.mult, ALU.add).then_inc(mean_ready, 1)
                ve.wait_ge(mean_ready, 3 + 3 * n)
                ve.tensor_scalar(stage[:, n, :], tmp[:], MAGIC, -1.0, ALU.subtract, ALU.max).then_inc(mean_ready, 1)
                ve.wait_ge(mean_ready, 4 + 3 * n)
                ve.tensor_scalar(wq[:, n, :], stage[:, n, :], 1.0, None, ALU.min).then_inc(mean_ready, 1)
            ve.wait_ge(mean_ready, 11)

            def token_scales(b, p):
                norm.apply(ve, r, b)
                ve.wait_ge(norm.xn_ready, b + 1)
                ve.tensor_reduce(amax[:], norm.xn[:], AX.X, ALU.max, apply_absolute_value=True).then_inc(token_step, 1)
                ve.wait_ge(token_step, b * 6 + 1)
                ve.tensor_scalar(amax[:], amax[:], 1e-5, None, ALU.max).then_inc(token_step, 1)
                ve.wait_ge(token_step, b * 6 + 2)
                ve.reciprocal(arec[:], amax[:]).then_inc(token_step, 1)
                for n in range(2):
                    ve.tensor_scalar(aq[:, p, n, :], amax[:], 1.0 / 127.0, wmean[:, n:n + 1], ALU.mult, ALU.mult).then_inc(token_step, 1)
                ve.wait_ge(token_step, b * 6 + 5)
                ve.tensor_scalar(ascale[:], arec[:], 127.0, None, ALU.mult).then_inc(token_step, 1)

            def quantise_tokens(b):
                ve.wait_ge(token_step, b * 6 + 6)
                for j in range(NJ):
                    ve.tensor_scalar(xr[:, j, :], norm.xn[:, j, :], ascale[:, j:j + 1], MAGIC, ALU.mult, ALU.add).then_inc(xq_ready, 1)
                ve.wait_ge(xq_ready, b * 5 + 4)
                ve.tensor_scalar(xq[:], xr[:], MAGIC, None, ALU.subtract).then_inc(xq_ready, 1)

            def hidden(b, p, j):
                ve.wait_ge(up_done, b * NJ + j + 1)
                ve.wait_ge(sg_ready, b * NJ + j + 1)
                ve.scalar_tensor_tensor(out=h[:, j % 2, :], in0=banks(r, UP, 2), scalar=aq[:, p, 1, j:j + 1], in1=sg[:, j % 2, :],
                                        op0=ALU.mult, op1=ALU.mult).then_inc(h_ready, 1)
                ve.wait_ge(h_ready, b * NJ + j + 1)
                ve.tensor_reduce(hmax[:, j:j + 1], h[:, j % 2, :], AX.X, ALU.max, apply_absolute_value=True).then_inc(step, 1)
                ve.wait_ge(step, (b * NJ + j) * 3 + 1)
                ve.tensor_scalar(hmax[:, j:j + 1], hmax[:, j:j + 1], 1e-5, None, ALU.max).then_inc(step, 1)
                ve.wait_ge(step, (b * NJ + j) * 3 + 2)
                ve.reciprocal(hrec[:, j:j + 1], hmax[:, j:j + 1]).then_inc(step, 1)
                ve.wait_ge(step, (b * NJ + j) * 3 + 3)
                ve.tensor_scalar(hdq[:, j:j + 1], hmax[:, j:j + 1], 1.0 / 127.0, wmean[:, 2:3], ALU.mult, ALU.mult)
                ve.tensor_scalar(hscale[:, j:j + 1], hrec[:, j:j + 1], 127.0, None, ALU.mult).then_inc(hscale_ready, 1)

            def update(b, j):
                ve.wait_ge(out_done, b * NJ + j + 1)
                x = r.X[:, bass.ds(b * BT + j * D, D)]
                ve.scalar_tensor_tensor(out=x, in0=banks(r, DOWN + j % 2)[:, 0:D], scalar=hdq[:, j:j + 1], in1=x,
                                        op0=ALU.mult, op1=ALU.add).then_inc(out_read, 1)

            def turn(b, p, before, after):
                for j in range(NJ):
                    hidden(b, p, j)
                    if j >= 2:
                        update(b, j - 2)
                    elif before:
                        update(b - 1, j + 2)
                    if after:
                        if j == 0:
                            norm.statistics(ve, r, b + 1)
                        elif j == 1:
                            token_scales(b + 1, 1 - p)
                        elif j == 2:
                            quantise_tokens(b + 1)
            token_scales(0, 0)
            quantise_tokens(0)
            staggered(ve, nb, turn)
            update(nb - 1, 2)
            update(nb - 1, 3)

        @block.tensor
        def _(pe):
            pe.wait_ge(abs_ready, 3)
            nc.tensor.matmul(banks(r, 0)[:, 0:3], r.ones[:], rowsum[:], start=True, stop=True).then_inc(tot_done, 1)
            pe.wait_ge(mean_ready, 11)
            gate_w, up_w = (wq[:, n, :].rearrange("p (c n) -> p c n", c=NC) for n in range(2))
            down_w = wq[:, 2, :].rearrange("p (c n) -> p c n", c=NI)

            def transpose_x(b):
                pe.wait_ge(xq_ready, 5 * (b + 1))
                for c in range(NC):
                    for j in range(NJ):
                        last = nc.tensor.transpose(banks(r, 0).bitcast(BF16)[:, c * T + j * P:c * T + (j + 1) * P],
                                                   xq[:, j, c * P:(c + 1) * P], r.identb[:])
                last.then_inc(xt_done, 1)

            def inner(b, j, first=False):
                if j == 0:
                    pe.wait_ge(xqt_ready, b + 1)
                if not first:
                    pe.wait_ge(sg_ready, b * NJ + j)
                for w, bank, done in ((gate_w, GATE, gate_done), (up_w, UP, up_done)):
                    if w is up_w and not first:
                        pe.wait_ge(h_ready, b * NJ + j)
                    for half in range(FI // BANK):
                        last = product(nc, banks(r, bank + half), [(xqt[:, c, j * P:(j + 1) * P], w[:, c, half * BANK:(half + 1) * BANK]) for c in range(NC)])
                    last.then_inc(done, 1)

            def turn(b, p, before, after):
                for j in range(NJ):
                    if j < 2:
                        inner(b, j + 2)
                    elif after:
                        inner(b + 1, j - 2)
                    pe.wait_ge(hq_ready, b * NJ + j + 1)
                    if before or j:
                        pe.wait_ge(ht_ready, b * NJ + j)
                    for i in range(NI):
                        last = nc.tensor.transpose(banks(r, HT).bitcast(BF16)[:, i * P:(i + 1) * P], hq[:, j % 2, i * P:(i + 1) * P], r.identb[:])
                    last.then_inc(htps_done, 1)
                    pe.wait_ge(ht_ready, b * NJ + j + 1)
                    if before or j >= 2:
                        pe.wait_ge(out_read, b * NJ + j - 1)
                    product(nc, banks(r, DOWN + j % 2)[:, 0:D], [(ht[:, j % 2, i, :], down_w[:, i, :]) for i in range(NI)]).then_inc(out_done, 1)
                    if after and j == 1:
                        transpose_x(b + 1)
            transpose_x(0)
            inner(0, 0, True)
            inner(0, 1)
            staggered(pe, nb, turn)


def cross1_phase(nc, r, d, nb=B):
    tag = "x1"
    with ExitStack() as es:
        sb = lambda n, s, t=F32: es.enter_context(nc.sbuf_tensor(f"{tag}_{n}", s, t))
        sem = lambda n: new_semaphore(nc, r, (f"{tag}_{n}"))
        norm = Norm(nc, es, tag, r)
        ctx32, ctxh, ctxl = sb("ctx32", [P, NC, B * SKV]), sb("ctxh", [P, NC, B * SKV], F16), sb("ctxl", [P, NC, B * SKV], F16)
        k32, kh, kl = sb("k32", [P, NC, B * SKV]), sb("kh", [P, NC, B * SKV], F16), sb("kl", [P, NC, B * SKV], F16)
        kst, vblk = sb("kst", [P, NP_ * B, P], F16), sb("vblk", [P, B, NP_, 64])
        kcur, vcur = sb("kcur", [P, NP_, P], F16), sb("vcur", [P, NP_, 64])
        xh, xl = sb("xh", [P, NC, T], F16), sb("xl", [P, NC, T], F16)
        q32, qh, ql = sb("q32", [P, NC, T]), sb("qh", [P, NC, T], F16), sb("ql", [P, NC, T], F16)
        qs = sb("qs", [P, 2, NP_, T], F16)
        nrow, krow = sb("nrow", [2, NP_, T], F16), sb("krow", [2, T], F16)
        mx, mh, ml = sb("mx", [P, NJ, H]), sb("mh", [H, T], F16), sb("ml", [H, T], F16)
        pexp, ot, rec = sb("pexp", [P, NP_, T]), sb("ot", [P, 4, T]), sb("rec", [P, NJ, H])
        y, yh, yl = sb("y", [P, NJ, D]), sb("yh", [P, NC, T], F16), sb("yl", [P, NC, T], F16)
        bq, bk = sb("bq", [P, NC, 1]), sb("bk", [P, NC, 1])
        bv_row, bias_out = sb("bv_row", [P, D]), sb("bias_out", [P, D])
        kscratch = nc.dram_tensor(f"{tag}_kscratch", (2, NC, DH, NP_ * B * SKV), F16, kind="Internal").ap()
        qscratch = nc.dram_tensor(f"{tag}_qscratch", (2, P, NC, T), F16, kind="Internal").ap()
        (w_in, consts, ctxh_ready, ctxl_ready, kps_done, kh_ready, kl_ready, vps_done, v_ready, ones_in, ksaved, kstacked) = (
            sem(n) for n in ("w_in", "consts", "ctxh_ready", "ctxl_ready", "kps_done", "kh_ready", "kl_ready", "vps_done", "v_ready", "ones_in", "ksaved", "kstacked"))
        (zeroed, xt_done, xh_ready, xl_ready, q_done, q_ready, ql_ready, saved, stacked, cur_ready, mxs_ready, mx_read, mt_done) = (
            sem(n) for n in ("zeroed", "xt_done", "xh_ready", "xl_ready", "q_done", "q_ready", "ql_ready", "saved", "stacked", "cur_ready", "mxs_ready", "mx_read", "mt_done"))
        (mh_ready, ml_ready, rows_in, st_ready, exp_done, av_done, ot_ready, ott_done, y_ready, yt_done, yh_ready, yl_ready, out_done, step) = (
            sem(n) for n in ("mh_ready", "ml_ready", "rows_in", "st_ready", "exp_done", "av_done", "ot_ready", "ott_done", "y_ready", "yt_done", "yh_ready", "yl_ready", "out_done", "step"))
        flat = lambda t: t[:].rearrange("p c t -> p (c t)")
        X_BANK, PAIR, AV = 0, (2, 4), 6
        NKD = 8
        block = es.enter_context(nc.Block())

        def three(name, m0, m1, hi, lo):
            at = COL[f"x1{name}"]
            return [(w[:, c, at + m0:at + m1], c, part) for c in range(NC) for w, part in ((r.wh, hi), (r.wh, lo), (r.wl, hi))]

        @block.sync
        def _(sp):
            def const(dst, src):
                sp.dma_start(dst, src, allow_slow_non_contiguous=True).then_inc(w_in, 16)
            const(ctx32[:], d["ctxT"].rearrange("(c p) n -> p c n", p=P))
            const(bq[:], d["x1_bq"].rearrange("(c p) -> p c", p=P).unsqueeze(2))
            const(bk[:], d["x1_bk"].rearrange("(c p) -> p c", p=P).unsqueeze(2))
            const(bv_row[:], d["x1_bv"].partition_broadcast(P))
            const(bias_out[:], d["x1_bo"].partition_broadcast(P))
            sp.wait_ge(kl_ready, 1)
            for n, part in enumerate((kh, kl)):
                for par in range(2):
                    sp.dma_start(kscratch[n, par].rearrange("d (i n) -> i d n", i=NP_), part[:, par, :]).then_inc(ksaved, 16)
            sp.wait_ge(consts, 2)
            sp.wait_ge(zeroed, 3)
            sp.wait_ge(ksaved, 64)
            for par in range(2):
                own = slice(par * SKV, (par + 1) * SKV)
                for rep, part in enumerate((0, 1, 0)):
                    at = 64 * par + 16 * rep
                    sp.dma_start(kst[at:at + 16, :, own], kscratch[part, par].rearrange("d (n s) -> d n s", s=SKV)).then_inc(kstacked, 16)
                sp.dma_start(kst[64 * par + 48:64 * par + 50, :, own],
                             krow[:, 0:SKV].unsqueeze(1).broadcast_to([2, NP_ * B, SKV])).then_inc(kstacked, 16)

            def save(b):
                sp.wait_ge(q_ready, b + 1)
                sp.dma_start(qscratch[0], qh[:]).then_inc(saved, 16)
                sp.wait_ge(ql_ready, b + 1)
                sp.dma_start(qscratch[1], ql[:]).then_inc(saved, 16)

            def stack(b, p):
                sp.wait_ge(saved, (b + 1) * 32)
                for par in range(2):
                    for rep, part in enumerate((0, 0, 1)):
                        at = 64 * par + 16 * rep
                        sp.dma_start(qs[at:at + 16, p], qscratch[part][:, par, :].rearrange("(i d) t -> d i t", d=DH)).then_inc(stacked, 16)
                    sp.dma_start(qs[64 * par + 48:64 * par + 50, p], nrow[:]).then_inc(stacked, 16)

            def rows(b, p):
                sp.wait_ge(ml_ready, b + 1)
                for par in range(2):
                    for row, m in ((48, mh), (49, ml)):
                        sp.dma_start(qs[64 * par + row:64 * par + row + 1, p], m[par * NP_:(par + 1) * NP_, :]).then_inc(rows_in, 16)

            def turn(b, p, before, after):
                rows(b, p)
                if after:
                    save(b + 1)
                    stack(b + 1, 1 - p)
            save(0)
            stack(0, 0)
            staggered(sp, nb, turn)

        @block.gpsimd
        def _(pool):
            pool.memset(krow[:], MS).then_inc(consts, 1)
            pool.memset(nrow[:], 0.0).then_inc(consts, 1)
            pool.memset(kst[:], 0.0).then_inc(zeroed, 1)
            norm.pool_start(pool)

            def queries(b):
                norm.pool(pool, b)
                pool.wait_ge(q_ready, b + 1)
                pool.tensor_tensor(ql[:], q32[:], qh[:], ALU.subtract).then_inc(ql_ready, 1)
            with pool.Fori(0, nb) as b:
                queries(b)

        @block.scalar
        def _(act):
            act.wait_ge(w_in, 16 * 5)
            act.activation(ctxh[:], ctx32[:], ACT.Copy).then_inc(ctxh_ready, 1)
            act.wait_ge(kps_done, 1)
            for m in range(NC):
                act.activation(k32[:, m, :], banks(r, 2 + m), ACT.Identity, bias=bk[:, m, :], scale=1.0 / WS)
                last = act.activation(kh[:, m, :], banks(r, 2 + m), ACT.Identity, bias=bk[:, m, :], scale=1.0 / WS)
            last.then_inc(kh_ready, 1)

            def high_x(b):
                act.wait_ge(xt_done, b + 1)
                act.activation(flat(xh), banks(r, X_BANK, 2), ACT.Copy).then_inc(xh_ready, 1)

            def queries(b):
                act.wait_ge(q_done, b + 1)
                for m in range(NC):
                    act.activation(q32[:, m, :], banks(r, X_BANK + m), ACT.Identity, bias=bq[:, m, :], scale=1.0 / WS)
                    last = act.activation(qh[:, m, :], banks(r, X_BANK + m), ACT.Identity, bias=bq[:, m, :], scale=1.0 / WS)
                last.then_inc(q_ready, 1)

            def turn(b, p, before, after):
                if after:
                    high_x(b + 1)
                act.wait_ge(mt_done, b + 1)
                act.activation(mh[:], banks(r, AV)[0:H, :], ACT.Copy, scale=-1.0 / MS).then_inc(mh_ready, 1)
                if after:
                    queries(b + 1)
                for k in range(4):
                    act.wait_ge(st_ready, b * 4 + k + 1)
                    act.activation(pexp[:, 2 * k:2 * k + 2, :].rearrange("p i t -> p (i t)"), banks(r, PAIR[k % 2], 2), ACT.Exp, scale=DH ** -0.5).then_inc(exp_done, 1)
                act.wait_ge(yt_done, b + 1)
                act.activation(flat(yh), banks(r, PAIR[1], 2), ACT.Copy).then_inc(yh_ready, 1)
            high_x(0)
            queries(0)
            staggered(act, nb, turn)

        @block.vector
        def _(ve):
            ve.memset(vblk[:], 0.0).then_inc(zeroed, 1)
            ve.memset(qs[:], 0.0).then_inc(zeroed, 1)
            ve.wait_ge(zeroed, 3)
            ve.memset(vblk[0:SKV, :, :, DH:DH + 1], 1.0)
            ve.memset(vblk[SKV:P, :, :, 32 + DH:32 + DH + 1], 1.0).then_inc(ones_in, 1)
            ve.wait_ge(ctxh_ready, 1)
            ve.tensor_tensor(ctxl[:], ctx32[:], ctxh[:], ALU.subtract).then_inc(ctxl_ready, 1)
            ve.wait_ge(kh_ready, 1)
            ve.tensor_tensor(kl[:], k32[:], kh[:], ALU.subtract).then_inc(kl_ready, 1)
            ve.wait_ge(vps_done, 1)
            for s in range(B):
                for par in range(2):
                    rows = slice(par * SKV, (par + 1) * SKV)
                    last = ve.scalar_tensor_tensor(out=vblk[rows, s, :, 32 * par:32 * par + DH],
                                                   in0=banks(r, 4, 2)[rows, s * P:(s + 1) * P].rearrange("p (i e) -> p i e", e=DH), scalar=1.0 / WS,
                                                   in1=bv_row[rows, par * P:(par + 1) * P].rearrange("p (i e) -> p i e", e=DH), op0=ALU.mult, op1=ALU.add)
            last.then_inc(v_ready, 1)
            ve.wait_ge(v_ready, 1)
            ve.wait_ge(ones_in, 1)

            def low_x(b):
                ve.wait_ge(xh_ready, b + 1)
                ve.tensor_tensor(flat(xl), banks(r, X_BANK, 2), flat(xh), ALU.subtract).then_inc(xl_ready, 1)

            def maximum(b, j):
                ve.wait_ge(mxs_ready, b * NJ + j + 1)
                ve.reduce_max(mx[:, j, :].rearrange("p (par i) -> p i par", par=2), banks(r, PAIR[j % 2], 2).rearrange("p (i par s) -> p i par s", par=2, s=SKV), AX.X).then_inc(mx_read, 1)

            def current(b):
                ve.tensor_scalar(kcur[:], kst[:].rearrange("p (i b) s -> p i b s", b=B)[:, :, bass.ds(b, 1)].rearrange("p i o s -> p (i o) s"), 1.0, None, ALU.mult)
                ve.tensor_scalar(vcur[:], vblk[:, bass.ds(b, 1)].rearrange("p o i s -> p (o i) s"), 1.0, None, ALU.mult).then_inc(cur_ready, 1)

            def turn(b, p, before, after):
                steps = Count(NJ + 1)
                maximum(b, 0)
                maximum(b, 1)
                if after:
                    norm.apply(ve, r, b + 1)
                maximum(b, 2)
                maximum(b, 3)
                ve.wait_ge(mh_ready, b + 1)
                ve.scalar_tensor_tensor(out=ml[:], in0=banks(r, AV)[0:H, :], scalar=-1.0 / MS, in1=mh[:], op0=ALU.mult, op1=ALU.subtract).then_inc(ml_ready, 1)
                if after:
                    low_x(b + 1)
                for g in range(4):
                    ve.wait_ge(av_done, b * 4 + g + 1)
                    ve.tensor_copy(ot[:, g, :], banks(r, AV + g % 2)).then_inc(ot_ready, 1)
                for j in range(NJ):
                    ve.wait_ge(ott_done, b * NJ + j + 1)
                    o = banks(r, PAIR[0] + j % 2).rearrange("p (i par e) -> p i par e", par=2, e=32)
                    ve.reciprocal(rec[:, j, :], banks(r, PAIR[0] + j % 2).rearrange("p (h e) -> p h e", e=32)[:, :, DH]).then_inc(step, 1)
                    steps.up()
                    ve.wait_ge(step, steps.at(b))
                    ve.tensor_tensor(y[:, j, :].rearrange("p (par i e) -> p i par e", par=2, e=DH), o[:, :, :, 0:DH],
                                     rec[:, j, :].rearrange("p (i par) -> p i par", par=2).unsqueeze(3).broadcast_to([P, NP_, 2, DH]), ALU.mult).then_inc(y_ready, 1)
                ve.wait_ge(yh_ready, b + 1)
                ve.tensor_tensor(flat(yl), banks(r, PAIR[1], 2), flat(yh), ALU.subtract).then_inc(yl_ready, 1)
                if after:
                    current(b + 1)
                    if not isinstance(b, int) or b + 2 < nb:
                        norm.statistics(ve, r, b + 2)
                ve.wait_ge(out_done, b + 1)
                x = r.X[:, bass.ds(b * BT, BT)]
                ve.scalar_tensor_tensor(out=x, in0=banks(r, AV, 2), scalar=1.0 / WS, in1=x, op0=ALU.mult, op1=ALU.add).then_inc(step, 1)
                steps.up()
                ve.wait_ge(step, steps.at(b))
                xj = x.rearrange("p (j n) -> p j n", n=D)
                ve.tensor_tensor(xj, xj, bias_out[:].unsqueeze(1).broadcast_to([P, NJ, D]), ALU.add)
                steps.done()
            norm.vector(ve, r, 0)
            low_x(0)
            ve.wait_ge(kstacked, 16 * NKD)
            current(0)
            norm.statistics(ve, r, 1)
            staggered(ve, nb, turn)

        @block.tensor
        def _(pe):
            pe.wait_ge(ctxh_ready, 1)
            pe.wait_ge(ctxl_ready, 1)
            for m in range(NC):
                last = product(nc, banks(r, 2 + m), [(w, part[:, c, :]) for w, c, part in three("k", m * P, (m + 1) * P, ctxh, ctxl)])
            last.then_inc(kps_done, 1)
            for s in range(B):
                for par in range(2):
                    last = product(nc, banks(r, 4, 2)[par * SKV:(par + 1) * SKV, s * P:(s + 1) * P],
                                   [(part[:, c, s * SKV:(s + 1) * SKV], w) for w, c, part in three("v", par * P, (par + 1) * P, ctxh, ctxl)])
            last.then_inc(vps_done, 1)
            pe.wait_ge(kh_ready, 1)
            pe.wait_ge(v_ready, 1)

            def transpose_x(b):
                pe.wait_ge(norm.xn_ready, b + 1)
                transpose_tiles(nc, r, norm.xn, X_BANK).then_inc(xt_done, 1)

            def queries(b):
                pe.wait_ge(xl_ready, b + 1)
                for m in range(NC):
                    last = product(nc, banks(r, X_BANK + m), [(w, part[:, c, :]) for w, c, part in three("q", m * P, (m + 1) * P, xh, xl)])
                last.then_inc(q_done, 1)

            def turn(b, p, before, after):
                pe.wait_ge(cur_ready, b + 1)
                pe.wait_ge(stacked, 16 * 8 * (b + 1))
                for j in range(NJ):
                    if j >= 2:
                        pe.wait_ge(mx_read, b * NJ + j - 1)
                    for i in range(NP_):
                        last = nc.tensor.matmul(banks(r, PAIR[j % 2], 2)[:, i * P:(i + 1) * P], qs[:, p, i, j * P:(j + 1) * P], kcur[:, i, :], start=True, stop=True)
                    last.then_inc(mxs_ready, 1)
                if after:
                    transpose_x(b + 1)
                pe.wait_ge(mx_read, (b + 1) * NJ)
                for j in range(NJ):
                    last = nc.tensor.transpose(banks(r, AV)[0:H, j * P:(j + 1) * P], mx[:, j, :], r.ident[:])
                last.then_inc(mt_done, 1)
                if after:
                    queries(b + 1)
                pe.wait_ge(rows_in, 64 * (b + 1))

                def values(g):
                    pe.wait_ge(exp_done, b * 4 + g + 1)
                    if g >= 2:
                        pe.wait_ge(ot_ready, b * 4 + g - 1)
                    for i in range(2):
                        last = nc.tensor.matmul(banks(r, AV + g % 2)[64 * i:64 * (i + 1), :], vcur[:, 2 * g + i, :], pexp[:, 2 * g + i, :], start=True, stop=True)
                    last.then_inc(av_done, 1)
                for k in range(4):
                    if k >= 2:
                        pe.wait_ge(exp_done, b * 4 + k - 1)
                    for i in range(2):
                        last = nc.tensor.matmul(banks(r, PAIR[k % 2] + i), kcur[:, 2 * k + i, :], qs[:, p, 2 * k + i, :], start=True, stop=True)
                    last.then_inc(st_ready, 1)
                    if k:
                        values(k - 1)
                values(3)
                pe.wait_ge(ot_ready, 4 * (b + 1))
                for j in range(NJ):
                    if j >= 2:
                        pe.wait_ge(y_ready, b * NJ + j - 1)
                    for g in range(4):
                        last = nc.tensor.transpose(banks(r, PAIR[0] + j % 2)[:, g * P:(g + 1) * P], ot[:, g, j * P:(j + 1) * P], r.ident[:])
                    last.then_inc(ott_done, 1)
                pe.wait_ge(y_ready, NJ * (b + 1))
                transpose_tiles(nc, r, y, PAIR[1]).then_inc(yt_done, 1)
                pe.wait_ge(yl_ready, b + 1)
                for j in range(NJ):
                    last = product(nc, banks(r, AV, 2)[:, j * D:(j + 1) * D], [(part[:, c, j * P:(j + 1) * P], w) for w, c, part in three("o", 0, D, yh, yl)])
                last.then_inc(out_done, 1)
            transpose_x(0)
            queries(0)
            staggered(pe, nb, turn)


def experts_phase(nc, r, d, out, nb=B):
    E, FI = 8, 512
    NI = FI // P
    NE = E + 1
    NW = NC * FI
    with ExitStack() as es0:
        wts = es0.enter_context(nc.sbuf_tensor("mo_wts", [P, B * NJ * NE], F32))
        xth = es0.enter_context(nc.sbuf_tensor("mo_xth", [P, NC, B * T], F16))
        xtl = es0.enter_context(nc.sbuf_tensor("mo_xtl", [P, NC, B * T], F16))
        stage = es0.enter_context(nc.sbuf_tensor("mo_stage", [P, 3, NW], F32))
        wh, wl = (es0.enter_context(nc.sbuf_tensor(f"mo_{n}", [P, 2, 3, NW], F16)) for n in ("wh", "wl"))

        def load_expert(sp, e, done):
            for n, w in enumerate(("m_gate", "m_up", "m_down")):
                k = NI if n == 2 else NC
                sp.dma_start(stage[:, n, :].rearrange("p (c n) -> p c n", c=k),
                             d[w][bass.ds(e, 1)].rearrange("e (c p) n -> p (e c) n", p=P)).then_inc(done, 16)

        def high_part(act, q, n):
            return act.activation(wh[:, q, n, :], stage[:, n, :], ACT.Copy, scale=WS)

        def low_part(ve, q, n):
            return ve.scalar_tensor_tensor(out=wl[:, q, n, :], in0=stage[:, n, :], scalar=WS, in1=wh[:, q, n, :],
                                           op0=ALU.mult, op1=ALU.subtract)
        route(nc, r, d, nb, wts, xth, xtl, E, load_expert, high_part, low_part)
        end_phase(nc, r)
        with ExitStack() as es:
            tag = "mo"
            sb = lambda n, s, t=F32: es.enter_context(nc.sbuf_tensor(f"{tag}_{n}", s, t))
            sem = lambda n: new_semaphore(nc, r, (f"{tag}_{n}"))
            pad = sb("pad", [P, 1])
            sg, h = sb("sg", [P, 2, FI]), sb("h", [P, 2, NI, T])
            hh, hl = sb("hh", [P, 2, NI, T], F16), sb("hl", [P, 2, NI, T], F16)
            (w_in, wh_ready, wl_ready, gu_done, sg_ready, h_ready, hh_ready, hl_ready, down_done, x_done, stored) = (
                sem(n) for n in ("w_in", "wh_ready", "wl_ready", "gu_done", "sg_ready", "h_ready", "hh_ready", "hl_ready", "down_done", "x_done", "stored"))
            GU = ((0, 1), (2, 3))
            DN = (4, 6)
            block = es.enter_context(nc.Block())
            pairs = nb // 2
            assert NE % 2 == 1

            def experts(eng, expert):
                with eng.Fori(0, NE // 2) as k:
                    expert(2 * k, 0, True)
                    expert(2 * k + 1, 1, True)
                expert(NE - 1, 0, False)

            @block.sync
            def _(sp):
                with sp.Fori(0, NE - 1) as e:
                    sp.wait_ge(wl_ready, e * 3 + 1)
                    load_expert(sp, e + 1, w_in)
                for b in range(nb):
                    sp.wait_ge(x_done, b + 1)
                    sp.dma_start(out[b].rearrange("(j p) c -> p j c", p=P),
                                 r.X[:, b * BT:(b + 1) * BT].rearrange("p (j c) -> p j c", c=D)).then_inc(stored, 16)
                sp.wait_ge(stored, 16 * nb)

            @block.scalar
            def _(act):
                def split(e, q, n):
                    if n == 0:
                        act.wait_ge(w_in, 48 * e)
                        act.wait_ge(down_done, nb * (e - 1) + 1)
                    high_part(act, q, n).then_inc(wh_ready, 1)

                def squash(e, b, par, then=None):
                    for i in range(NI):
                        n = (e * nb + b) * NI + i
                        act.wait_ge(gu_done, n + 1)
                        act.activation(sg[:, i % 2, :], banks(r, GU[i % 2][0]), ACT.Silu, scale=1.0 / WS).then_inc(sg_ready, 1)
                        act.wait_ge(h_ready, n + 1)
                        act.activation(hh[:, par, i, :], h[:, par, i, :], ACT.Copy).then_inc(hh_ready, 1)
                        if then is not None and i < 3:
                            then(i)

                def expert(e, q, after):
                    with act.Fori(0, pairs - 1) as k:
                        squash(e, 2 * k + 1, 1)
                        squash(e, 2 * k + 2, 0)
                    squash(e, nb - 1, 1, (lambda n: split(e + 1, 1 - q, n)) if after else None)
                    if after:
                        squash(e + 1, 0, 0)
                squash(0, 0, 0)
                experts(act, expert)

            @block.vector
            def _(ve):
                ve.memset(pad[:], 0.0).then_inc(wl_ready, 1)

                def split(e, q, n):
                    ve.wait_ge(wh_ready, 3 * (e - 1) + n + 1)
                    low_part(ve, q, n).then_inc(wl_ready, 1)

                def hidden(e, b, par, then=None):
                    for i in range(NI):
                        n = (e * nb + b) * NI + i
                        ve.wait_ge(sg_ready, n + 1)
                        ve.scalar_tensor_tensor(out=h[:, par, i, :], in0=banks(r, GU[i % 2][1]), scalar=1.0 / WS, in1=sg[:, i % 2, :],
                                                op0=ALU.mult, op1=ALU.mult).then_inc(h_ready, 1)
                        ve.wait_ge(hh_ready, n + 1)
                        ve.tensor_tensor(hl[:, par, i, :], h[:, par, i, :], hh[:, par, i, :], ALU.subtract).then_inc(hl_ready, 1)
                        if then is not None and i < 3:
                            then(i)

                def update(e, b, par, final):
                    ve.wait_ge(down_done, e * nb + b + 2)
                    for j in range(NJ):
                        x = r.X[:, bass.ds(b * BT + j * D, D)]
                        last = ve.scalar_tensor_tensor(out=x, in0=banks(r, DN[par], 2)[:, j * D:(j + 1) * D],
                                                       scalar=wts[:, bass.ds(b * NJ * NE + j * NE + e, 1)], in1=x, op0=ALU.mult, op1=ALU.add)
                    if final:
                        last.then_inc(x_done, 1)

                def expert(e, q, after):
                    with ve.Fori(0, pairs - 1) as k:
                        hidden(e, 2 * k + 1, 1)
                        update(e, 2 * k, 0, not after)
                        hidden(e, 2 * k + 2, 0)
                        update(e, 2 * k + 1, 1, not after)
                    hidden(e, nb - 1, 1, (lambda n: split(e + 1, 1 - q, n)) if after else None)
                    update(e, nb - 2, 0, not after)
                    if after:
                        hidden(e + 1, 0, 0)
                    update(e, nb - 1, 1, not after)
                hidden(0, 0, 0)
                experts(ve, expert)

            @block.tensor
            def _(pe):
                gate, up = (lambda w, q, n=n: w[:, q, n, :].rearrange("p (c n) -> p c n", c=NC) for n in range(2))
                down = lambda w, q: w[:, q, 2, :].rearrange("p (c n) -> p c n", c=NI)
                nc.tensor.matmul(banks(r, 0)[:, 0:1], r.ones[:], r.ones[:, 0:1], start=True, stop=True).then_inc(down_done, 1)

                def gate_up(e, b, q, first=False):
                    for i in range(NI):
                        n = (e * nb + b) * NI + i
                        if i >= 2 or not first:
                            pe.wait_ge(h_ready, n - 1)
                        for w, bank in ((gate, GU[i % 2][0]), (up, GU[i % 2][1])):
                            m = slice(i * P, (i + 1) * P)
                            last = product(nc, banks(r, bank), [(w(part, q)[:, c, m], x[:, c, bass.ds(b * T, T)]) for c in range(NC)
                                                                for part, x in ((wh, xth), (wh, xtl), (wl, xth))])
                        last.then_inc(gu_done, 1)

                def project(e, b, par, q):
                    pe.wait_ge(hl_ready, (e * nb + b + 1) * NI)
                    for j in range(NJ):
                        t = slice(j * P, (j + 1) * P)
                        last = product(nc, banks(r, DN[par], 2)[:, j * D:(j + 1) * D],
                                       [(x[:, par, i, t], down(part, q)[:, i, :]) for i in range(NI) for x, part in ((hh, wh), (hl, wh), (hh, wl))])
                    last.then_inc(down_done, 1)

                def expert(e, q, after):
                    with pe.Fori(0, pairs - 1) as k:
                        gate_up(e, 2 * k + 1, q)
                        project(e, 2 * k, 0, q)
                        gate_up(e, 2 * k + 2, q)
                        project(e, 2 * k + 1, 1, q)
                    gate_up(e, nb - 1, q)
                    project(e, nb - 2, 0, q)
                    if after:
                        pe.wait_ge(wl_ready, 3 * (e + 1) + 1)
                        gate_up(e + 1, 0, 1 - q)
                    project(e, nb - 1, 1, q)
                gate_up(0, 0, 0, True)
                experts(pe, expert)


def route(nc, r, d, nb, wts, xth, xtl, E, load_expert, high_part, low_part):
    tag = "ro"
    NE = E + 1
    with ExitStack() as es:
        sb = lambda n, s, t=F32: es.enter_context(nc.sbuf_tensor(f"{tag}_{n}", s, t))
        sem = lambda n: new_semaphore(nc, r, (f"{tag}_{n}"))
        norm = Norm(nc, es, tag, r)
        xh, xl = sb("xh", [P, NC, T], F16), sb("xl", [P, NC, T], F16)
        w32, rwh, rwl = sb("w32", [P, NC, E]), sb("rwh", [P, NC, E], F16), sb("rwl", [P, NC, E], F16)
        bias, iota = sb("bias", [P, E]), sb("iota", [P, E])
        lg, pr = sb("lg", [P, NJ, E]), sb("pr", [P, NJ, E])
        top, idx, idxf = sb("top", [P, NJ, E]), sb("idx", [P, NJ, E], U32), sb("idxf", [P, NJ, E])
        total, rec, share = sb("total", [P, NJ, 1]), sb("rec", [P, NJ, 1]), sb("share", [P, NJ, 2])
        pick, pad = sb("pick", [P, 2, NJ, E]), sb("hold", [P, 1])
        (w_in, expert_in, wh_ready, iota_in, rwh_ready, rwl_ready, ones_in, xt_done, xh_ready, xl_ready, lg_done, lg_ready, pr_ready, kept, step) = (
            sem(n) for n in ("w_in", "expert_in", "wh_ready", "iota_in", "rwh_ready", "rwl_ready", "ones_in", "xt_done", "xh_ready", "xl_ready", "lg_done", "lg_ready", "pr_ready", "kept", "step"))
        flat = lambda t: t[:].rearrange("p c t -> p (c t)")
        block = es.enter_context(nc.Block())

        @block.sync
        def _(sp):
            sp.dma_start(w32[:], d["m_router"].rearrange("(c p) n -> p c n", p=P)).then_inc(w_in, 16)
            sp.dma_start(bias[:], d["m_bias"].partition_broadcast(P)).then_inc(kept, 16)
            load_expert(sp, 0, expert_in)
            with sp.Fori(0, nb) as b:
                sp.wait_ge(xh_ready, b + 1)
                sp.wait_ge(xl_ready, b + 1)
                sp.dma_start(xth[:, :, bass.ds(b * T, T)], xh[:]).then_inc(kept, 16)
                sp.dma_start(xtl[:, :, bass.ds(b * T, T)], xl[:]).then_inc(kept, 16)
            sp.wait_ge(kept, 32 * nb + 16)

        @block.gpsimd
        def _(pool):
            for n in range(E):
                last = pool.memset(iota[:, n:n + 1], float(n))
            last.then_inc(iota_in, 1)
            norm.pool_start(pool)
            with pool.Fori(0, nb) as b:
                norm.pool(pool, b)

        @block.scalar
        def _(act):
            act.wait_ge(w_in, 16)
            act.activation(rwh[:], w32[:], ACT.Copy, scale=WS).then_inc(rwh_ready, 1)
            act.wait_ge(expert_in, 48)
            for n in range(3):
                high_part(act, 0, n).then_inc(wh_ready, 1)
            with act.Fori(0, nb) as b:
                act.wait_ge(xt_done, b + 1)
                act.wait_ge(kept, 32 * b + 16)
                act.activation(flat(xh), banks(r, 0, 2), ACT.Copy).then_inc(xh_ready, 1)
                act.wait_ge(lg_ready, b + 1)
                act.activation(pr[:], lg[:], ACT.Sigmoid).then_inc(pr_ready, 1)

        @block.vector
        def _(ve):
            ve.wait_ge(rwh_ready, 1)
            ve.scalar_tensor_tensor(out=rwl[:], in0=w32[:], scalar=WS, in1=rwh[:], op0=ALU.mult, op1=ALU.subtract).then_inc(rwl_ready, 1)
            ve.memset(wts[:], 1.0 / WS).then_inc(ones_in, 1)
            ve.wait_ge(kept, 16)
            ve.wait_ge(ones_in, 1)
            ve.wait_ge(iota_in, 1)

            def logits(b):
                ve.wait_ge(xh_ready, b + 1)
                ve.tensor_tensor(flat(xl), banks(r, 0, 2), flat(xh), ALU.subtract).then_inc(xl_ready, 1)
                ve.wait_ge(lg_done, b + 1)
                ve.scalar_tensor_tensor(out=lg[:], in0=banks(r, 2)[:, 0:NJ * E].rearrange("p (j e) -> p j e", e=E), scalar=1.0 / WS,
                                        in1=bias[:].unsqueeze(1).broadcast_to([P, NJ, E]), op0=ALU.mult, op1=ALU.add).then_inc(lg_ready, 1)

            def turn(b, after):
                steps = Count(2 * NJ + 4 + 2 * NJ)
                if after:
                    norm.statistics(ve, r, b + 1)
                    norm.apply(ve, r, b + 1)
                ve.wait_ge(pr_ready, b + 1)
                ve.memset(pad[:], 0.0)
                for j in range(NJ):
                    ve.max(top[:, j, :], pr[:, j, :]).then_inc(step, 1)
                    steps.up()
                ve.wait_ge(step, steps.at(b))
                ve.tensor_tensor(total[:], top[:, :, 0:1], top[:, :, 1:2], ALU.add).then_inc(step, 1)
                for j in range(NJ):
                    ve.max_index(idx[:, j, :], top[:, j, :], pr[:, j, :]).then_inc(step, 1)
                    steps.up()
                steps.up()
                ve.wait_ge(step, steps.at(b))
                ve.tensor_copy(idxf[:], idx[:]).then_inc(step, 1)
                ve.reciprocal(rec[:], total[:]).then_inc(step, 1)
                steps.up()
                steps.up()
                ve.wait_ge(step, steps.at(b))
                ve.scalar_tensor_tensor(out=share[:], in0=top[:, :, 0:2], scalar=1.0 / WS, in1=rec[:].broadcast_to([P, NJ, 2]),
                                        op0=ALU.mult, op1=ALU.mult).then_inc(step, 1)
                steps.up()
                ve.wait_ge(step, steps.at(b))
                for j in range(NJ):
                    for k in range(2):
                        ve.tensor_scalar(pick[:, k, j, :], iota[:], idxf[:, j, k:k + 1], share[:, j, k:k + 1], ALU.is_equal, ALU.mult).then_inc(step, 1)
                        steps.up()
                ve.wait_ge(step, steps.at(b))
                ve.tensor_tensor(wts[:, bass.ds(b * NJ * NE, NJ * NE)].rearrange("p (j e) -> p j e", e=NE)[:, :, 1:NE],
                                 pick[:, 0], pick[:, 1], ALU.add)
                steps.done()
            norm.vector(ve, r, 0)
            logits(0)
            ve.wait_ge(wh_ready, 3)
            for n in range(3):
                low_part(ve, 0, n)
            with ve.Fori(0, nb - 1) as b:
                turn(b, True)
                logits(b + 1)
            turn(nb - 1, False)

        @block.tensor
        def _(pe):
            pe.wait_ge(rwl_ready, 1)
            with pe.Fori(0, nb) as b:
                pe.wait_ge(norm.xn_ready, b + 1)
                transpose_tiles(nc, r, norm.xn, 0).then_inc(xt_done, 1)
                pe.wait_ge(xl_ready, b + 1)
                for j in range(NJ):
                    t = slice(j * P, (j + 1) * P)
                    last = product(nc, banks(r, 2)[:, j * E:(j + 1) * E],
                                   [(x[:, c, t], w[:, c, :]) for c in range(NC) for x, w in ((xh, rwh), (xl, rwh), (xh, rwl))])
                last.then_inc(lg_done, 1)


def kernel(**inputs):
    import numpy as _np
    import concourse.bacc as _bacc
    from concourse import mybir as _mybir
    from concourse.bass_utils import run_bass_kernel_spmd as _run

    nc = _bacc.Bacc("TRN2", target_bir_lowering=False, num_devices=1)
    arrays, d = {}, {}
    for name, a in layout(inputs).items():
        a = _np.ascontiguousarray(a)
        arrays[f"in_{name}"] = a
        d[name] = nc.dram_tensor(f"in_{name}", a.shape, _mybir.dt.from_np(a.dtype), kind="ExternalInput").ap()
    out = nc.dram_tensor("out_dram", (B, T, D), F32, kind="ExternalOutput").ap()
    build(nc, d, out)
    r = _run(nc, [arrays], core_ids=[0])
    return r.results[0]["out_dram"]
```
